# Optimizing a Trainium2 kernel written in Bass

```python
import numpy as np
import jax
import jax.numpy as jnp

def _softmax(x, axis=-1):
    return jax.nn.softmax(x, axis=axis)

def _gelu(x):
    return jax.nn.gelu(x, approximate=True)

def _silu(x):
    return jax.nn.silu(x)

def _sigmoid(x):
    return jax.nn.sigmoid(x)

def _layernorm(x, axis=-1, eps=1e-05):
    m = jnp.mean(x, axis=axis, keepdims=True)
    v = jnp.var(x, axis=axis, keepdims=True)
    return (x - m) / jnp.sqrt(v + eps)

def _scatter_add(tgt, idx, src, axis=0):
    return tgt.at[idx].add(src)

def _segment_sum(src, seg, n):
    return jax.ops.segment_sum(src, seg, n)
kernel_name = 'mk_audio_tower_d2_tok_audfeat1024_r4_2c41ab'

def setup_inputs(seed: int=0):
    np.random.seed(seed)
    _w = jnp.asarray

    def _rec_inputs():
        import jax
        import jax.numpy as jnp
        _rk = jax.random.key(seed)
        x = -0.000125008 + 0.999885 * jax.random.normal(jax.random.fold_in(_rk, 1), (16, 512, 250), jnp.float32)
        return x
    x = _rec_inputs()

    def _L0_tok_setup():
        import jax, jax.numpy as jnp
        import numpy as np
        B, L, N, K, D = (32, 512, 128, 64, 256)

        def dct_fft(x):
            n = x.shape[-1]
            v = jnp.concatenate([x[..., ::2], x[..., 1::2][..., ::-1]], axis=-1)
            return jnp.fft.fft(v).real[..., :n]
        key = jax.random.key(seed)
        k1, k2, k3, k4 = jax.random.split(key, 4)
        x = jax.random.normal(k1, (B, L, N), jnp.float32)
        W = jax.random.normal(k2, (K, D), jnp.float32) * (1.0 / np.sqrt(K))
        b = jax.random.normal(k3, (D,), jnp.float32) * 0.01
        alpha = jax.random.normal(k4, (1,), jnp.float32) * 0.1
        return {'x': x, 'W': W, 'b': b, 'alpha': alpha}
    _L0_tok_all = _L0_tok_setup()
    _L0_tok_in = {k: v for k, v in _L0_tok_all.items() if k in ('W', 'b', 'alpha')}
    del _L0_tok_all

    def _L0_attn_setup():
        import jax, jax.numpy as jnp
        import numpy as np
        DIM = 256
        HEADS = 16
        HEAD_DIM = 64
        ROT = 32
        BASE = 10000.0
        SEQ = 512
        BATCH = 2

        def _rotate_half(t):
            x1, x2 = (t[..., :ROT // 2], t[..., ROT // 2:])
            return jnp.concatenate([-x2, x1], axis=-1)

        def _apply_rope(t, cos, sin):
            t_rot, t_pass = (t[..., :ROT], t[..., ROT:])
            t_rot = t_rot * cos + _rotate_half(t_rot) * sin
            return jnp.concatenate([t_rot, t_pass], axis=-1)
        key = jax.random.key(seed)
        k1, k2, k3, k4 = jax.random.split(key, 4)
        s = 0.02
        return {'x': jax.random.normal(k1, (BATCH, SEQ, DIM), dtype=jnp.float32), 'w_q': jax.random.normal(k2, (DIM, HEADS * HEAD_DIM), dtype=jnp.float32) * s, 'w_kv': jax.random.normal(k3, (DIM, 2 * HEADS * HEAD_DIM), dtype=jnp.float32) * s, 'w_out': jax.random.normal(k4, (HEADS * HEAD_DIM, DIM), dtype=jnp.float32) * s}
    _L0_attn_all = _L0_attn_setup()
    _L0_attn_in = {k: v for k, v in _L0_attn_all.items() if k in ('w_q', 'w_kv', 'w_out')}
    del _L0_attn_all

    def _L0_ffn_setup():
        import jax, jax.numpy as jnp
        import numpy as np
        H = 256
        I = 256
        E = 8
        key = jax.random.key(seed)
        ks = jax.random.split(key, 8)
        s = 0.02
        x = jax.random.normal(ks[0], (4, 512, H), dtype=jnp.float32)
        Wg = jax.random.normal(ks[1], (H, E), dtype=jnp.float32) * s
        bg = jnp.zeros((E,), dtype=jnp.float32)
        W1 = jax.random.normal(ks[2], (E, H, I), dtype=jnp.float32) * s
        b1 = jnp.zeros((E, I), dtype=jnp.float32)
        W2 = jax.random.normal(ks[3], (E, I, H), dtype=jnp.float32) * s
        b2 = jnp.zeros((E, H), dtype=jnp.float32)
        return {'x': x, 'Wg': Wg, 'bg': bg, 'W1': W1, 'b1': b1, 'W2': W2, 'b2': b2}
    _L0_ffn_all = _L0_ffn_setup()
    _L0_ffn_in = {k: v for k, v in _L0_ffn_all.items() if k in ('Wg', 'bg', 'W1', 'b1', 'W2', 'b2')}
    del _L0_ffn_all

    def _L1_attn_setup():
        import math
        import jax, jax.numpy as jnp
        import numpy as np
        DIM = 256
        B, T = (4, 512)
        key = jax.random.key(seed)
        ks = jax.random.split(key, 7)
        std = 0.02
        x = jax.random.normal(ks[0], (B, T, DIM), dtype=jnp.float32)
        Wq = jax.random.normal(ks[1], (DIM, DIM), dtype=jnp.float32) * std
        Wk = jax.random.normal(ks[2], (DIM, DIM), dtype=jnp.float32) * std
        Wv = jax.random.normal(ks[3], (DIM, DIM), dtype=jnp.float32) * std
        Wo = jax.random.normal(ks[4], (DIM, DIM), dtype=jnp.float32) * std
        Wd = jax.random.normal(ks[5], (1, DIM), dtype=jnp.float32) * std
        bd = jnp.full((1,), 3.0, dtype=jnp.float32)
        out_scale = jnp.full((1,), 0.1, dtype=jnp.float32)
        return {'x': x, 'Wq': Wq, 'Wk': Wk, 'Wv': Wv, 'Wo': Wo, 'Wd': Wd, 'bd': bd, 'out_scale': out_scale}
    _L1_attn_all = _L1_attn_setup()
    _L1_attn_in = {k: v for k, v in _L1_attn_all.items() if k in ('Wq', 'Wk', 'Wv', 'Wo', 'Wd', 'bd', 'out_scale')}
    del _L1_attn_all

    def _L1_ffn_setup():
        import jax, jax.numpy as jnp
        import numpy as np
        E = 32
        K = 4
        H = 256
        I = 128
        B, S = (2, 512)
        T = B * S
        C = 256
        ROUTED_SCALE = 1.0

        def _silu_and_mul(gu):
            g, u = jnp.split(gu, 2, axis=-1)
            return jax.nn.silu(g) * u
        key = jax.random.key(seed)
        ks = jax.random.split(key, 6)
        s = 0.02
        return {'hidden_states': jax.random.normal(ks[0], (B, S, H), jnp.float32), 'gate_w': jax.random.normal(ks[1], (E, H), jnp.float32) * s, 'w_gate_up': jax.random.normal(ks[2], (E, H, 2 * I), jnp.float32) * s, 'w_down': jax.random.normal(ks[3], (E, I, H), jnp.float32) * s, 'shared_w_gate_up': jax.random.normal(ks[4], (H, 2 * I), jnp.float32) * s, 'shared_w_down': jax.random.normal(ks[5], (I, H), jnp.float32) * s}
    _L1_ffn_all = _L1_ffn_setup()
    _L1_ffn_in = {k: v for k, v in _L1_ffn_all.items() if k in ('gate_w', 'w_gate_up', 'w_down', 'shared_w_gate_up', 'shared_w_down')}
    del _L1_ffn_all
    return {'x': x, 'L0_tok_W': _L0_tok_in['W'], 'L0_tok_b': _L0_tok_in['b'], 'L0_tok_alpha': _L0_tok_in['alpha'], 'L0_attn_w_q': _L0_attn_in['w_q'], 'L0_attn_w_kv': _L0_attn_in['w_kv'], 'L0_attn_w_out': _L0_attn_in['w_out'], 'L0_ffn_Wg': _L0_ffn_in['Wg'], 'L0_ffn_bg': _L0_ffn_in['bg'], 'L0_ffn_W1': _L0_ffn_in['W1'], 'L0_ffn_b1': _L0_ffn_in['b1'], 'L0_ffn_W2': _L0_ffn_in['W2'], 'L0_ffn_b2': _L0_ffn_in['b2'], 'L1_attn_Wq': _L1_attn_in['Wq'], 'L1_attn_Wk': _L1_attn_in['Wk'], 'L1_attn_Wv': _L1_attn_in['Wv'], 'L1_attn_Wo': _L1_attn_in['Wo'], 'L1_attn_Wd': _L1_attn_in['Wd'], 'L1_attn_bd': _L1_attn_in['bd'], 'L1_attn_out_scale': _L1_attn_in['out_scale'], 'L1_ffn_gate_w': _L1_ffn_in['gate_w'], 'L1_ffn_w_gate_up': _L1_ffn_in['w_gate_up'], 'L1_ffn_w_down': _L1_ffn_in['w_down'], 'L1_ffn_shared_w_gate_up': _L1_ffn_in['shared_w_gate_up'], 'L1_ffn_shared_w_down': _L1_ffn_in['shared_w_down']}

def reference(x, L0_tok_W, L0_tok_b, L0_tok_alpha, L0_attn_w_q, L0_attn_w_kv, L0_attn_w_out, L0_ffn_Wg, L0_ffn_bg, L0_ffn_W1, L0_ffn_b1, L0_ffn_W2, L0_ffn_b2, L1_attn_Wq, L1_attn_Wk, L1_attn_Wv, L1_attn_Wo, L1_attn_Wd, L1_attn_bd, L1_attn_out_scale, L1_ffn_gate_w, L1_ffn_w_gate_up, L1_ffn_w_down, L1_ffn_shared_w_gate_up, L1_ffn_shared_w_down):
    import jax
    import jax.numpy as jnp

    def _L0_tok_ref(x, W, b, alpha):
        import jax, jax.numpy as jnp
        import numpy as np
        B, L, N, K, D = (32, 512, 128, 64, 256)

        def dct_fft(x):
            n = x.shape[-1]
            v = jnp.concatenate([x[..., ::2], x[..., 1::2][..., ::-1]], axis=-1)
            return jnp.fft.fft(v).real[..., :n]
        Bs, Ls, Ns = x.shape
        k = W.shape[0]
        xt = jnp.transpose(x, (0, 2, 1)).reshape(-1, Ls)
        freq_k = dct_fft(xt)[:, :k].reshape(Bs, Ns, k)
        out = jnp.einsum('bnk,kd->bnd', freq_k, W) + b
        return alpha * out

    def _L0_attn_ref(x, w_q, w_kv, w_out):
        import jax, jax.numpy as jnp
        import numpy as np
        DIM = 256
        HEADS = 16
        HEAD_DIM = 64
        ROT = 32
        BASE = 10000.0
        SEQ = 512
        BATCH = 2

        def _rotate_half(t):
            x1, x2 = (t[..., :ROT // 2], t[..., ROT // 2:])
            return jnp.concatenate([-x2, x1], axis=-1)

        def _apply_rope(t, cos, sin):
            t_rot, t_pass = (t[..., :ROT], t[..., ROT:])
            t_rot = t_rot * cos + _rotate_half(t_rot) * sin
            return jnp.concatenate([t_rot, t_pass], axis=-1)
        b, n, _ = x.shape
        q = (x @ w_q).reshape(b, n, HEADS, HEAD_DIM).transpose(0, 2, 1, 3)
        k, v = jnp.split(x @ w_kv, 2, axis=-1)
        k = k.reshape(b, n, HEADS, HEAD_DIM).transpose(0, 2, 1, 3)
        v = v.reshape(b, n, HEADS, HEAD_DIM).transpose(0, 2, 1, 3)
        inv_freq = 1.0 / BASE ** (jnp.arange(0, ROT, 2, dtype=jnp.float32) / ROT)
        freqs = jnp.arange(n, dtype=jnp.float32)[:, None] * inv_freq[None, :]
        freqs = jnp.concatenate([freqs, freqs], axis=-1)
        cos, sin = (jnp.cos(freqs), jnp.sin(freqs))
        q = _apply_rope(q, cos, sin)
        k = _apply_rope(k, cos, sin)
        scale = HEAD_DIM ** (-0.5)
        scores = jnp.einsum('bhid,bhjd->bhij', q, k) * scale
        causal_mask = jnp.tril(jnp.ones((n, n), dtype=bool))
        scores = jnp.where(causal_mask, scores, jnp.finfo(scores.dtype).min)
        attn = jax.nn.softmax(scores, axis=-1)
        out = jnp.einsum('bhij,bhjd->bhid', attn, v)
        out = out.transpose(0, 2, 1, 3).reshape(b, n, HEADS * HEAD_DIM)
        return out @ w_out

    def _L0_ffn_ref(x, Wg, bg, W1, b1, W2, b2):
        import jax, jax.numpy as jnp
        import numpy as np
        H = 256
        I = 256
        E = 8
        B, S, Hd = x.shape
        xf = x.reshape(-1, Hd)
        logits = xf @ Wg + bg
        gates = jax.nn.softmax(logits, axis=-1)
        idx = jnp.argmax(gates, axis=-1)
        h = jax.nn.gelu(jnp.einsum('th,ehi->tei', xf, W1) + b1, approximate=False)
        y = jnp.einsum('tei,eih->teh', h, W2) + b2
        out = jnp.take_along_axis(y, idx[:, None, None], axis=1)[:, 0, :]
        return out.reshape(B, S, Hd)

    def _L1_attn_ref(x, Wq, Wk, Wv, Wo, Wd, bd, out_scale):
        import math
        import jax, jax.numpy as jnp
        import numpy as np
        DIM = 256
        B, T = (4, 512)
        Bsz, Tlen, dim = x.shape
        scale = 1.0 / math.sqrt(dim)
        q = jnp.einsum('btd,ed->bte', x, Wq)
        k = jnp.einsum('btd,ed->bte', x, Wk)
        v = jnp.einsum('btd,ed->bte', x, Wv)
        scores = jnp.einsum('btd,bsd->bts', q, k) * scale
        decay_logits = jnp.einsum('btd,ed->bte', x, Wd)[..., 0] + bd
        decay = jax.nn.sigmoid(decay_logits)
        pos = jnp.arange(Tlen)
        diff = pos[None, :] - pos[:, None]
        causal = (diff > 0).astype(x.dtype)
        log_decay = jnp.log(decay + 1e-08)
        dist = jnp.clip(diff.astype(x.dtype) - 1.0, 0.0)
        log_weights = log_decay[:, None, :] * dist[None, :, :]
        weights = jnp.exp(log_weights) * causal[None, :, :]
        scores = scores * weights
        retrieved = jnp.einsum('bts,bsd->btd', scores, v)
        out = jnp.einsum('btd,ed->bte', retrieved, Wo) * out_scale
        return out

    def _L1_ffn_ref(hidden_states, gate_w, w_gate_up, w_down, shared_w_gate_up, shared_w_down):
        import jax, jax.numpy as jnp
        import numpy as np
        E = 32
        K = 4
        H = 256
        I = 128
        B, S = (2, 512)
        T = B * S
        C = 256
        ROUTED_SCALE = 1.0

        def _silu_and_mul(gu):
            g, u = jnp.split(gu, 2, axis=-1)
            return jax.nn.silu(g) * u
        b, s, h = hidden_states.shape
        x = hidden_states.reshape(-1, h)
        t = x.shape[0]
        logits = x @ gate_w.T
        probs = jax.nn.softmax(logits, axis=-1)
        topk_w, topk_idx = jax.lax.top_k(probs, K)
        topk_w = topk_w / jnp.sum(topk_w, axis=-1, keepdims=True)
        topk_w = topk_w * ROUTED_SCALE
        e_flat = topk_idx.reshape(-1)
        w_flat = topk_w.reshape(-1)
        t_flat = jnp.repeat(jnp.arange(t), K)
        order = jnp.argsort(e_flat)
        e_s, w_s, t_s = (e_flat[order], w_flat[order], t_flat[order])
        counts = jax.ops.segment_sum(jnp.ones_like(e_s), e_s, num_segments=E)
        starts = jnp.cumsum(counts) - counts
        pos = jnp.arange(t * K) - starts[e_s]
        slot = jnp.minimum(pos, C)
        buf = jnp.zeros((E, C + 1, h), x.dtype).at[e_s, slot].set(x[t_s])
        gu = jnp.einsum('ech,ehi->eci', buf[:, :C], w_gate_up)
        expert_out = jnp.einsum('eci,eih->ech', _silu_and_mul(gu), w_down)
        expert_out = jnp.pad(expert_out, ((0, 0), (0, 1), (0, 0)))
        gate = jnp.where(pos < C, w_s, 0.0)[:, None]
        routed = jnp.zeros_like(x).at[t_s].add(expert_out[e_s, slot] * gate)
        shared = _silu_and_mul(x @ shared_w_gate_up) @ shared_w_down
        return (routed + shared).reshape(b, s, h)
    h = _L0_tok_ref(x, L0_tok_W, L0_tok_b, L0_tok_alpha)
    h = h + _L0_attn_ref(_layernorm(h, axis=-1), L0_attn_w_q, L0_attn_w_kv, L0_attn_w_out)
    h = h + _L0_ffn_ref(_layernorm(h, axis=-1), L0_ffn_Wg, L0_ffn_bg, L0_ffn_W1, L0_ffn_b1, L0_ffn_W2, L0_ffn_b2)
    h = h + _L1_attn_ref(_layernorm(h, axis=-1), L1_attn_Wq, L1_attn_Wk, L1_attn_Wv, L1_attn_Wo, L1_attn_Wd, L1_attn_bd, L1_attn_out_scale)
    h = h + _L1_ffn_ref(_layernorm(h, axis=-1), L1_ffn_gate_w, L1_ffn_w_gate_up, L1_ffn_w_down, L1_ffn_shared_w_gate_up, L1_ffn_shared_w_down)
    return h

_drawn_inputs = setup_inputs


def setup_inputs(seed=0):
    import zlib

    import numpy as np

    out = dict(_drawn_inputs(seed))
    spreads = {'L0_ffn_bg': (0.0, 0.1), 'L0_ffn_b1': (0.0, 0.453), 'L0_ffn_b2': (0.0, 0.1)}
    factors = {'L0_tok_b': 23.676,
     'L0_attn_w_q': 7.318,
     'L1_attn_Wq': 8.0,
     'L1_attn_Wk': 8.0,
     'L1_attn_Wv': 8.0,
     'L1_attn_Wo': 8.0,
     'L1_attn_Wd': 8.0,
     'L1_ffn_gate_w': 8.0,
     'L1_ffn_w_gate_up': 8.0,
     'L1_ffn_w_down': 8.0,
     'L1_ffn_shared_w_gate_up': 4.823,
     'L1_ffn_shared_w_down': 4.863}
    for name, (base, spread) in spreads.items():
        noise = np.random.default_rng([zlib.crc32(name.encode()), seed]).standard_normal(out[name].shape)
        drawn = base * np.exp(spread * noise) if base else spread * noise
        out[name] = jnp.asarray(drawn.astype(out[name].dtype))
    for name, factor in factors.items():
        out[name] = (out[name] * factor).astype(out[name].dtype)
    return out
```

```python
import concourse.bass as bass
from concourse import mybir
from contextlib import ExitStack

F32 = mybir.dt.float32
BF16 = mybir.dt.bfloat16
I32 = mybir.dt.int32
U32 = mybir.dt.uint32
ALU = mybir.AluOpType
ACT = mybir.ActivationFunctionType
AX = mybir.AxisListType

B, L, N = 16, 512, 250
D = 256
KF = 64
HT = N // 2
NT = 2 * B
DC = D // 128
H, HD = 16, 64
PAIRS = H // 2
EPS = 1e-5

E0 = 8
XROWS = B * N + 128
TILES0 = (B * N + E0 * 127) // 128
E1, TOPK, CAP1 = 32, 4, 256
ZROWS = 4
I1 = 128

C_DCT, C_COS, C_SIN, C_ID = 0, 256, 256 + N, 256 + 2 * N
C_MASK = C_ID + 128
C_UP = C_MASK + HT
C_IOTA = C_UP + HT
C_PART = C_IOTA + 32
C_SEQ = C_PART + 1
C_M128 = C_SEQ + 64
C_TRI = C_M128 + NT
C_BASE0 = C_TRI + E0 * E0
C_DIST = C_BASE0 + E0
C_LATER = C_DIST + 3 * HT
C_END = C_LATER + 3 * HT

UNITS = [("q", 0), ("k", 0), ("v", 0), ("q", 1), ("k", 1), ("v", 1),
         ("q", 2), ("k", 2), ("v", 2), ("q", 3), ("k", 3), ("v", 3)]
QK = [u for u in UNITS if u[0] != "v"]
STEPS = [[("xT", 0), ("q", 0), ("k", 0), ("turn", 2)],
         [("v", 0), ("freq", 0), ("turn", 3)],
         [("q", 1), ("k", 1)],
         [("v", 1), ("proj", 0), ("tok", 0)],
         [("q", 2), ("k", 2)],
         [("v", 2), ("proj", 1), ("turn", 0)],
         [("q", 3), ("k", 3)],
         [("v", 3), ("turn", 1)]]
PROLOGUE = [("freq", 0), ("tok", 0), ("xT", 0), ("freq", 1), ("tok", 1)] + UNITS


def in_step(b, t):
    names = STEPS[t]
    if isinstance(b, int):
        if b == 0:
            names = [n for n in names if n[0] != "proj" and n not in (("turn", 2), ("turn", 3))]
        if b >= B - 2:
            names = [n for n in names if n[0] not in ("freq", "tok")]
        if b >= B - 1:
            names = [n for n in names if n[0] in ("turn", "proj")]
        if b >= B:
            names = [n for n in names if n not in (("turn", 0), ("turn", 1))]
    return names


def in_batch(b):
    return [n for t in range(PAIRS) for n in in_step(b, t)]


class Step:

    def __init__(self, i, par):
        self.i, self.par = i, par
        self.b = 2 * i + par

    def gen(self, name):
        i, b = (self.i, self.b) if isinstance(self.i, int) else (1, 2 + self.par)
        k = len(PROLOGUE) + sum(len(in_batch(e)) for e in range(b)) + in_batch(self.b).index(name)
        per_two = len(in_batch(2))
        return k % 2, k // 2 + 1 + per_two * (self.i - i)

    def before(self):
        return Step(self.i, 0) if self.par else Step(self.i - 1, 1)


def within(b):
    return not isinstance(b, int) or 0 <= b < B


class Start:

    def gen(self, name):
        k = PROLOGUE.index(name)
        return k % 2, k // 2 + 1


def wait_for(eng, s, n):
    if not (isinstance(n, int) and n < 1):
        eng.wait_ge(s, n)
def stage_attention0(nc, g, x, w, xe):
    ctx = ExitStack()
    with ctx:
        def sb(name, shape, dt=F32):
            return ctx.enter_context(nc.sbuf_tensor(name, shape, dt))

        def sem(name):
            return ctx.enter_context(nc.semaphore(name))

        h, cst, mhalf = g.h, g.cst, g.mhalf
        idb = sb("idb", [HT, HT], BF16)
        maskb = sb("maskb", [HT, HT], BF16)
        tokw = sb("tokw", [KF + 1, D])
        alpha = sb("alpha", [HT, 1])
        wq = sb("wq", [128, DC, H * HD])
        wkv = sb("wkv", [128, DC, 2 * H * HD])
        wo = sb("wo", [128, 8, D])
        xin = sb("xin", [128, 4, N])
        freq = sb("freq", [KF + 1, N])
        stats = sb("stats", [HT, 2, 6])
        mv = sb("mv", [HT, 2, 2])
        rstd = sb("rstd", [HT, 2])
        xn = sb("xn", [HT, 2, D])
        xT = sb("xT", [128, DC, N])
        scrap = sb("scrap", [1, 1])
        zeros = sb("zeros", [128, ZROWS * D])
        raw = sb("raw", [128, 2, 2 * N])
        rot = sb("rot", [128, 2, 2 * N])
        qT = sb("qT", [128, 2, PAIRS, N])
        kT = sb("kT", [128, 2, PAIRS, N])
        v = sb("v", [HT, 2, 2, H * HD])
        nmax = sb("nmax", [HT, 2, 2, 2])
        sums = sb("sums", [HT, 2, 2, 4])
        rinv = sb("rinv", [HT, 2, 2, 4])
        pr = sb("pr", [HT, 2, 2, 3 * HT])
        prT = sb("prT", [HT, 2, 3 * HT])
        o = sb("o", [HT, 2, H * HD])
        oT = sb("oT", [128, 8, N])
        gen = [ctx.enter_context(nc.psum_tensor(f"gen{i}", [128, 512], F32)) for i in range(2)]
        S = ctx.enter_context(nc.psum_tensor("Sp", [128, 2, 512], F32))
        PT = ctx.enter_context(nc.psum_tensor("PT", [128, 2, 512], F32))
        O = [ctx.enter_context(nc.psum_tensor(f"O{i}", [128, 512], F32)) for i in range(2)]

        loaded = sem("loaded")
        ones_set = sem("ones_set")
        const_b = sem("const_b")
        xe_zero, xe_clear = sem("xe_zero"), sem("xe_clear")
        x_in = sem("x_in")
        filled = [sem("filled0"), sem("filled1")]
        emptied = [sem("emptied0"), sem("emptied1")]
        s_full = sem("s_full")
        nmax_set = sem("nmax_set")
        exped = sem("exped")
        pt_full = sem("pt_full")
        pt_out0 = sem("pt_out0")
        pt_out1 = sem("pt_out1")
        av_done = sem("av_done")
        rinv_set = sem("rinv_set")
        o_set = sem("o_set")
        shuf_set = sem("shuf_set")
        rot_set = sem("rot_set")
        cos_set = sem("cos_set")
        roped = sem("roped")
        ln_stat, ln_mv, ln_eps, ln_pow, ln_done = (sem(n) for n in ("ln_stat", "ln_mv", "ln_eps", "ln_pow", "ln_done"))

        ident = cst[:, C_ID:C_ID + 128]
        loads = [(cst[:, :], w["consts"]), (tokw[0:KF, :], w["L0_tok_W"]), (tokw[KF:KF + 1, :], w["L0_tok_b"].rearrange("(a d) -> a d", a=1)),
                 (alpha[:, :], w["L0_tok_alpha"].rearrange("(a d) -> a d", a=1).broadcast_to([HT, 1])),
                 (wq[:, :, :], w["L0_attn_w_q"].rearrange("(c p) n -> p c n", p=128)),
                 (wkv[:, :, :], w["L0_attn_w_kv"].rearrange("(c p) n -> p c n", p=128)),
                 (wo[:, :, :], w["L0_attn_w_out"].rearrange("(c p) n -> p c n", p=128))]
        LOADED = 16 * len(loads)
        block = ctx.enter_context(nc.Block())

        def halves(bank, width=N):
            return bank[:, 0:2 * width].rearrange("p (a n) -> p a n", a=2)

        def x_of(b):
            return x[bass.ds(b, 1), :, :].rearrange("b (p c) n -> p (b c) n", c=4)

        @block.sync
        def _(sp):
            for dst, src in loads:
                sp.dma_start(dst, src).then_inc(loaded, 16)
            sp.dma_start(xin[:, :, :], x_of(0)).then_inc(x_in, 16)
            sp.wait_ge(xe_zero, 1)
            for r in range(E1 * CAP1 // (128 * ZROWS)):
                sp.dma_start(xe[128 * ZROWS * r:128 * ZROWS * (r + 1), :].rearrange("(p a) d -> p (a d)", a=ZROWS),
                             zeros[:, :]).then_inc(xe_clear, 16)
            for b in range(2):
                bank, n = Start().gen(("freq", b))
                sp.wait_ge(emptied[bank], n)
                sp.dma_start(xin[:, :, :], x_of(b + 1)).then_inc(x_in, 16)

            def body(s):
                bank, n = s.gen(("freq", 0))
                sp.wait_ge(emptied[bank], n)
                sp.dma_start(xin[:, :, :], x_of(s.b + 3)).then_inc(x_in, 16)

            body(Step(0, 0))
            body(Step(0, 1))
            with sp.Fori(1, B // 2 - 2) as i:
                body(Step(i, 0))
                body(Step(i, 1))
            body(Step(B // 2 - 2, 0))
            sp.wait_ge(xe_clear, 16 * (E1 * CAP1 // (128 * ZROWS)))

        @block.tensor
        def _(pe):
            def fill(s, name):
                bank, n = s.gen(name)
                wait_for(pe, emptied[bank], n - 1)
                return gen[bank], filled[bank]

            def after(s, name):
                bank, n = s.gen(name)
                pe.wait_ge(emptied[bank], n)

            def freq_product(s, name, b):
                pe.wait_ge(x_in, 16 * b + 16)
                g, done = fill(s, name)
                for c in range(4):
                    mm = pe.matmul(g[0:KF, 0:N], cst[:, C_DCT + KF * c:C_DCT + KF * c + KF], xin[:, c, :],
                                   start=(c == 0), stop=(c == 3))
                mm.then_inc(done, 1)

            def tok_product(s, name, freq_name):
                g, done = fill(s, name)
                after(s, freq_name)
                for it in range(2):
                    mm = pe.matmul(g[0:HT, D * it:D * it + D], freq[:, HT * it:HT * it + HT], tokw[:, :],
                                   start=True, stop=True)
                mm.then_inc(done, 1)

            def turn_xn(s, name, b):
                g, done = fill(s, name)
                pe.wait_ge(ln_done, b + 1)
                for c in range(DC):
                    for it in range(2):
                        mm = pe.transpose(g[:, N * c + HT * it:N * c + HT * it + HT],
                                          xn[:, it, 128 * c:128 * c + 128], ident[0:HT, 0:HT])
                mm.then_inc(done, 1)

            def unit(s, u):
                kind, j = u
                g, done = fill(s, u)
                if kind == "v":
                    it, half = j // 2, j % 2
                    for c in range(DC):
                        mm = pe.matmul(g[0:HT, :], xT[:, c, HT * it:HT * it + HT],
                                       wkv[:, c, H * HD + 512 * half:H * HD + 512 * half + 512],
                                       start=(c == 0), stop=(c == DC - 1))
                else:
                    wt = wq if kind == "q" else wkv
                    for a in range(2):
                        col = 128 * (2 * j + a)
                        for c in range(DC):
                            mm = pe.matmul(g[:, N * a:N * a + N], wt[:, c, col:col + 128], xT[:, c, :],
                                           start=(c == 0), stop=(c == DC - 1))
                mm.then_inc(done, 1)

            def scores(s, t):
                pe.wait_ge(roped, len(QK) * s.b + 2 * (t // 2) + 2)
                wait_for(pe, exped, PAIRS * s.b + t)
                for it in range(2):
                    for hd in range(2):
                        r = slice(64 * hd, 64 * hd + 64)
                        at = HT * it
                        pe.matmul(S[0:HT, hd, at:at + HT * (it + 1)], qT[r, s.par, t, at:at + HT],
                                  kT[r, s.par, t, 0:HT * (it + 1)], start=True, stop=False)
                    for hd in range(2):
                        mm = pe.matmul(S[0:HT, hd, 2 * HT * it:2 * HT * it + HT], maskb[:, :], idb[:, :],
                                       start=False, stop=True)
                mm.then_inc(s_full, 1)

            def turn_probs(s, t):
                pe.wait_ge(exped, PAIRS * s.b + t + 1)
                wait_for(pe, pt_out0, PAIRS * s.b + t)
                wait_for(pe, pt_out1, PAIRS * s.b + t)
                for hd in range(2):
                    for j in range(3):
                        mm = pe.transpose(PT[0:HT, hd, HT * j:HT * j + HT], pr[:, t % 2, hd, HT * j:HT * j + HT],
                                          ident[0:HT, 0:HT])
                mm.then_inc(pt_full, 1)

            def weigh_values(s, t):
                grp = t // 2
                pe.wait_ge(pt_out0, PAIRS * s.b + t + 1)
                pe.wait_ge(pt_out1, PAIRS * s.b + t + 1)
                if t % 2 == 0:
                    wait_for(pe, o_set, 4 * s.b + grp - 1)
                for hd in range(2):
                    hh = 2 * t + hd
                    hc = slice(HD * hh, HD * hh + HD)
                    at = HD * (hh % 4)
                    pe.matmul(O[grp % 2][0:HT, at:at + HD], prT[:, hd, 0:HT], v[:, s.par, 0, hc],
                              start=True, stop=True)
                    pe.matmul(O[grp % 2][0:HT, 256 + at:256 + at + HD], prT[:, hd, HT:2 * HT], v[:, s.par, 0, hc],
                              start=True, stop=False)
                    mm = pe.matmul(O[grp % 2][0:HT, 256 + at:256 + at + HD], prT[:, hd, 2 * HT:3 * HT],
                                   v[:, s.par, 1, hc], start=False, stop=True)
                mm.then_inc(av_done, 1)

            def turn_o(s, grp, b):
                g, done = fill(s, ("turn", grp))
                pe.wait_ge(o_set, 4 * b + grp + 1)
                for cc in range(2):
                    for it in range(2):
                        at = N * cc + HT * it
                        mm = pe.transpose(g[:, at:at + HT], o[:, it, 256 * grp + 128 * cc:256 * grp + 128 * cc + 128],
                                          ident[0:HT, 0:HT])
                mm.then_inc(done, 1)

            def project(s, it):
                g, done = fill(s, ("proj", it))
                if it == 0:
                    after(s, ("turn", 2))
                    after(s, ("turn", 3))
                for c in range(8):
                    mm = pe.matmul(g[0:HT, 0:D], oT[:, c, HT * it:HT * it + HT], wo[:, c, :], start=(c == 0), stop=(c == 7))
                mm.then_inc(done, 1)

            def body(s):
                before = s.before()
                for t in range(PAIRS):
                    p = (s, t - 1) if t else (before, PAIRS - 1)
                    names = in_step(s.b, t)
                    if ("xT", 0) in names:
                        turn_xn(s, ("xT", 0), s.b + 1)
                    if within(s.b):
                        scores(s, t)
                    if within(p[0].b):
                        turn_probs(*p)
                    if ("xT", 0) in names:
                        after(s, ("xT", 0))
                    for n in names:
                        if n in UNITS:
                            unit(s, n)
                        elif n[0] == "proj":
                            project(s, n[1])
                        elif n[0] == "freq":
                            freq_product(s, n, s.b + 2)
                        elif n[0] == "tok":
                            tok_product(s, n, ("freq", 0))
                    if within(p[0].b):
                        weigh_values(*p)
                    for n in names:
                        if n[0] == "turn":
                            turn_o(s, n[1], s.b if n[1] < 2 else before.b)

            st = Start()
            pe.wait_ge(loaded, LOADED)
            pe.wait_ge(ones_set, 2)
            pe.wait_ge(const_b, 2)
            freq_product(st, ("freq", 0), 0)
            tok_product(st, ("tok", 0), ("freq", 0))
            turn_xn(st, ("xT", 0), 0)
            after(st, ("xT", 0))
            freq_product(st, ("freq", 1), 1)
            tok_product(st, ("tok", 1), ("freq", 1))
            for u in UNITS:
                unit(st, u)
            body(Step(0, 0))
            body(Step(0, 1))
            with pe.Fori(1, B // 2 - 1) as i:
                body(Step(i, 0))
                body(Step(i, 1))
            for b in range(B - 2, B + 1):
                body(Step(b // 2, b % 2))

        @block.scalar
        def _(act):
            def evict(s, name, dst, src, scale=None):
                bank, n = s.gen(name)
                act.wait_ge(filled[bank], n)
                if scale is None:
                    act.copy(dst, src(gen[bank])).then_inc(emptied[bank], 1)
                else:
                    act.mul(dst, src(gen[bank]), scale).then_inc(emptied[bank], 1)

            def freq_out(s, name):
                evict(s, name, freq[0:KF, :], lambda g: g[0:KF, 0:N])

            def xT_out(s, name):
                evict(s, name, xT[:, :, :], halves)

            def unit_out(s, u, par, b):
                kind, j = u
                if kind == "v":
                    evict(s, u, v[:, par, j // 2, 512 * (j % 2):512 * (j % 2) + 512], lambda g: g[0:HT, :])
                else:
                    k = QK.index(u)
                    n = len(QK) * b + k - 1
                    wait_for(act, cos_set, n)
                    wait_for(act, shuf_set, n)
                    evict(s, u, raw[:, k % 2, :], lambda g: g[:, 0:2 * N], scale=HD ** -0.5 if kind == "q" else None)

            def exponentials(s, t):
                act.wait_ge(nmax_set, PAIRS * s.b + t + 1)
                grp = t // 2
                for it in range(2):
                    for hd in range(2):
                        c = slice(HT * it, HT * it + HT * (it + 1))
                        e = act.activation(pr[:, t % 2, hd, c], S[0:HT, hd, c], ACT.Exp,
                                           bias=nmax[:, t % 2, it, hd:hd + 1],
                                           accum_out=sums[:, grp % 2, it, 2 * (t % 2) + hd:2 * (t % 2) + hd + 1])
                e.then_inc(exped, 1)

            def probs_out(s, t):
                act.wait_ge(pt_full, PAIRS * s.b + t + 1)
                act.copy(prT[:, 0, :], PT[0:HT, 0, 0:3 * HT]).then_inc(pt_out0, 1)

            def tok_out(s, name, b):
                bank, n = s.gen(name)
                act.wait_ge(filled[bank], n)
                act.activation(h[:, bass.ds(b * (2 * D), 2 * D)], gen[bank][0:HT, :], ACT.Copy,
                               scale=alpha[:, 0:1]).then_inc(emptied[bank], 1)

            def turn_out(s, grp):
                evict(s, ("turn", grp), oT[:, 2 * grp:2 * grp + 2, :], halves)

            def body(s):
                before = s.before()
                for t in range(PAIRS):
                    p = (s, t - 1) if t else (before, PAIRS - 1)
                    names = in_step(s.b, t)
                    if ("xT", 0) in names:
                        xT_out(s, ("xT", 0))
                    if within(p[0].b):
                        probs_out(*p)
                    if within(s.b):
                        exponentials(s, t)
                    for n in names:
                        if n in UNITS:
                            unit_out(s, n, 1 - s.par, s.b + 1)
                        elif n[0] == "freq":
                            freq_out(s, n)
                        elif n[0] == "tok":
                            tok_out(s, n, s.b + 2)
                        elif n[0] == "turn":
                            turn_out(s, n[1])

            st = Start()
            act.wait_ge(loaded, LOADED)
            act.copy(idb[:, :], cst[0:HT, C_ID:C_ID + HT]).then_inc(const_b, 1)
            act.copy(maskb[:, :], cst[0:HT, C_MASK:C_MASK + HT]).then_inc(const_b, 1)
            act.copy(g.upb[:, :], cst[0:HT, C_UP:C_UP + HT])
            freq_out(st, ("freq", 0))
            tok_out(st, ("tok", 0), 0)
            xT_out(st, ("xT", 0))
            freq_out(st, ("freq", 1))
            tok_out(st, ("tok", 1), 1)
            for u in UNITS:
                unit_out(st, u, 0, 0)
            body(Step(0, 0))
            body(Step(0, 1))
            with act.Fori(1, B // 2 - 1) as i:
                body(Step(i, 0))
                body(Step(i, 1))
            for b in range(B - 2, B + 1):
                body(Step(b // 2, b % 2))

        @block.vector
        def _(dve):
            def settle(s, n):
                dve.wait_ge(s, n)
                dve.memset(scrap[0:1, 0:1], 0.0)

            def h_tiles(b):
                return h[:, bass.ds(b * (2 * D), 2 * D)]

            def norm_stats(s, name, b):
                bank, n = s.gen(name)
                settle(emptied[bank], n)
                for it in range(2):
                    dve.bn_stats(stats[:, it, :], h[:, bass.ds(b * (2 * D) + D * it, D)]).then_inc(ln_stat, 1)
                settle(ln_stat, 2 * b + 2)
                for it in range(2):
                    dve.bn_aggr(mv[:, it, :], stats[:, it, :]).then_inc(ln_mv, 1)
                dve.wait_ge(ln_mv, 2 * b + 2)
                dve.tensor_scalar(rstd[:, :], mv[:, :, 1], EPS, None, ALU.add).then_inc(ln_eps, 1)

            def norm(b):
                dve.wait_ge(ln_pow, b + 1)
                for it in range(2):
                    e = dve.tensor_scalar(xn[:, it, :], h[:, bass.ds(b * (2 * D) + D * it, D)], mv[:, it, 0:1],
                                          rstd[:, it:it + 1], ALU.subtract, ALU.mult)
                e.then_inc(ln_done, 1)

            def maxima(s, t):
                dve.wait_ge(s_full, PAIRS * s.b + t + 1)
                for it in range(2):
                    e = dve.tensor_reduce(nmax[:, t % 2, it, :], S[0:HT, :, HT * it:HT * it + HT * (it + 1)],
                                          AX.X, ALU.max, negate=True)
                e.then_inc(nmax_set, 1)

            def probs_out(s, t):
                dve.wait_ge(pt_full, PAIRS * s.b + t + 1)
                dve.tensor_copy(prT[:, 1, :], PT[0:HT, 1, 0:3 * HT]).then_inc(pt_out1, 1)

            def rope_parts(s, u, par, b):
                kind, j = u
                k = QK.index(u)
                bank, n = s.gen(u)
                cos = cst[:, C_COS:C_COS + N].unsqueeze(1).broadcast_to([128, 2, N])
                src = raw[:, k % 2, :].rearrange("p (a n) -> p a n", a=2)
                dve.wait_ge(emptied[bank], n)
                wait_for(dve, roped, len(QK) * b + k - 1)
                dve.tensor_tensor(rope_to(u, par), src, cos, ALU.mult).then_inc(cos_set, 1)
                dve.stream_shuffle(rot[:, k % 2, :], raw[:, k % 2, :], [(i + 16) % 32 for i in range(32)]).then_inc(shuf_set, 1)

            def rope_sum(u, par, b):
                k = QK.index(u)
                turned = rot[:, k % 2, :].rearrange("p (a n) -> p a n", a=2)
                dve.wait_ge(cos_set, len(QK) * b + k + 1)
                dve.wait_ge(rot_set, len(QK) * b + k + 1)
                dve.tensor_tensor(rope_to(u, par), rope_to(u, par), turned, ALU.add).then_inc(roped, 1)

            def rope_to(u, par):
                return (qT if u[0] == "q" else kT)[:, par, 2 * u[1]:2 * u[1] + 2, :]

            def normalise(s, grp):
                G = 4 * s.b + grp + 1
                dve.wait_ge(av_done, PAIRS * s.b + 2 * grp + 2)
                dve.reciprocal(rinv[:, grp % 2, :, :], sums[:, grp % 2, :, :]).then_inc(rinv_set, 1)
                dve.wait_ge(rinv_set, G)
                for it in range(2):
                    e = dve.tensor_tensor(o[:, it, 256 * grp:256 * grp + 256].rearrange("p (h d) -> p h d", d=HD),
                                      O[grp % 2][0:HT, 256 * it:256 * it + 256].rearrange("p (h d) -> p h d", d=HD),
                                      rinv[:, grp % 2, it, :].unsqueeze(2).broadcast_to([HT, 4, HD]), ALU.mult)
                e.then_inc(o_set, 1)

            def add_attention(s, it, b):
                bank, n = s.gen(("proj", it))
                tile = h[:, bass.ds(b * (2 * D) + D * it, D)]
                dve.wait_ge(filled[bank], n)
                dve.tensor_tensor(tile, gen[bank][0:HT, 0:D], tile, ALU.add).then_inc(emptied[bank], 1)

            def body(s):
                before = s.before()
                for t in range(PAIRS):
                    p = (s, t - 1) if t else (before, PAIRS - 1)
                    names = in_step(s.b, t)
                    if within(s.b):
                        maxima(s, t)
                    if within(p[0].b):
                        probs_out(*p)
                    if t == 1 and within(before.b):
                        normalise(before, 3)
                    if t in (3, 5, 7) and within(s.b):
                        normalise(s, (t - 3) // 2)
                    if t == 0 and within(s.b) and within(before.b):
                        rope_sum(QK[-1], s.par, s.b)
                    if t and within(s.b + 1):
                        rope_sum(QK[t - 1], 1 - s.par, s.b + 1)
                    if within(s.b + 1):
                        rope_parts(s, QK[t], 1 - s.par, s.b + 1)
                    if t == 4 and within(s.b + 2):
                        norm_stats(s, ("tok", 0), s.b + 2)
                    if t == 5 and within(s.b + 2):
                        norm(s.b + 2)
                    for n in names:
                        if n[0] == "proj":
                            add_attention(s, n[1], before.b)

            st = Start()
            dve.memset(freq[KF:KF + 1, :], 1.0).then_inc(ones_set, 1)
            dve.memset(zeros[:, :], 0.0).then_inc(xe_zero, 1)
            dve.memset(g.onesb[:, :], 1.0)
            dve.wait_ge(loaded, LOADED)
            norm_stats(st, ("tok", 0), 0)
            norm(0)
            bank, n = st.gen(("xT", 0))
            norm_stats(st, ("tok", 1), 1)
            dve.wait_ge(filled[bank], n)
            norm(1)
            for u in QK:
                rope_parts(st, u, 0, 0)
                rope_sum(u, 0, 0)
            body(Step(0, 0))
            body(Step(0, 1))
            with dve.Fori(1, B // 2 - 1) as i:
                body(Step(i, 0))
                body(Step(i, 1))
            for b in range(B - 2, B + 1):
                body(Step(b // 2, b % 2))

        @block.gpsimd
        def _(pool):
            def power(b):
                pool.wait_ge(ln_eps, b + 1)
                pool.tensor_tensor(rstd[:, :], rstd[:, :], mhalf[:, :], ALU.pow).then_inc(ln_pow, 1)

            def times_sine(b, k):
                pool.wait_ge(shuf_set, len(QK) * b + k + 1)
                turned = rot[:, k % 2, :].rearrange("p (a n) -> p a n", a=2)
                pool.tensor_tensor(turned, turned, cst[:, C_SIN:C_SIN + N].unsqueeze(1).broadcast_to([128, 2, N]),
                                   ALU.mult).then_inc(rot_set, 1)

            def body(s):
                for k in range(len(QK)):
                    if within(s.b + 1):
                        times_sine(s.b + 1, k)
                    if k == 4 and within(s.b + 2):
                        power(s.b + 2)

            pool.memset(mhalf[:, :], -0.5).then_inc(ones_set, 1)
            pool.wait_ge(ones_set, 2)
            pool.wait_ge(loaded, LOADED)
            power(0)
            power(1)
            for k in range(len(QK)):
                times_sine(0, k)
            body(Step(0, 0))
            body(Step(0, 1))
            with pool.Fori(1, B // 2 - 1) as i:
                body(Step(i, 0))
                body(Step(i, 1))
            for b in range(B - 2, B):
                body(Step(b // 2, b % 2))
def stage_ffn0(nc, g, w, xs, ys):
    ctx = ExitStack()
    with ctx:
        def sb(name, shape, dt=F32):
            return ctx.enter_context(nc.sbuf_tensor(name, shape, dt))

        def sem(name):
            s = ctx.enter_context(nc.semaphore(name))
            assert not used_before(nc, [s])
            return s

        def ps(name):
            return ctx.enter_context(nc.psum_tensor(name, [128, 512], F32))

        h, cst = g.h, g.cst
        ident = cst[:, C_ID:C_ID + 128]
        SLOTS = 4
        xn = sb("b_xn", [HT, SLOTS, 2, D])
        stats = sb("b_stats", [HT, 2, 6])
        mv = sb("b_mv", [HT, 2, 2])
        rstd = sb("b_rstd", [HT, 2])
        xT = sb("b_xT", [128, DC, N])
        lg = sb("b_lg", [HT, 2, E0])
        top = sb("b_top", [HT, 2, 8])
        topi = sb("b_topi", [HT, 2, 8], U32)
        pick = sb("b_pick", [HT, 2])
        hot = sb("b_hot", [HT, 2, E0], BF16)
        rank = sb("b_rank", [HT, 2, E0])
        row = sb("b_row", [HT, 2])
        rowi = sb("b_rowi", [HT, SLOTS, 2], U32)
        fill_row = sb("b_fill", [128, E0])
        picks = sb("b_picks", [HT, NT])
        rows = sb("b_rows", [HT, NT])
        more = sb("b_more", [128, E0, NT])
        ntile = sb("b_ntile", [128, E0])
        tri = sb("b_tri", [128, E0, E0])
        tend = sb("b_tend", [128, E0])
        shift = sb("b_shift", [128, E0])
        hots = sb("b_hots", [HT, NT, E0])
        move = sb("b_move", [HT, NT])
        padf = sb("b_padf", [128, E0])
        padr = sb("b_padr", [128, E0])
        padi = sb("b_padi", [128, E0], U32)
        zero = sb("b_zero", [128, D])
        over = sb("b_over", [1, TILES0, E0])
        te = sb("b_te", [1, 3, TILES0])
        tfirst = sb("b_tfirst", [1, TILES0])
        tab = sb("b_tab", [1, 2 * TILES0], I32)
        scrap = sb("b_scrap", [1, 8])
        wgate = sb("b_wgate", [128, DC, E0])
        bgate = sb("b_bgate", [HT, E0])
        w1 = sb("b_w1", [128, E0 * DC * D])
        w2 = sb("b_w2", [128, E0 * DC * D])
        b1 = sb("b_b1", [128, E0 * D])
        b2 = sb("b_b2", [128, E0 * D])
        W_IN = 16 * (2 * E0 + 2)
        gate_in, w_in = sem("b_gate_in"), sem("b_w_in")

        ln_stat, ln_mv, ln_eps, ln_pow, ln_done = (sem("b_" + n) for n in ("ln_stat", "ln_mv", "ln_eps", "ln_pow", "ln_done"))
        t_full, t_out = sem("b_t_full"), sem("b_t_out")
        lg_full, lg_out = sem("b_lg_full"), sem("b_lg_out")
        topped, indexed, picked, hot_set = (sem("b_" + n) for n in ("topped", "indexed", "picked", "hot_set"))
        rank_full, ranked, masked, rowed, row_set, counted = (sem("b_" + n) for n in ("rank_full", "ranked", "masked", "rowed", "row_set", "counted"))
        scattered = [sem(f"b_scattered{i}") for i in range(SLOTS)]
        zeroed, padded, chain, tabled, pad_set = (sem("b_" + n) for n in ("zeroed", "padded", "chain", "tabled", "pad_set"))

        tps, lps, rps = ps("b_tps"), ps("b_lps"), ps("b_rps")
        block = ctx.enter_context(nc.Block())

        @block.sync
        def _(sp):
            sp.dma_start(wgate[:, :, :], w["L0_ffn_Wg"].rearrange("(c p) e -> p c e", p=128)).then_inc(gate_in, 16)
            sp.dma_start(bgate[:, :], w["L0_ffn_bg"].rearrange("(a e) -> a e", a=1).broadcast_to([HT, E0])).then_inc(gate_in, 16)
            for e in range(E0):
                at = slice(DC * D * e, DC * D * (e + 1))
                for dst, src in ((w1, w["L0_ffn_W1"]), (w2, w["L0_ffn_W2"])):
                    sp.dma_start(dst[:, at].rearrange("p (c i) -> p c i", c=DC),
                                 src[e].rearrange("(c p) i -> p c i", p=128)).then_inc(w_in, 16)
            for dst, src in ((b1, w["L0_ffn_b1"]), (b2, w["L0_ffn_b2"])):
                sp.dma_start(dst[:, :], src.rearrange("(a e) i -> a (e i)", a=1).broadcast_to([128, E0 * D])).then_inc(w_in, 16)

        @block.tensor
        def _(pe):
            def turn(b, slot):
                pe.wait_ge(ln_done, b + 1)
                for c in range(DC):
                    for it in range(2):
                        mm = pe.transpose(tps[:, N * c + HT * it:N * c + HT * it + HT],
                                          xn[:, slot, it, 128 * c:128 * c + 128], ident[0:HT, 0:HT])
                mm.then_inc(t_full, 1)

            def logits(b):
                pe.wait_ge(t_out, b + 1)
                pe.wait_ge(lg_out, b)
                for it in range(2):
                    for c in range(DC):
                        mm = pe.matmul(lps[0:HT, E0 * it:E0 * it + E0], xT[:, c, HT * it:HT * it + HT],
                                       wgate[:, c, :], start=(c == 0), stop=(c == DC - 1))
                mm.then_inc(lg_full, 1)

            def ranks(b):
                pe.wait_ge(hot_set, b + 1)
                pe.wait_ge(counted, b)
                pe.matmul(rps[0:HT, 0:E0], g.upb[:, :], hot[:, 0, :], start=True, stop=True)
                pe.matmul(rps[0:HT, E0:2 * E0], g.upb[:, :], hot[:, 1, :], start=True, stop=False)
                pe.matmul(rps[0:HT, E0:2 * E0], g.onesb[:, 0:HT], hot[:, 0, :], start=False, stop=True)
                pe.matmul(rps[:, 2 * E0:3 * E0], g.onesb[:, :], hot[:, 0, :], start=True, stop=False)
                pe.matmul(rps[:, 2 * E0:3 * E0], g.onesb[:, :], hot[:, 1, :], start=False, stop=True).then_inc(rank_full, 1)

            def body(b, q, last=False):
                if not last:
                    turn(b + 1, (q + 1) % SLOTS)
                ranks(b)
                if not last:
                    logits(b + 1)

            pe.wait_ge(gate_in, 32)
            turn(0, 0)
            logits(0)
            for q in range(SLOTS):
                body(q, q)
            with pe.Fori(1, B // SLOTS - 1) as i:
                for q in range(SLOTS):
                    body(SLOTS * i + q, q)
            for q in range(SLOTS):
                body(B - SLOTS + q, q, last=(q == SLOTS - 1))

        @block.scalar
        def _(act):
            def turn_out(b):
                act.wait_ge(t_full, b + 1)
                if not (isinstance(b, int) and b == 0):
                    act.wait_ge(lg_full, b)
                act.copy(xT[:, :, :], tps[:, 0:2 * N].rearrange("p (c n) -> p c n", c=DC)).then_inc(t_out, 1)

            turn_out(0)
            turn_out(1)
            with act.Fori(2, B) as b:
                turn_out(b)

        @block.vector
        def _(dve):
            def settle(s, n):
                dve.wait_ge(s, n)
                dve.memset(scrap[0:1, 0:1], 0.0)

            def norm(b, slot, i):
                for it in range(2):
                    dve.bn_stats(stats[:, it, :], h[:, bass.ds(b * (2 * D) + D * it, D)]).then_inc(ln_stat, 1)
                settle(ln_stat, 2 * b + 2)
                for it in range(2):
                    dve.bn_aggr(mv[:, it, :], stats[:, it, :]).then_inc(ln_mv, 1)
                dve.wait_ge(ln_mv, 2 * b + 2)
                dve.tensor_scalar(rstd[:, :], mv[:, :, 1], EPS, None, ALU.add).then_inc(ln_eps, 1)
                if i is not None:
                    dve.wait_ge(scattered[slot], 32 * i)
                dve.wait_ge(ln_pow, b + 1)
                for it in range(2):
                    e = dve.tensor_scalar(xn[:, slot, it, :], h[:, bass.ds(b * (2 * D) + D * it, D)], mv[:, it, 0:1],
                                          rstd[:, it:it + 1], ALU.subtract, ALU.mult)
                e.then_inc(ln_done, 1)

            def choose(b):
                dve.wait_ge(lg_full, b + 1)
                dve.tensor_tensor(lg[:, :, :], lps[0:HT, 0:2 * E0].rearrange("p (t e) -> p t e", t=2),
                                  bgate[:, :].unsqueeze(1).broadcast_to([HT, 2, E0]), ALU.add).then_inc(lg_out, 1)
                settle(lg_out, b + 1)
                for it in range(2):
                    dve.max(top[:, it, :], lg[:, it, :]).then_inc(topped, 1)
                settle(topped, 2 * b + 2)
                for it in range(2):
                    dve.max_index(topi[:, it, :], top[:, it, :], lg[:, it, :]).then_inc(indexed, 1)
                dve.wait_ge(indexed, 2 * b + 2)
                dve.tensor_copy(pick[:, :], topi[:, :, 0]).then_inc(picked, 1)
                dve.wait_ge(picked, b + 1)
                dve.tensor_copy(picks[:, bass.ds(2 * b, 2)], pick[:, :])
                dve.tensor_tensor(hot[:, :, :], pick[:, :].unsqueeze(2).broadcast_to([HT, 2, E0]),
                                  cst[0:HT, C_IOTA:C_IOTA + E0].unsqueeze(1).broadcast_to([HT, 2, E0]),
                                  ALU.is_equal).then_inc(hot_set, 1)

            def place(b, slot):
                dve.wait_ge(rank_full, b + 1)
                dve.wait_ge(counted, b)
                dve.tensor_tensor(rank[:, :, :], rps[0:HT, 0:2 * E0].rearrange("p (t e) -> p t e", t=2),
                                  fill_row[0:HT, :].unsqueeze(1).broadcast_to([HT, 2, E0]), ALU.add).then_inc(ranked, 1)
                dve.wait_ge(ranked, b + 1)
                dve.tensor_tensor(rank[:, :, :], rank[:, :, :], hot[:, :, :], ALU.mult).then_inc(masked, 1)
                dve.tensor_tensor(fill_row[:, :], rps[:, 2 * E0:3 * E0], fill_row[:, :], ALU.add).then_inc(counted, 1)
                dve.wait_ge(masked, b + 1)
                dve.tensor_reduce(row[:, :], rank[:, :, :], AX.X, ALU.add).then_inc(rowed, 1)
                dve.wait_ge(rowed, b + 1)
                dve.tensor_copy(rows[:, bass.ds(2 * b, 2)], row[:, :])
                dve.tensor_copy(rowi[:, slot, :], row[:, :]).then_inc(row_set, 1)

            steps = [0]

            def then(ins):
                steps[0] += 1
                ins.then_inc(chain, 1)
                dve.wait_ge(chain, steps[0])

            dve.wait_ge(gate_in, 32)
            dve.memset(zero[:, :], 0.0).then_inc(zeroed, 1)
            then(dve.tensor_copy(fill_row[:, :], cst[:, C_BASE0:C_BASE0 + E0]))
            norm(0, 0, None)
            for b in range(SLOTS):
                norm(b + 1, (b + 1) % SLOTS, 1 if b == SLOTS - 1 else None)
                choose(b)
                place(b, b)
            with dve.Fori(1, B // SLOTS - 1) as i:
                for q in range(SLOTS):
                    b = SLOTS * i + q
                    norm(b + 1, (q + 1) % SLOTS, i + (q == SLOTS - 1))
                    choose(b)
                    place(b, q)
            for q in range(SLOTS):
                b = B - SLOTS + q
                if q < SLOTS - 1:
                    norm(b + 1, q + 1, B // SLOTS - 1)
                choose(b)
                place(b, q)

            dve.wait_ge(counted, B)
            then(dve.tensor_tensor(padr[:, :], fill_row[:, :], cst[:, C_PART:C_PART + 1].broadcast_to([128, E0]), ALU.add))
            dve.tensor_copy(padi[:, :], padr[:, :]).then_inc(pad_set, 1)
            then(dve.tensor_tensor(padf[:, :], fill_row[:, :], cst[:, C_BASE0:C_BASE0 + E0], ALU.subtract))
            then(dve.tensor_tensor(more[:, :, :], padf[:, :].unsqueeze(2).broadcast_to([128, E0, NT]),
                                   cst[:, C_M128:C_M128 + NT].unsqueeze(1).broadcast_to([128, E0, NT]), ALU.is_gt))
            then(dve.tensor_reduce(ntile[:, :], more[:, :, :], AX.X, ALU.add))
            then(dve.tensor_tensor(tri[:, :, :], ntile[:, :].unsqueeze(1).broadcast_to([128, E0, E0]),
                                   cst[:, C_TRI:C_TRI + E0 * E0].rearrange("p (a b) -> p a b", a=E0), ALU.mult))
            then(dve.tensor_reduce(tend[:, :], tri[:, :, :], AX.X, ALU.add))
            then(dve.tensor_tensor(shift[:, :], tend[:, :], ntile[:, :], ALU.subtract))
            then(dve.scalar_tensor_tensor(out=shift[:, :], in0=shift[:, :], scalar=128.0, in1=cst[:, C_BASE0:C_BASE0 + E0],
                                          op0=ALU.mult, op1=ALU.subtract))
            then(dve.tensor_tensor(hots[:, :, :], picks[:, :].unsqueeze(2).broadcast_to([HT, NT, E0]),
                                   cst[0:HT, C_IOTA:C_IOTA + E0].unsqueeze(1).broadcast_to([HT, NT, E0]), ALU.is_equal))
            then(dve.tensor_tensor(hots[:, :, :], hots[:, :, :], shift[0:HT, :].unsqueeze(1).broadcast_to([HT, NT, E0]), ALU.mult))
            then(dve.tensor_reduce(move[:, :], hots[:, :, :], AX.X, ALU.add))
            then(dve.tensor_tensor(move[:, :], move[:, :], rows[:, :], ALU.add))
            then(dve.tensor_copy(g.back[:, :], move[:, :]))
            then(dve.tensor_tensor(over[:, :, :], cst[0:1, C_SEQ:C_SEQ + TILES0].unsqueeze(2).broadcast_to([1, TILES0, E0]),
                                   tend[0:1, :].unsqueeze(1).broadcast_to([1, TILES0, E0]), ALU.is_ge))
            then(dve.tensor_reduce(te[:, 0, :], over[:, :, :], AX.X, ALU.add))
            then(dve.tensor_scalar(te[:, 1, :], te[:, 0, :], float(E0 - 1), None, ALU.min))
            then(dve.tensor_tensor(over[:, :, :], te[:, 1, :].unsqueeze(2).broadcast_to([1, TILES0, E0]),
                                   cst[0:1, C_IOTA:C_IOTA + E0].unsqueeze(1).broadcast_to([1, TILES0, E0]), ALU.is_equal))
            then(dve.tensor_tensor(over[:, :, :], over[:, :, :], shift[0:1, :].unsqueeze(1).broadcast_to([1, TILES0, E0]), ALU.mult))
            then(dve.tensor_reduce(te[:, 2, :], over[:, :, :], AX.X, ALU.add))
            then(dve.scalar_tensor_tensor(out=te[:, 2, :], in0=cst[0:1, C_SEQ:C_SEQ + TILES0], scalar=128.0, in1=te[:, 2, :],
                                          op0=ALU.mult, op1=ALU.subtract))
            then(dve.tensor_scalar(te[:, 2, :], te[:, 2, :], -float((E0 - 1) * XROWS), None, ALU.add))
            then(dve.tensor_scalar(tfirst[:, :], te[:, 0, :], float(E0 - 1), None, ALU.is_le))
            then(dve.tensor_tensor(te[:, 2, :], te[:, 2, :], tfirst[:, :], ALU.mult))
            then(dve.tensor_scalar(te[:, 2, :], te[:, 2, :], float((E0 - 1) * XROWS), None, ALU.add))
            dve.tensor_copy(tab[:, 0:TILES0], te[:, 1, :]).then_inc(tabled, 1)
            dve.tensor_copy(tab[:, TILES0:2 * TILES0], te[:, 2, :]).then_inc(tabled, 1)

        @block.gpsimd
        def _(pool):
            def power(b):
                pool.wait_ge(ln_eps, b + 1)
                pool.tensor_tensor(rstd[:, :], rstd[:, :], g.mhalf[:, :], ALU.pow).then_inc(ln_pow, 1)

            def scatter(b, slot):
                pool.wait_ge(row_set, b + 1)
                pool.tensor_tensor(scrap[0:1, 4 + slot:5 + slot], scrap[0:1, 2:3], scrap[0:1, 3:4], ALU.add)
                for it in range(2):
                    pool.indirect_dma_start(xs[:, :], bass.IndirectOffsetOnAxis(ap=rowi[:, slot, it:it + 1], axis=0),
                                            xn[:, slot, it, :], None, bounds_check=E0 * XROWS - 1,
                                            oob_is_err=True).then_inc(scattered[slot], 16)

            pool.memset(scrap[0:1, 2:4], 0.0).then_inc(zeroed, 1)
            pool.wait_ge(zeroed, 2)
            power(0)
            with pool.Fori(0, B // SLOTS - 1) as i:
                for q in range(SLOTS):
                    power(SLOTS * i + q + 1)
                    scatter(SLOTS * i + q, q)
            for q in range(SLOTS):
                if q < SLOTS - 1:
                    power(B - SLOTS + q + 1)
                scatter(B - SLOTS + q, q)
            pool.wait_ge(pad_set, 1)
            for e in range(E0):
                pool.indirect_dma_start(xs[:, :], bass.IndirectOffsetOnAxis(ap=padi[:, e:e + 1], axis=0),
                                        zero[:, :], None, bounds_check=E0 * XROWS - 1, oob_is_err=True).then_inc(padded, 16)

        RING = 3
        xg = sb("b_xg", [128, RING, D])
        xgT = sb("b_xgT", [128, RING, D])
        pre = sb("b_pre", [128, RING, D])
        act1 = sb("b_act", [128, RING, D])
        aT = sb("b_aT", [128, RING, D])
        yo = sb("b_yo", [128, RING, D])
        pT = [tps, lps]
        pA, pB = rps, ps("b_pB")
        x_in = [sem(f"b_x_in{i}") for i in range(RING)]
        xgt_full, xgt_out, a_full, a_pre, a_act, at_full, at_out, y_full, y_set = (sem("b_" + n) for n in (
            "xgt_full", "xgt_out", "a_full", "a_pre", "a_act", "at_full", "at_out", "y_full", "y_set"))
        y_out = [sem(f"b_y_out{i}") for i in range(RING)]
        pxT = ps("b_pxT")
        paT = ps("b_paT")

        @block.sync
        def _(sp):
            for s in range(SLOTS):
                sp.wait_ge(scattered[s], 32 * (B // SLOTS))
            sp.wait_ge(padded, 16 * E0)
            sp.wait_ge(tabled, 2)

            def load(s, r, i):
                if i is not None:
                    sp.wait_ge(xgt_full, s - RING + 1)
                first = sp.value_load(tab[0:1, bass.ds(s + TILES0, 1)], min_val=0, max_val=E0 * XROWS - 128)
                sp.dma_start(xg[:, r, :], xs[bass.ds(first, 128), :]).then_inc(x_in[r], 16)

            def store(s, r):
                sp.wait_ge(y_set, s + 1)
                sp.dma_start(ys[bass.ds(s * 128, 128), :], yo[:, r, :]).then_inc(y_out[r], 16)

            for s in range(RING):
                load(s, s, None)
            with sp.Fori(0, TILES0 // RING - 1) as i:
                for r in range(RING):
                    load(RING * i + RING + r, r, i)
                    store(RING * i + r, r)
            for r in range(RING):
                store(TILES0 - RING + r, r)
            for r in range(RING):
                sp.wait_ge(y_out[r], 16 * (TILES0 // RING))

        @block.tensor
        def _(pe):
            pe.wait_ge(tabled, 2)
            pe.wait_ge(counted, B)
            pe.wait_ge(w_in, W_IN)

            def turn_x(s, r, i):
                pe.wait_ge(x_in[r], 16 * i + 16)
                if not (isinstance(s, int) and s == 0):
                    pe.wait_ge(xgt_out, s)
                for c in range(DC):
                    mm = pe.transpose(pxT[:, 128 * c:128 * c + 128], xg[:, r, 128 * c:128 * c + 128], ident)
                mm.then_inc(xgt_full, 1)

            def up(s, r):
                e = pe.value_load(tab[0:1, bass.ds(s, 1)], min_val=0, max_val=E0 - 1)
                pe.wait_ge(xgt_out, s + 1)
                pe.wait_ge(a_pre, s)
                for c in range(DC):
                    mm = pe.matmul(pA[:, 0:D], xgT[:, r, 128 * c:128 * c + 128],
                                   w1[:, bass.ds(e * (DC * D) + D * c, D)], start=(c == 0), stop=(c == DC - 1))
                mm.then_inc(a_full, 1)

            def turn_a(s, r):
                pe.wait_ge(a_act, s + 1)
                pe.wait_ge(at_out, s)
                for c in range(DC):
                    mm = pe.transpose(paT[:, 128 * c:128 * c + 128], act1[:, r, 128 * c:128 * c + 128], ident)
                mm.then_inc(at_full, 1)

            def down(s, r):
                e = pe.value_load(tab[0:1, bass.ds(s, 1)], min_val=0, max_val=E0 - 1)
                pe.wait_ge(at_out, s + 1)
                pe.wait_ge(y_set, s)
                for c in range(DC):
                    mm = pe.matmul(pB[:, 0:D], aT[:, r, 128 * c:128 * c + 128],
                                   w2[:, bass.ds(e * (DC * D) + D * c, D)], start=(c == 0), stop=(c == DC - 1))
                mm.then_inc(y_full, 1)

            turn_x(0, 0, 0)
            turn_x(1, 1, 0)
            up(0, 0)

            def steps(i):
                for r in range(RING):
                    s = RING * i + r
                    turn_a(s, r)
                    up(s + 1, (r + 1) % RING)
                    turn_x(s + 2, (r + 2) % RING, i + (r + 2) // RING)
                    down(s, r)

            steps(0)
            with pe.Fori(1, TILES0 // RING - 1) as i:
                steps(i)
            for r in range(RING):
                s = TILES0 - RING + r
                turn_a(s, r)
                if r < RING - 1:
                    up(s + 1, r + 1)
                if r == 0:
                    turn_x(s + 2, 2, TILES0 // RING - 1)
                down(s, r)

        @block.scalar
        def _(act):
            def xT_out(s, r):
                act.wait_ge(xgt_full, s + 1)
                act.copy(xgT[:, r, :], pxT[:, 0:D]).then_inc(xgt_out, 1)

            def gelu(s, r):
                act.wait_ge(a_pre, s + 1)
                act.activation(act1[:, r, :], pre[:, r, :], ACT.Gelu).then_inc(a_act, 1)

            def aT_out(s, r):
                act.wait_ge(at_full, s + 1)
                act.copy(aT[:, r, :], paT[:, 0:D]).then_inc(at_out, 1)

            xT_out(0, 0)
            xT_out(1, 1)
            gelu(0, 0)
            with act.Fori(0, TILES0 // RING - 1) as i:
                for r in range(RING):
                    s = RING * i + r
                    aT_out(s, r)
                    gelu(s + 1, (r + 1) % RING)
                    xT_out(s + 2, (r + 2) % RING)
            for r in range(RING):
                s = TILES0 - RING + r
                aT_out(s, r)
                if r < RING - 1:
                    gelu(s + 1, r + 1)
                if r == 0:
                    xT_out(s + 2, 2)

        @block.vector
        def _(dve):
            dve.wait_ge(tabled, 2)
            dve.wait_ge(w_in, W_IN)

            def bias1(s, r):
                e = dve.value_load(tab[0:1, bass.ds(s, 1)], min_val=0, max_val=E0 - 1)
                dve.wait_ge(a_full, s + 1)
                dve.tensor_tensor(pre[:, r, :], pA[:, 0:D], b1[:, bass.ds(e * D, D)], ALU.add).then_inc(a_pre, 1)

            def bias2(s, r, i):
                e = dve.value_load(tab[0:1, bass.ds(s, 1)], min_val=0, max_val=E0 - 1)
                dve.wait_ge(y_out[r], 16 * i)
                dve.wait_ge(y_full, s + 1)
                dve.tensor_tensor(yo[:, r, :], pB[:, 0:D], b2[:, bass.ds(e * D, D)], ALU.add).then_inc(y_set, 1)

            bias1(0, 0)

            def steps(i):
                for r in range(RING):
                    s = RING * i + r
                    bias1(s + 1, (r + 1) % RING)
                    bias2(s, r, i)

            steps(0)
            with dve.Fori(1, TILES0 // RING - 1) as i:
                steps(i)
            for r in range(RING):
                s = TILES0 - RING + r
                if r < RING - 1:
                    bias1(s + 1, r + 1)
                bias2(s, r, TILES0 // RING - 1)
def stage_attention1(nc, g, w, ys, xe):
    ctx = ExitStack()
    with ctx:
        def sb(name, shape, dt=F32):
            return ctx.enter_context(nc.sbuf_tensor("c_" + name, shape, dt))

        def ps(name):
            return ctx.enter_context(nc.psum_tensor("c_" + name, [128, 512], F32))

        taken = []

        def sem(name):
            taken.append(ctx.enter_context(nc.semaphore(name)))
            return taken[-1]

        def sems(names):
            return [sem("c_" + n) for n in names.split()]

        h, cst = g.h, g.cst
        ident = cst[:, C_ID:C_ID + 128]
        E, K, CAP = E1, TOPK, CAP1

        wraw = sb("wraw", [128, 4, DC, D])
        wT = sb("wT", [128, 4, DC, D])
        graw = sb("graw", [E, D])
        gT = sb("gT", [128, DC, E])
        wd = sb("wd", [128, DC])
        nbd = sb("nbd", [HT, 1])
        oscale = sb("oscale", [HT, 1])

        idx = sb("idx", [HT, 2, 2], U32)
        yg = sb("yg", [HT, 2, 2, D])
        stats = sb("stats", [HT, 2, 2, 6])
        mv = sb("mv", [HT, 2, 2, 2])
        rstd = sb("rstd", [HT, 2, 2])
        xn = sb("xn", [HT, 2, D])
        xT = sb("xT", [128, DC, N])
        qT = sb("qT", [128, DC, N])
        kT = sb("kT", [128, DC, N])
        v = sb("v", [HT, 2, D])
        dec = sb("dec", [HT, 4, 2])
        wgt = sb("wgt", [HT, 3 * HT])
        wgm = sb("wgm", [HT, 3 * HT])
        sc = sb("sc", [HT, 3 * HT])
        rT = sb("rT", [128, DC, N])
        xr = sb("xr", [HT, 2, 2, D])
        xTr = sb("xTr", [128, DC, N])
        lg = sb("lg", [HT, 2, E])
        top = sb("top", [HT, 2, 8])
        topi = sb("topi", [HT, 2, 8], U32)
        nmax = sb("nmax", [HT, 2])
        e4 = sb("e4", [HT, 2, K])
        esum = sb("esum", [HT, 2])
        einv = sb("einv", [HT, 2])
        pick = sb("pick", [HT, 2, K])
        hot = sb("hot", [HT, 2 * K, E], BF16)
        hots = sb("hots", [HT, 2, E], BF16)
        rank = sb("rank", [HT, 2, E])
        run = sb("run", [HT, E])
        spread = sb("spread", [HT, 2, K, E])
        slot = sb("slot", [HT, 2, K])
        keep = sb("keep", [HT, 2, K])
        lost = sb("lost", [HT, 2, K])
        row = sb("row", [HT, 2, K])
        gate = sb("gate", [HT, 2, K])
        rowi = sb("rowi", [HT, 2, 2, K], U32)
        scrap = sb("scrap", [1, 16])

        pT, pq, pk, pv, psc, pr, po, psm = (ps(n) for n in ("pT", "pq", "pk", "pv", "psc", "pr", "po", "psm"))

        loaded, turned, turned_out, zeroed = sems("loaded turned turned_out zeroed")
        fetched = sems("fetched0 fetched1")
        idx_set, y_added, stat3, mv3, eps3, pow3, norm3 = sems("idx_set y_added stat3 mv3 eps3 pow3 norm3")
        t3_full, t3_out, q_full, q_out, k_full, k_out, v_full, v_out = sems(
            "t3_full t3_out q_full q_out k_full k_out v_full v_out")
        dec_exp, dec1, dec_set, ln_set, wgt_set, wgm_set = sems("dec_exp dec1 dec_set ln_set wgt_set wgm_set")
        dec2 = sem("c_dec2")
        s_full, s_out, r_full, r_out, o_full, o_added = sems("s_full s_out r_full r_out o_full o_added")
        stat4, mv4, eps4, pow4, norm4, t4_full, t4_out, t4_kept = sems("stat4 mv4 eps4 pow4 norm4 t4_full t4_out t4_kept")
        l_full, choosing, nmax_set, e4_set, hots_set = sems(
            "l_full choosing nmax_set e4_set hots_set")
        rank_full, placing, run_set = sems(
            "rank_full placing run_set")
        rowi_set = sem("c_rowi_set")
        scattered = sems("scattered0 scattered1")

        
        assert not used_before(nc, taken)
        g.ffn1_sems = {name: g.sem("d_" + name) for name in FFN1_SEMS.split()}
        loads = [(wraw[:, n, :, :], w[name].rearrange("(c p) d -> p c d", p=128))
                 for n, name in enumerate(("L1_attn_Wq", "L1_attn_Wk", "L1_attn_Wv", "L1_attn_Wo"))]
        loads += [(graw[:, :], w["L1_ffn_gate_w"]),
                  (nbd[:, :], w["L1_attn_bd"].rearrange("(a d) -> a d", a=1).broadcast_to([HT, 1])),
                  (oscale[:, :], w["L1_attn_out_scale"].rearrange("(a d) -> a d", a=1).broadcast_to([HT, 1]))]
        LOADED = 16 * (len(loads) + 1)
        block = ctx.enter_context(nc.Block())

        class At:

            def __init__(self, k, par, half=None):
                self.k, self.par = k, par
                self.half = k // 2 if half is None else half
                known = isinstance(k, int)
                self.now = not known or 0 <= k < B
                self.next = not known or 0 <= k + 1 < B
                self.soon = not known or 0 <= k + 2 < B
                self.past = not known or 0 <= k - 1 < B

        def run_steps(eng, body):
            for k in range(-2, 4):
                body(At(k, k % 2))
            with eng.Fori(2, B // 2 - 2) as i:
                for par in range(2):
                    body(At(2 * i + par, par, i))
            for k in range(B - 4, B + 1):
                body(At(k, k % 2))

        @block.sync
        def _(sp):
            for dst, src in loads:
                sp.dma_start(dst, src).then_inc(loaded, 16)
            for s in g.ffn1_sems.values():
                sp.sem_clear(s)
            with nc.allow_non_contiguous_dma(reason="256 numbers, once"):
                sp.dma_start(wd[:, :], w["L1_attn_Wd"].rearrange("a (c p) -> p (a c)", p=128)).then_inc(loaded, 16)


        @block.tensor
        def _(pe):
            pe.wait_ge(loaded, LOADED)
            for n, bank in enumerate((pq, pk, pv, po)):
                for c in range(DC):
                    for r in range(DC):
                        mm = pe.transpose(bank[:, D * c + 128 * r:D * c + 128 * r + 128],
                                          wraw[:, n, r, 128 * c:128 * c + 128], ident)
                mm.then_inc(turned, 1)
            for c in range(DC):
                mm = pe.transpose(psm[:, E * c:E * c + E], graw[:, 128 * c:128 * c + 128], ident[0:E, 0:E])
            mm.then_inc(turned, 1)
            pe.wait_ge(turned_out, 5)

            def turn(dst_full, src):
                for c in range(DC):
                    for it in range(2):
                        mm = pe.transpose(pT[:, N * c + HT * it:N * c + HT * it + HT],
                                          src[:, it, 128 * c:128 * c + 128], ident[0:HT, 0:HT])
                mm.then_inc(dst_full, 1)

            def step(s):
                k = s.k
                if s.now:
                    pe.wait_ge(q_out, k + 1)
                    pe.wait_ge(k_out, k + 1)
                    pe.wait_ge(s_out, k)
                    for st in range(2):
                        for c in range(DC):
                            mm = pe.matmul(psc[0:HT, HT * st:HT * st + HT * (st + 1)], kT[:, c, HT * st:HT * st + HT],
                                           qT[:, c, 0:HT * (st + 1)], start=(c == 0), stop=(c == DC - 1))
                    mm.then_inc(s_full, 1)
                if s.past:
                    pe.wait_ge(norm4, k)
                    if s.next:
                        pe.wait_ge(t3_out, k + 2)
                    else:
                        pe.wait_ge(t4_kept, k - 1)
                    turn(t4_full, xr[:, 1 - s.par, :, :])
                if s.next:
                    pe.wait_ge(t3_out, k + 2)
                    for n, (bank, full, out) in enumerate(((pq, q_full, q_out), (pk, k_full, k_out))):
                        if not (isinstance(k, int) and k < 0):
                            pe.wait_ge(out, k + 1)
                            if n:
                                pe.wait_ge(dec_exp, k + 1)
                        for a in range(DC):
                            for c in range(DC):
                                mm = pe.matmul(bank[:, N * a:N * a + N], wT[:, n, c, 128 * a:128 * a + 128], xT[:, c, :],
                                               start=(c == 0), stop=(c == DC - 1))
                        if n:
                            for it in range(2):
                                for c in range(DC):
                                    mm = pe.matmul(bank[0:HT, 2 * N + it:2 * N + it + 1], xT[:, c, HT * it:HT * it + HT],
                                                   wd[:, c:c + 1], start=(c == 0), stop=(c == DC - 1))
                        mm.then_inc(full, 1)
                if s.now:
                    pe.wait_ge(s_out, k + 1)
                    pe.wait_ge(v_out, k + 1)
                    pe.wait_ge(r_out, k)
                    for a in range(DC):
                        pe.matmul(pr[:, N * a:N * a + N], v[:, 1, 128 * a:128 * a + 128], sc[:, HT:3 * HT],
                                  start=True, stop=False)
                        mm = pe.matmul(pr[:, N * a:N * a + HT], v[:, 0, 128 * a:128 * a + 128], sc[:, 0:HT],
                                       start=False, stop=True)
                    mm.then_inc(r_full, 1)
                if s.next:
                    if not (isinstance(k, int) and k < 0):
                        pe.wait_ge(v_out, k + 1)
                    for it in range(2):
                        for c in range(DC):
                            mm = pe.matmul(pv[0:HT, D * it:D * it + D], xT[:, c, HT * it:HT * it + HT], wT[:, 2, c, :],
                                           start=(c == 0), stop=(c == DC - 1))
                    mm.then_inc(v_full, 1)
                if s.past:
                    pe.wait_ge(t4_out, k)
                    pe.wait_ge(run_set, k)
                    for it in range(2):
                        for c in range(DC):
                            mm = pe.matmul(psm[0:HT, E * it:E * it + E], xTr[:, c, HT * it:HT * it + HT], gT[:, c, :],
                                           start=(c == 0), stop=(c == DC - 1))
                    mm.then_inc(l_full, 1)
                if s.now:
                    pe.wait_ge(r_out, k + 1)
                    pe.wait_ge(o_added, k)
                    for it in range(2):
                        for c in range(DC):
                            mm = pe.matmul(po[0:HT, D * it:D * it + D], rT[:, c, HT * it:HT * it + HT], wT[:, 3, c, :],
                                           start=(c == 0), stop=(c == DC - 1))
                    mm.then_inc(o_full, 1)
                if s.soon:
                    pe.wait_ge(norm3, k + 3)
                    if s.past:
                        pe.wait_ge(t4_kept, k)
                    elif k > -2:
                        pe.wait_ge(t3_out, k + 2)
                    turn(t3_full, xn)
                if s.past:
                    pe.wait_ge(hots_set, k)
                    pe.matmul(psm[0:HT, 0:E], g.upb[:, :], hots[:, 0, :], start=True, stop=True)
                    pe.matmul(psm[0:HT, E:2 * E], g.upb[:, :], hots[:, 1, :], start=True, stop=False)
                    pe.matmul(psm[0:HT, E:2 * E], g.onesb[:, 0:HT], hots[:, 0, :], start=False, stop=True)
                    pe.matmul(psm[0:HT, 2 * E:3 * E], g.onesb[:, 0:HT], hots[:, 0, :], start=True, stop=False)
                    pe.matmul(psm[0:HT, 2 * E:3 * E], g.onesb[:, 0:HT], hots[:, 1, :], start=False, stop=True).then_inc(rank_full, 1)

            run_steps(pe, step)

        @block.scalar
        def _(act):
            for n, bank in enumerate((pq, pk, pv, po)):
                act.wait_ge(turned, n + 1)
                act.copy(wT[:, n, :, :], bank[:, :].rearrange("p (c e) -> p c e", c=DC)).then_inc(turned_out, 1)
            act.wait_ge(turned, 5)
            act.copy(gT[:, :, :], psm[:, 0:DC * E].rearrange("p (c e) -> p c e", c=DC)).then_inc(turned_out, 1)
            act.mul(nbd[:, :], nbd[:, :], -1.0).then_inc(zeroed, 1)

            def halves(bank):
                return bank[:, 0:2 * N].rearrange("p (c n) -> p c n", c=DC)

            def step(s):
                k = s.k
                if s.past:
                    act.wait_ge(t4_full, k)
                    act.copy(xTr[:, :, :], halves(pT)).then_inc(t4_out, 1)
                    act.copy(g.xTs[:, :, bass.ds(N * k - N, N)], halves(pT)).then_inc(t4_kept, 1)
                if s.next:
                    act.wait_ge(q_full, k + 2)
                    act.copy(qT[:, :, :], halves(pq)).then_inc(q_out, 1)
                    act.wait_ge(k_full, k + 2)
                    act.copy(kT[:, :, :], halves(pk)).then_inc(k_out, 1)
                    act.activation(dec[:, 0, :], pk[0:HT, 2 * N:2 * N + 2], ACT.Exp, bias=nbd[:, 0:1], scale=-1.0).then_inc(dec_exp, 1)
                if s.now:
                    act.wait_ge(r_full, k + 1)
                    act.copy(rT[:, :, :], halves(pr)).then_inc(r_out, 1)
                if s.next:
                    act.wait_ge(v_full, k + 2)
                    act.copy(v[:, :, :], pv[0:HT, :].rearrange("p (t d) -> p t d", t=2)).then_inc(v_out, 1)
                    act.wait_ge(dec_set, k + 2)
                    act.activation(dec[:, 3, :], dec[:, 2, :], ACT.Ln).then_inc(ln_set, 1)
                    act.wait_ge(ln_set, k + 2)
                    if s.now:
                        act.wait_ge(wgm_set, k + 1)
                    for st in range(2):
                        e = act.activation(wgt[:, HT * st:HT * st + HT * (st + 1)],
                                           cst[0:HT, C_DIST + HT * st:C_DIST + HT * st + HT * (st + 1)], ACT.Exp,
                                           scale=dec[:, 3, st:st + 1])
                    e.then_inc(wgt_set, 1)
                if s.past:
                    act.wait_ge(nmax_set, k)
                    for it in range(2):
                        e = act.activation(e4[:, it, :], top[:, it, 0:K], ACT.Exp, bias=nmax[:, it:it + 1],
                                           accum_out=esum[:, it:it + 1])
                    e.then_inc(e4_set, 1)
                if s.soon:
                    act.wait_ge(t3_full, k + 3)
                    act.copy(xT[:, :, :], halves(pT)).then_inc(t3_out, 1)

            run_steps(act, step)

        @block.vector
        def _(dve):
            def settle(s, n):
                dve.wait_ge(s, n)
                dve.memset(scrap[0:1, 0:1], 0.0)

            def h_tile(b, it=None):
                if it is None:
                    return h[:, bass.ds(b * (2 * D), 2 * D)]
                return h[:, bass.ds(b * (2 * D) + D * it, D)]

            def statistics(b, n, added, stat, aggregated, eps):
                settle(added, b + 1)
                for it in range(2):
                    dve.bn_stats(stats[:, n, it, :], h_tile(b, it)).then_inc(stat, 1)
                settle(stat, 2 * b + 2)
                for it in range(2):
                    dve.bn_aggr(mv[:, n, it, :], stats[:, n, it, :]).then_inc(aggregated, 1)
                dve.wait_ge(aggregated, 2 * b + 2)
                dve.tensor_scalar(rstd[:, n, :], mv[:, n, :, 1], EPS, None, ALU.add).then_inc(eps, 1)

            def scale(b, n, power, dst, done):
                dve.wait_ge(power, b + 1)
                for it in range(2):
                    e = dve.tensor_scalar(dst[:, it, :], h_tile(b, it), mv[:, n, it, 0:1], rstd[:, n, it:it + 1],
                                          ALU.subtract, ALU.mult)
                e.then_inc(done, 1)

            def wide(ap, n):
                return ap.unsqueeze(2).broadcast_to([HT, ap.shape[1], n])

            dve.memset(run[:, :], 0.0).then_inc(run_set, 1)
            dve.wait_ge(loaded, LOADED)

            def step(s):
                k = s.k
                if s.now:
                    dve.wait_ge(wgm_set, k + 1)
                    dve.wait_ge(s_full, k + 1)
                    dve.tensor_tensor(sc[:, :], psc[0:HT, 0:3 * HT], wgm[:, :], ALU.mult).then_inc(s_out, 1)
                if s.past:
                    if not isinstance(k, int) or k >= 3:
                        dve.wait_ge(scattered[1 - s.par], 16 * 2 * K * (s.half - (1 - s.par)))
                    scale(k - 1, 1, pow4, xr[:, 1 - s.par, :, :], norm4)
                if s.soon:
                    b = k + 2
                    dve.wait_ge(fetched[s.par], 32 * (s.half + 2))
                    dve.tensor_tensor(h_tile(b), h_tile(b), yg[:, s.par, :, :].rearrange("p t d -> p (t d)"), ALU.add).then_inc(y_added, 1)
                    statistics(b, 0, y_added, stat3, mv3, eps3)
                    if not (isinstance(k, int) and k == -2):
                        dve.wait_ge(t3_full, k + 2)
                    scale(b, 0, pow3, xn, norm3)
                if s.next:
                    dve.wait_ge(dec_exp, k + 2)
                    dve.tensor_scalar(dec[:, 1, :], dec[:, 0, :], 1.0, None, ALU.add).then_inc(dec1, 1)
                    dve.wait_ge(dec1, k + 2)
                    dve.reciprocal(dec[:, 1, :], dec[:, 1, :]).then_inc(dec2, 1)
                    dve.wait_ge(dec2, k + 2)
                    dve.tensor_scalar(dec[:, 2, :], dec[:, 1, :], 1e-8, None, ALU.add).then_inc(dec_set, 1)
                if s.past:
                    dve.wait_ge(l_full, k)
                    dve.tensor_copy(lg[:, :, :], psm[0:HT, 0:2 * E].rearrange("p (t e) -> p t e", t=2)).then_inc(choosing, 1)
                    settle(choosing, 7 * k - 6)
                    for it in range(2):
                        dve.max(top[:, it, :], lg[:, it, :]).then_inc(choosing, 1)
                    dve.wait_ge(choosing, 7 * k - 4)
                    dve.tensor_scalar(nmax[:, :], top[:, :, 0], -1.0, None, ALU.mult).then_inc(nmax_set, 1)
                    for it in range(2):
                        dve.max_index(topi[:, it, :], top[:, it, :], lg[:, it, :]).then_inc(choosing, 1)
                    dve.wait_ge(choosing, 7 * k - 2)
                    dve.tensor_copy(pick[:, :, :], topi[:, :, 0:K]).then_inc(choosing, 1)
                    dve.wait_ge(choosing, 7 * k - 1)
                    dve.tensor_tensor(hot[:, :, :], wide(pick[:, :, :].rearrange("p t k -> p (t k)"), E),
                                      cst[0:HT, C_IOTA:C_IOTA + E].unsqueeze(1).broadcast_to([HT, 2 * K, E]),
                                      ALU.is_equal).then_inc(choosing, 1)
                    dve.wait_ge(choosing, 7 * k)
                    with nc.allow_low_precision(reason="a sum of 0 and 1 that is at most 1"):
                        dve.tensor_reduce(hots[:, :, :], hot[:, :, :].rearrange("p (t k) e -> p t e k", k=K), AX.X,
                                          ALU.add).then_inc(hots_set, 1)
                if s.now:
                    dve.wait_ge(o_full, k + 1)
                    dve.scalar_tensor_tensor(out=h_tile(k), in0=po[0:HT, :], scalar=oscale[:, 0:1], in1=h_tile(k),
                                             op0=ALU.mult, op1=ALU.add).then_inc(o_added, 1)
                    statistics(k, 1, o_added, stat4, mv4, eps4)
                if s.past:
                    dve.wait_ge(rank_full, k)
                    dve.wait_ge(run_set, k)
                    dve.tensor_tensor(rank[:, :, :], psm[0:HT, 0:2 * E].rearrange("p (t e) -> p t e", t=2),
                                      run[:, :].unsqueeze(1).broadcast_to([HT, 2, E]), ALU.add).then_inc(placing, 1)
                    dve.wait_ge(placing, 9 * k - 8)
                    dve.tensor_tensor(spread[:, :, :, :], hot[:, :, :].rearrange("p (t k) e -> p t k e", k=K),
                                      rank[:, :, :].unsqueeze(2).broadcast_to([HT, 2, K, E]), ALU.mult).then_inc(placing, 1)
                    dve.tensor_tensor(run[:, :], psm[0:HT, 2 * E:3 * E], run[:, :], ALU.add).then_inc(run_set, 1)
                    dve.wait_ge(placing, 9 * k - 7)
                    dve.tensor_reduce(slot[:, :, :], spread[:, :, :, :], AX.X, ALU.add).then_inc(placing, 1)
                    dve.wait_ge(placing, 9 * k - 6)
                    dve.tensor_scalar(lost[:, :, :], slot[:, :, :], float(CAP), float(2 * E * CAP), ALU.is_ge, ALU.mult).then_inc(placing, 1)
                    dve.tensor_scalar(keep[:, :, :], slot[:, :, :], float(CAP), None, ALU.is_lt).then_inc(placing, 1)
                    dve.scalar_tensor_tensor(out=row[:, :, :], in0=pick[:, :, :], scalar=float(CAP), in1=slot[:, :, :],
                                             op0=ALU.mult, op1=ALU.add).then_inc(placing, 1)
                    dve.wait_ge(placing, 9 * k - 3)
                    dve.tensor_tensor(row[:, :, :], row[:, :, :], lost[:, :, :], ALU.add).then_inc(placing, 1)
                    dve.wait_ge(placing, 9 * k - 2)
                    dve.tensor_copy(g.rows[:, bass.ds(2 * K * k - 2 * K, 2 * K)], row[:, :, :].rearrange("p t k -> p (t k)"))
                    dve.tensor_copy(rowi[:, 1 - s.par, :, :], row[:, :, :]).then_inc(rowi_set, 1)
                    dve.wait_ge(e4_set, k)
                    dve.reciprocal(einv[:, :], esum[:, :]).then_inc(placing, 1)
                    dve.wait_ge(placing, 9 * k - 1)
                    dve.tensor_tensor(gate[:, :, :], e4[:, :, :], wide(einv[:, :], K), ALU.mult).then_inc(placing, 1)
                    dve.wait_ge(placing, 9 * k)
                    dve.tensor_tensor(g.gates[:, bass.ds(2 * K * k - 2 * K, 2 * K)], gate[:, :, :].rearrange("p t k -> p (t k)"),
                                      keep[:, :, :].rearrange("p t k -> p (t k)"), ALU.mult)
                if s.next:
                    dve.wait_ge(wgt_set, k + 2)
                    dve.tensor_tensor(wgm[:, :], wgt[:, :], cst[0:HT, C_LATER:C_LATER + 3 * HT], ALU.mult).then_inc(wgm_set, 1)

            run_steps(dve, step)

        @block.gpsimd
        def _(pool):
            def fetch(b, par):
                if isinstance(b, int):
                    if b >= 2:
                        pool.wait_ge(y_added, b - 1)
                else:
                    pool.wait_ge(y_added, b - 1)
                pool.tensor_copy(idx[:, par, :], g.back[:, bass.ds(2 * b, 2)]).then_inc(idx_set, 1)
                pool.wait_ge(idx_set, b + 1)
                pool.tensor_tensor(scrap[0:1, 4 + par:5 + par], scrap[0:1, 2:3], scrap[0:1, 3:4], ALU.add)
                for it in range(2):
                    pool.indirect_dma_start(yg[:, par, it, :], None, ys[:, :],
                                            bass.IndirectOffsetOnAxis(ap=idx[:, par, it:it + 1], axis=0),
                                            bounds_check=128 * TILES0 - 1, oob_is_err=True).then_inc(fetched[par], 16)

            def power(n, eps, done, b):
                pool.wait_ge(eps, b + 1)
                pool.tensor_tensor(rstd[:, n, :], rstd[:, n, :], g.mhalf[:, :], ALU.pow).then_inc(done, 1)

            def scatter(par, it):
                for c in range(K):
                    pool.indirect_dma_start(xe[:, :], bass.IndirectOffsetOnAxis(ap=rowi[:, par, it, c:c + 1], axis=0),
                                            xr[:, par, it, :], None, bounds_check=E * CAP - 1,
                                            oob_is_err=False).then_inc(scattered[par], 16)

            pool.memset(scrap[0:1, 2:4], 0.0).then_inc(zeroed, 1)
            pool.wait_ge(zeroed, 2)
            fetch(0, 0)

            def step(s):
                k = s.k
                if s.soon:
                    power(0, eps3, pow3, k + 2)
                    if not isinstance(k, int) or k + 3 < B:
                        fetch(k + 3, 1 - s.par)
                if s.now:
                    power(1, eps4, pow4, k)
                if s.past:
                    pool.wait_ge(rowi_set, k)
                    pool.tensor_tensor(scrap[0:1, 6 + s.par:7 + s.par], scrap[0:1, 2:3], scrap[0:1, 3:4], ALU.add)
                    scatter(1 - s.par, 0)
                    scatter(1 - s.par, 1)

            run_steps(pool, step)
            for par in range(2):
                pool.wait_ge(scattered[par], 16 * 2 * K * (B // 2))
FFN1_SEMS = """sw_in sgu_full sgs_set sa_set sdn_full sh_added x_in0 x_in1
x_in2 x_in3 w_in0 w_in1 w_in2 w_in3 y_out0 y_out1
t_full t_out gu_full gs_set a_set dn_full y_set cleared
idx_set summed h_set fetched0 fetched1 stored zeroed gate_set"""


def stage_ffn1(nc, g, w, xe, ye, out):
    ctx = ExitStack()
    with ctx:
        def sb(name, shape, dt=F32):
            return ctx.enter_context(nc.sbuf_tensor("d_" + name, shape, dt))

        def ps(name):
            return ctx.enter_context(nc.psum_tensor("d_" + name, [128, 512], F32))

        def sems(names):
            return [g.ffn1_sems[n] for n in names.split()]

        h, cst = g.h, g.cst
        ident = cst[:, C_ID:C_ID + 128]
        E, K, CAP = E1, TOPK, CAP1
        RING = 4
        AHEAD = RING - 1
        CT = CAP // 128

        swg = sb("swg", [128, DC, 2 * I1])
        swd = sb("swd", [I1, D])
        gs = sb("gs", [128, 2, CAP])
        a = sb("a", [128, 2, CAP])
        x = sb("x", [128, RING, CT, D])
        wgu = sb("wgu", [128, RING, DC, 2 * I1])
        wdn = sb("wdn", [I1, RING, D])
        xT = sb("xT", [128, 2, DC, CAP])
        yo = sb("yo", [128, 2, CT, D])
        idx = sb("idx", [HT, 2, 2 * K], U32)
        gate = sb("gate", [HT, 2, 2 * K])
        yg = sb("yg", [HT, 2, 2 * K, D])
        scrap = sb("scrap", [1, 8])
        pT, pgu, pdn = [ps("pT0"), ps("pT1")], [ps("pgu0"), ps("pgu1")], [ps("pdn0"), ps("pdn1")]

        sw_in, = sems("sw_in")
        sgu_full, sgs_set, sa_set, sdn_full, sh_added = sems("sgu_full sgs_set sa_set sdn_full sh_added")
        x_in = sems("x_in0 x_in1 x_in2 x_in3")
        w_in = sems("w_in0 w_in1 w_in2 w_in3")
        y_out = sems("y_out0 y_out1")
        t_full, t_out, gu_full, gs_set, a_set, dn_full, y_set = sems("t_full t_out gu_full gs_set a_set dn_full y_set")
        cleared, idx_set, summed, h_set = sems("cleared idx_set summed h_set")
        fetched = sems("fetched0 fetched1")
        stored, zeroed = sems("stored zeroed")
        gate_set, = sems("gate_set")
        block = ctx.enter_context(nc.Block())

        @block.sync
        def _(sp):
            sp.dma_start(swg[:, :, :], w["L1_ffn_shared_w_gate_up"].rearrange("(c p) i -> p c i", p=128)).then_inc(sw_in, 16)
            sp.dma_start(swd[:, :], w["L1_ffn_shared_w_down"]).then_inc(sw_in, 16)

            def load(e, r, first=False):
                if not first:
                    sp.wait_ge(t_full, e - RING + 1)
                    sp.wait_ge(dn_full, e - RING + 1)
                sp.dma_start(x[:, r, :, :], xe[bass.ds(e * CAP, CAP), :].rearrange("(a p) d -> p a d", p=128)).then_inc(x_in[r], 16)
                sp.dma_start(wgu[:, r, :, :], w["L1_ffn_w_gate_up"][bass.ds(e, 1), :, :].rearrange(
                    "e (c p) i -> p (e c) i", p=128)).then_inc(w_in[r], 16)
                sp.dma_start(wdn[:, r, :], w["L1_ffn_w_down"][bass.ds(e, 1), :, :].rearrange("e i d -> (e i) d")).then_inc(w_in[r], 16)

            def store(e, r):
                sp.wait_ge(y_set, e + 1)
                sp.dma_start(ye[bass.ds(e * CAP, CAP), :].rearrange("(a p) d -> p a d", p=128), yo[:, r % 2, :, :]).then_inc(y_out[r % 2], 16)

            for e in range(AHEAD):
                load(e, e, True)
            load(AHEAD, AHEAD, True)
            store(0, 0)
            with sp.Fori(0, E // RING - 1) as i:
                for r in range(RING):
                    load(RING * i + RING + r, r)
                    store(RING * i + r + 1, (r + 1) % RING)
            for r in range(1, RING):
                store(E - RING + r, r)
            for r in range(2):
                sp.wait_ge(y_out[r], 16 * E // 2)

            def put(b, par):
                sp.wait_ge(h_set, b + 1)
                sp.dma_start(out[bass.ds(b, 1), :, :].rearrange("b (t p) d -> p (b t) d", t=2),
                             h[:, bass.ds(b * (2 * D), 2 * D)].rearrange("p (t d) -> p t d", t=2)).then_inc(stored, 16)

            with sp.Fori(0, B) as b:
                put(b, 0)
            sp.wait_ge(stored, 16 * B)

        @block.tensor
        def _(pe):
            pe.wait_ge(sw_in, 32)

            def shared_up(b, par):
                pe.wait_ge(sa_set, b - 1)
                for n in range(2):
                    for c in range(DC):
                        mm = pe.matmul(pgu[par][:, N * n:N * n + N], swg[:, c, I1 * n:I1 * n + I1],
                                       g.xTs[:, c, bass.ds(b * N, N)], start=(c == 0), stop=(c == DC - 1))
                mm.then_inc(sgu_full, 1)

            def shared_down(b, par):
                pe.wait_ge(sa_set, b + 1)
                pe.wait_ge(sh_added, b - 1)
                for it in range(2):
                    mm = pe.matmul(pdn[par][0:HT, D * it:D * it + D], a[:, par, HT * it:HT * it + HT], swd[:, :],
                                   start=True, stop=True)
                mm.then_inc(sdn_full, 1)

            def first_up(b):
                for n in range(2):
                    for c in range(DC):
                        mm = pe.matmul(pgu[b][:, N * n:N * n + N], swg[:, c, I1 * n:I1 * n + I1],
                                       g.xTs[:, c, N * b:N * b + N], start=(c == 0), stop=(c == DC - 1))
                mm.then_inc(sgu_full, 1)

            def first_down(b):
                pe.wait_ge(sa_set, b + 1)
                for it in range(2):
                    mm = pe.matmul(pdn[b][0:HT, D * it:D * it + D], a[:, b, HT * it:HT * it + HT], swd[:, :],
                                   start=True, stop=True)
                mm.then_inc(sdn_full, 1)

            first_up(0)
            first_up(1)
            first_down(0)
            shared_up(2, 0)
            first_down(1)
            with pe.Fori(1, B // 2 - 1) as i:
                for par in range(2):
                    shared_up(2 * i + par + 1, 1 - par)
                    shared_down(2 * i + par, par)
            shared_up(B - 1, 1)
            shared_down(B - 2, 0)
            shared_down(B - 1, 1)
            pe.wait_ge(sa_set, B)
            pe.wait_ge(sh_added, B)

            def turn(e, r, i):
                pe.wait_ge(x_in[r], 16 * i + 16)
                pe.wait_ge(t_out, e - 1) if not isinstance(e, int) or e > 1 else None
                for c in range(DC):
                    for t in range(CT):
                        mm = pe.transpose(pT[r % 2][:, CAP * c + 128 * t:CAP * c + 128 * t + 128],
                                          x[:, r, t, 128 * c:128 * c + 128], ident)
                mm.then_inc(t_full, 1)

            def up(e, r, i):
                pe.wait_ge(w_in[r], 32 * i + 32)
                pe.wait_ge(t_out, e + 1)
                pe.wait_ge(a_set, e - 1) if not isinstance(e, int) or e > 1 else None
                for n in range(2):
                    for c in range(DC):
                        mm = pe.matmul(pgu[r % 2][:, CAP * n:CAP * n + CAP], wgu[:, r, c, I1 * n:I1 * n + I1],
                                       xT[:, r % 2, c, :], start=(c == 0), stop=(c == DC - 1))
                mm.then_inc(gu_full, 1)

            def down(e, r):
                pe.wait_ge(a_set, e + 1)
                pe.wait_ge(y_set, e - 1) if not isinstance(e, int) or e > 1 else None
                for t in range(CT):
                    mm = pe.matmul(pdn[r % 2][:, D * t:D * t + D], a[:, r % 2, 128 * t:128 * t + 128], wdn[:, r, :],
                                   start=True, stop=True)
                mm.then_inc(dn_full, 1)

            turn(0, 0, 0)
            turn(1, 1, 0)
            up(0, 0, 0)
            turn(2, 2, 0)
            up(1, 1, 0)
            down(0, 0)
            turn(3, 3, 0)
            up(2, 2, 0)
            down(1, 1)
            with pe.Fori(0, E // RING - 1) as i:
                for r in range(RING):
                    e = RING * i + r
                    turn(e + RING, r, i + 1)
                    up(e + 3, (r + 3) % RING, i + (r + 3) // RING)
                    down(e + 2, (r + 2) % RING)
            up(E - 1, RING - 1, E // RING - 1)
            down(E - 2, RING - 2)
            down(E - 1, RING - 1)

        @block.scalar
        def _(act):
            def shared_silu(b, par):
                act.wait_ge(sgu_full, b + 1)
                if not (isinstance(b, int) and b < 2):
                    act.wait_ge(sa_set, b - 1)
                act.activation(gs[:, par, 0:N], pgu[par][:, 0:N], ACT.Silu).then_inc(sgs_set, 1)

            shared_silu(0, 0)
            shared_silu(1, 1)
            with act.Fori(1, B // 2) as i:
                for par in range(2):
                    shared_silu(2 * i + par, par)
            act.wait_ge(sa_set, B)

            def turn_out(e, r):
                act.wait_ge(t_full, e + 1)
                if not (isinstance(e, int) and e < 2):
                    act.wait_ge(gu_full, e - 1)
                act.copy(xT[:, r % 2, :, :], pT[r % 2][:, :].rearrange("p (c n) -> p c n", c=DC)).then_inc(t_out, 1)

            def silu(e, r):
                act.wait_ge(gu_full, e + 1)
                if not (isinstance(e, int) and e < 2):
                    act.wait_ge(a_set, e - 1)
                act.activation(gs[:, r % 2, :], pgu[r % 2][:, 0:CAP], ACT.Silu).then_inc(gs_set, 1)

            turn_out(0, 0)
            turn_out(1, 1)
            silu(0, 0)
            turn_out(2, 0)
            silu(1, 1)
            turn_out(3, 1)
            silu(2, 0)
            with act.Fori(0, E // 2 - 2) as i:
                for r in range(2):
                    turn_out(2 * i + r + 4, r)
                    silu(2 * i + r + 3, 1 - r)
            silu(E - 1, 1)

        @block.vector
        def _(dve):
            dve.memset(yg[:, :, :, :], 0.0).then_inc(cleared, 1)

            def shared_product(b, par):
                dve.wait_ge(sgs_set, b + 1)
                if not (isinstance(b, int) and b < 2):
                    dve.wait_ge(sdn_full, b - 1)
                dve.tensor_tensor(a[:, par, 0:N], pgu[par][:, N:2 * N], gs[:, par, 0:N], ALU.mult).then_inc(sa_set, 1)

            def shared_add(b, par):
                dve.wait_ge(sdn_full, b + 1)
                hb = h[:, bass.ds(b * (2 * D), 2 * D)]
                dve.tensor_tensor(hb, pdn[par][0:HT, :], hb, ALU.add).then_inc(sh_added, 1)

            shared_product(0, 0)
            shared_product(1, 1)
            shared_add(0, 0)
            with dve.Fori(1, B // 2) as i:
                for par in range(2):
                    shared_product(2 * i + par, par)
                    shared_add(2 * i + par - 1, 1 - par)
            shared_add(B - 1, 1)
            dve.wait_ge(sdn_full, B)

            def product(e, r):
                dve.wait_ge(gs_set, e + 1)
                if not (isinstance(e, int) and e < 2):
                    dve.wait_ge(dn_full, e - 1)
                dve.tensor_tensor(a[:, r, :], pgu[r][:, CAP:2 * CAP], gs[:, r, :], ALU.mult).then_inc(a_set, 1)

            def result(e, r, i):
                dve.wait_ge(dn_full, e + 1)
                dve.wait_ge(y_out[r], 16 * i)
                dve.tensor_copy(yo[:, r, :, :], pdn[r][:, :].rearrange("p (t d) -> p t d", t=CT)).then_inc(y_set, 1)

            product(0, 0)

            def steps(i):
                for r in range(2):
                    product(2 * i + r + 1, 1 - r)
                    result(2 * i + r, r, i)

            steps(0)
            with dve.Fori(1, E // 2 - 1) as i:
                steps(i)
            product(E - 1, 1)
            result(E - 2, 0, E // 2 - 1)
            result(E - 1, 1, E // 2 - 1)

            def combine(b, par, i):
                dve.wait_ge(fetched[par], 16 * 2 * K * (i + 1))
                dve.tensor_copy(gate[:, par, :], g.gates[:, bass.ds(b * (2 * K), 2 * K)]).then_inc(gate_set, 1)
                dve.wait_ge(gate_set, b + 1)
                for j in range(K):
                    for it in range(2):
                        ht = h[:, bass.ds(b * (2 * D) + D * it, D)]
                        ins = dve.scalar_tensor_tensor(out=ht, in0=yg[:, par, K * it + j, :],
                                                       scalar=gate[:, par, K * it + j:K * it + j + 1], in1=ht,
                                                       op0=ALU.mult, op1=ALU.add)
                    if j < K - 1:
                        ins.then_inc(summed, 1)
                        dve.wait_ge(summed, b * (K - 1) + j + 1)
                ins.then_inc(h_set, 1)

            with dve.Fori(0, B // 2) as i:
                for par in range(2):
                    combine(2 * i + par, par, i)

        @block.gpsimd
        def _(pool):
            pool.memset(scrap[0:1, 0:2], 0.0).then_inc(zeroed, 1)
            pool.wait_ge(zeroed, 1)
            pool.wait_ge(cleared, 1)
            for r in range(2):
                pool.wait_ge(y_out[r], 16 * E // 2)

            def fetch(b, par, first=False):
                if not first:
                    pool.wait_ge(h_set, b - 1)
                pool.tensor_copy(idx[:, par, :], g.rows[:, bass.ds(b * (2 * K), 2 * K)]).then_inc(idx_set, 1)
                pool.wait_ge(idx_set, b + 1)
                pool.tensor_tensor(scrap[0:1, 4 + par:5 + par], scrap[0:1, 0:1], scrap[0:1, 1:2], ALU.add)
                for c in range(2 * K):
                    pool.indirect_dma_start(yg[:, par, c, :], None, ye[:, :],
                                            bass.IndirectOffsetOnAxis(ap=idx[:, par, c:c + 1], axis=0),
                                            bounds_check=E * CAP - 1, oob_is_err=False).then_inc(fetched[par], 16)

            fetch(0, 0, True)
            fetch(1, 1, True)
            with pool.Fori(1, B // 2) as i:
                for par in range(2):
                    fetch(2 * i + par, par)


class Shared:
    pass


def used_before(nc, sems):
    return any(s.num in nc.released_uncleared_semaphores for s in sems)


def audio_tower(nc, x, w, out):
    ctx = ExitStack()
    with ctx:
        def sb(name, shape, dt=F32):
            return ctx.enter_context(nc.sbuf_tensor(name, shape, dt))

        g = Shared()
        g.sem = lambda name: ctx.enter_context(nc.semaphore(name))
        g.h = sb("h", [HT, NT * D])
        g.cst = sb("cst", [128, C_END])
        g.mhalf = sb("mhalf", [HT, 2])
        g.upb = sb("upb", [HT, HT], BF16)
        g.onesb = sb("onesb", [HT, 128], BF16)
        g.back = sb("back", [HT, NT], U32)
        g.rows = sb("rows", [HT, NT * TOPK])
        g.gates = sb("gates", [HT, NT * TOPK])
        xe = nc.dram_tensor("xe", (E1 * CAP1, D), F32, kind="Internal").ap()
        ye = nc.dram_tensor("ye", (E1 * CAP1, D), F32, kind="Internal").ap()
        xs = nc.dram_tensor("xs", (E0 * XROWS, D), F32, kind="Internal").ap()
        ys = nc.dram_tensor("ys", (128 * TILES0, D), F32, kind="Internal").ap()
        stage_attention0(nc, g, x, w, xe)
        g.xTs = sb("xTs", [128, DC, B * N])
        stage_ffn0(nc, g, w, xs, ys)
        stage_attention1(nc, g, w, ys, xe)
        stage_ffn1(nc, g, w, xe, ye, out)

_INS = ["x", "L0_tok_W", "L0_tok_b", "L0_tok_alpha", "L0_attn_w_q", "L0_attn_w_kv", "L0_attn_w_out",
        "L0_ffn_Wg", "L0_ffn_bg", "L0_ffn_W1", "L0_ffn_b1", "L0_ffn_W2", "L0_ffn_b2",
        "L1_attn_Wq", "L1_attn_Wk", "L1_attn_Wv", "L1_attn_Wo", "L1_attn_Wd", "L1_attn_bd", "L1_attn_out_scale",
        "L1_ffn_gate_w", "L1_ffn_w_gate_up", "L1_ffn_w_down", "L1_ffn_shared_w_gate_up", "L1_ffn_shared_w_down"]


def constants():
    import numpy as np
    c = np.zeros((128, C_END), np.float32)
    l = np.arange(L)
    j = np.where(l % 2 == 0, l // 2, L - 1 - l // 2)
    dct = np.cos(2 * np.pi * ((j[:, None] * np.arange(KF)[None, :]) % L) / L)
    c[:, C_DCT:C_DCT + 256] = dct.reshape(128, 256)
    inv = (np.float32(1.0) / np.float32(10000.0) ** (np.arange(0, 32, 2, dtype=np.float32) / np.float32(32))).astype(np.float32)
    f = (np.arange(N, dtype=np.float32)[:, None] * inv[None, :]).astype(np.float32)
    d = np.arange(128) % HD
    c[:, C_COS:C_COS + N] = np.where(d[:, None] < 32, np.cos(f[:, d % 16]).T, 1.0)
    sign = np.where(d < 16, -1.0, np.where(d < 32, 1.0, 0.0))
    c[:, C_SIN:C_SIN + N] = sign[:, None] * np.sin(f[:, d % 16]).T
    c[:, C_ID:C_ID + 128] = np.eye(128)
    r = np.arange(HT)
    c[0:HT, C_MASK:C_MASK + HT] = np.where(r[:, None] > r[None, :], -1e30, 0.0)
    c[0:HT, C_UP:C_UP + HT] = r[:, None] < r[None, :]
    c[:, C_IOTA:C_IOTA + 32] = np.arange(32)
    c[:, C_PART] = np.arange(128)
    c[:, C_SEQ:C_SEQ + 64] = np.arange(64)
    c[:, C_M128:C_M128 + NT] = 128 * np.arange(NT)
    e = np.arange(E0)
    c[:, C_TRI:C_TRI + E0 * E0] = (e[None, :] <= e[:, None]).reshape(-1)
    c[:, C_BASE0:C_BASE0 + E0] = XROWS * e
    behind = np.concatenate([r[:, None] - r[None, :], HT + r[:, None] - np.arange(N)[None, :]], axis=1)
    c[0:HT, C_DIST:C_DIST + 3 * HT] = np.maximum(behind - 1, 0)
    c[0:HT, C_LATER:C_LATER + 3 * HT] = (behind > 0) / D ** 0.5
    return c


def kernel(**inputs):
    import numpy as np
    import concourse.bacc as bacc
    from concourse.bass_utils import run_bass_kernel_spmd as run

    nc = bacc.Bacc("TRN2", target_bir_lowering=False, num_devices=1)
    arrays, aps = {}, {}
    given = {n: np.ascontiguousarray(inputs[n]) for n in _INS}
    given["consts"] = constants()
    for name, a in given.items():
        arrays[f"in_{name}_dram"] = a
        aps[name] = nc.dram_tensor(f"in_{name}_dram", a.shape, mybir.dt.from_np(a.dtype), kind="ExternalInput").ap()
    out = nc.dram_tensor("out_0_dram", (B, N, D), F32, kind="ExternalOutput").ap()
    audio_tower(nc, aps["x"], aps, out)
    r = run(nc, [arrays], core_ids=[0])
    return r.results[0]["out_0_dram"]
```

```python
import concourse.bass as bass
from concourse import mybir
from contextlib import ExitStack

F32 = mybir.dt.float32
F32R = mybir.dt.float32r
BF16 = mybir.dt.bfloat16
I32 = mybir.dt.int32
U32 = mybir.dt.uint32
ALU = mybir.AluOpType
ACT = mybir.ActivationFunctionType
AX = mybir.AxisListType

B, L, N = 16, 512, 250
D = 256
KF = 64
HT = N // 2
NT = 2 * B
DC = D // 128
H, HD = 16, 64
PAIRS = H // 2
EPS = 1e-5
CHUNK = D

E0 = 8
XROWS = B * N + 128
TILES0 = (B * N + E0 * 127) // 128
E1, TOPK, CAP1 = 32, 4, 256
ZROWS = 4
ROW = D + 2 * TOPK + 1
OUTROWS = 1 + B * N + CAP1
I1 = 128

C_DCT, C_COS, C_SIN, C_ID = 0, 256, 256 + N, 256 + 2 * N
C_MASK = C_ID + 128
C_UP = C_MASK + HT
C_IOTA = C_UP + HT
C_PART = C_IOTA + 32
C_END = C_PART + 1
C_SEQ = 0
C_M128 = C_SEQ + 64
C_TRI = C_M128 + NT
C_BASE0 = C_TRI + E0 * E0
C_END3 = C_BASE0 + E0
C_DIST = 0
C_LATER = C_DIST + 3 * HT
C_END2 = C_LATER + 3 * HT

UNITS = [("q", 0), ("k", 0), ("v", 0), ("q", 1), ("k", 1), ("v", 1),
         ("q", 2), ("k", 2), ("v", 2), ("q", 3), ("k", 3), ("v", 3)]
QK = [u for u in UNITS if u[0] != "v"]
STEPS = [[("xT", 0), ("q", 0), ("k", 0), ("turn", 2)],
         [("v", 0), ("freq", 0), ("turn", 3)],
         [("q", 1), ("k", 1)],
         [("v", 1), ("proj", 0), ("tok", 0)],
         [("q", 2), ("k", 2)],
         [("v", 2), ("proj", 1), ("turn", 0)],
         [("q", 3), ("k", 3)],
         [("v", 3), ("turn", 1)]]
PROLOGUE = [("freq", 0), ("tok", 0), ("xT", 0), ("freq", 1), ("tok", 1)] + UNITS


def in_step(b, t):
    names = STEPS[t]
    if isinstance(b, int):
        if b == 0:
            names = [n for n in names if n[0] != "proj" and n not in (("turn", 2), ("turn", 3))]
        if b >= B - 2:
            names = [n for n in names if n[0] not in ("freq", "tok")]
        if b >= B - 1:
            names = [n for n in names if n[0] in ("turn", "proj")]
        if b >= B:
            names = [n for n in names if n not in (("turn", 0), ("turn", 1))]
    return names


def in_batch(b):
    return [n for t in range(PAIRS) for n in in_step(b, t)]


class Step:

    def __init__(self, i, par):
        self.i, self.par = i, par
        self.b = 2 * i + par

    def gen(self, name):
        i, b = (self.i, self.b) if isinstance(self.i, int) else (1, 2 + self.par)
        k = len(PROLOGUE) + sum(len(in_batch(e)) for e in range(b)) + in_batch(self.b).index(name)
        per_two = len(in_batch(2))
        return k % 2, k // 2 + 1 + per_two * (self.i - i)

    def before(self):
        return Step(self.i, 0) if self.par else Step(self.i - 1, 1)


def within(b):
    return not isinstance(b, int) or 0 <= b < B


class Start:

    def gen(self, name):
        k = PROLOGUE.index(name)
        return k % 2, k // 2 + 1


def wait_for(eng, s, n):
    if not (isinstance(n, int) and n < 1):
        eng.wait_ge(s, n)
def stage_attention0(nc, g, x, w):
    ctx = ExitStack()
    with ctx:
        def sb(name, shape, dt=F32):
            return ctx.enter_context(nc.sbuf_tensor(name, shape, dt))

        def sem(name):
            return ctx.enter_context(nc.semaphore(name))

        h, cst, mhalf = g.h, g.cst, g.mhalf
        SLOTS = 3
        idb = sb("idb", [HT, HT], BF16)
        maskb = sb("maskb", [HT, HT], BF16)
        tokw = sb("tokw", [KF + 1, D])
        alpha = sb("alpha", [HT, 1])
        wraw = sb("wraw", [128, SLOTS, DC, CHUNK])
        wqkv = sb("wqkv", [128, 2, DC, 3 * H * HD], F32R)
        wo = sb("wo", [128, 2, 8, D], F32R)
        xin = sb("xin", [128, 4, N])
        freq = sb("freq", [KF + 1, N])
        stats = sb("stats", [HT, 2, 6])
        mv = sb("mv", [HT, 2, 2])
        rstd = sb("rstd", [HT, 2])
        xn = sb("xn", [HT, 2, D])
        xT = sb("xT", [128, 2, DC, N], F32R)
        scrap = sb("scrap", [1, 1])
        raw = sb("raw", [128, 2, 2 * N])
        rot = sb("rot", [128, 2, 2 * N])
        qT = sb("qT", [128, 2, PAIRS, N])
        kT = sb("kT", [128, 2, PAIRS, N])
        v = sb("v", [HT, 2, 2, H * HD])
        nmax = sb("nmax", [HT, 2, 2, 2])
        sums = sb("sums", [HT, 2, 2, 4])
        rinv = sb("rinv", [HT, 2, 2, 4])
        pr = sb("pr", [HT, 2, 2, 3 * HT])
        prT = sb("prT", [HT, 2, 3 * HT])
        o = sb("o", [HT, 2, H * HD])
        oT = sb("oT", [128, 2, 8, N], F32R)
        gen = [ctx.enter_context(nc.psum_tensor(f"gen{i}", [128, 512], F32)) for i in range(2)]
        S = ctx.enter_context(nc.psum_tensor("Sp", [128, 2, 512], F32))
        PT = ctx.enter_context(nc.psum_tensor("PT", [128, 2, 512], F32))
        O = [ctx.enter_context(nc.psum_tensor(f"O{i}", [128, 512], F32)) for i in range(2)]

        loaded = sem("loaded")
        oT_high = sem("oT_high")
        w_in = [sem(f"w_in{n}") for n in range(SLOTS)]
        w_high = sem("w_high")
        w_split = sem("w_split")
        xT_high = sem("xT_high")
        ones_set = sem("ones_set")
        const_b = sem("const_b")
        x_in = sem("x_in")
        filled = [sem("filled0"), sem("filled1")]
        emptied = [sem("emptied0"), sem("emptied1")]
        s_full = sem("s_full")
        nmax_set = sem("nmax_set")
        exped = sem("exped")
        pt_full = sem("pt_full")
        pt_out0 = sem("pt_out0")
        pt_out1 = sem("pt_out1")
        av_done = sem("av_done")
        rinv_set = sem("rinv_set")
        o_set = sem("o_set")
        shuf_set = sem("shuf_set")
        rot_set = sem("rot_set")
        cos_set = sem("cos_set")
        roped = sem("roped")
        ln_stat, ln_mv, ln_eps, ln_pow, ln_done = (sem(n) for n in ("ln_stat", "ln_mv", "ln_eps", "ln_pow", "ln_done"))

        ident = cst[:, C_ID:C_ID + 128]
        loads = [(cst[:, :], w["consts"]), (tokw[0:KF, :], w["L0_tok_W"]), (tokw[KF:KF + 1, :], w["L0_tok_b"].rearrange("(a d) -> a d", a=1)),
                 (alpha[:, :], w["L0_tok_alpha"].rearrange("(a d) -> a d", a=1).broadcast_to([HT, 1])),
                 ]
        chunks, needs = [], {}
        for kind, j in UNITS:
            for n in [j] if kind != "v" else [] if j > 1 else [2 * j, 2 * j + 1]:
                name, at = ("L0_attn_w_q", 0) if kind == "q" else ("L0_attn_w_kv", H * HD)
                n += 0 if kind != "v" else H * HD // CHUNK
                chunks.append((w[name][:, CHUNK * n:CHUNK * (n + 1)].rearrange("(c p) n -> p c n", p=128),
                               wqkv[:, :, :, at + CHUNK * n:at + CHUNK * (n + 1)]))
            needs[kind, j] = len(chunks)
        for n in range(0, 8, DC):
            chunks.append((w["L0_attn_w_out"][128 * n:128 * (n + DC), :].rearrange("(c p) n -> p c n", p=128),
                           wo[:, :, n:n + DC, :]))
        LOADED = 16 * len(loads)
        block = ctx.enter_context(nc.Block())

        def halves(bank, width=N):
            return bank[:, 0:2 * width].rearrange("p (a n) -> p a n", a=2)

        def x_of(b):
            return x[bass.ds(b, 1), :, :].rearrange("b (p c) n -> p (b c) n", c=4)

        @block.sync
        def _(sp):
            for dst, src in loads:
                sp.dma_start(dst, src).then_inc(loaded, 16)
            sp.dma_start(xin[:, :, :], x_of(0)).then_inc(x_in, 16)
            for n, (src, _) in enumerate(chunks):
                if n == SLOTS:
                    bank, k = Start().gen(("freq", 0))
                    sp.wait_ge(emptied[bank], k)
                    sp.dma_start(xin[:, :, :], x_of(1)).then_inc(x_in, 16)
                if n == needs[UNITS[-1]]:
                    bank, k = Start().gen(("freq", 1))
                    sp.wait_ge(emptied[bank], k)
                    sp.dma_start(xin[:, :, :], x_of(2)).then_inc(x_in, 16)
                if n >= SLOTS:
                    sp.wait_ge(w_split, n - SLOTS + 1)
                sp.dma_start(wraw[:, n % SLOTS, :, :], src).then_inc(w_in[n % SLOTS], 16)
            def body(s):
                bank, n = s.gen(("freq", 0))
                sp.wait_ge(emptied[bank], n)
                sp.dma_start(xin[:, :, :], x_of(s.b + 3)).then_inc(x_in, 16)

            body(Step(0, 0))
            body(Step(0, 1))
            with sp.Fori(1, B // 2 - 2) as i:
                body(Step(i, 0))
                body(Step(i, 1))
            body(Step(B // 2 - 2, 0))

        @block.tensor
        def _(pe):
            def fill(s, name):
                bank, n = s.gen(name)
                wait_for(pe, emptied[bank], n - 1)
                return gen[bank], filled[bank]

            def after(s, name):
                bank, n = s.gen(name)
                pe.wait_ge(emptied[bank], n)

            def freq_product(s, name, b):
                pe.wait_ge(x_in, 16 * b + 16)
                g, done = fill(s, name)
                for c in range(4):
                    mm = pe.matmul(g[0:KF, 0:N], cst[:, C_DCT + KF * c:C_DCT + KF * c + KF], xin[:, c, :],
                                   start=(c == 0), stop=(c == 3))
                mm.then_inc(done, 1)

            def tok_product(s, name, freq_name):
                g, done = fill(s, name)
                after(s, freq_name)
                for it in range(2):
                    mm = pe.matmul(g[0:HT, D * it:D * it + D], freq[:, HT * it:HT * it + HT], tokw[:, :],
                                   start=True, stop=True)
                mm.then_inc(done, 1)

            def turn_xn(s, name, b):
                g, done = fill(s, name)
                pe.wait_ge(ln_done, b + 1)
                for c in range(DC):
                    for it in range(2):
                        mm = pe.transpose(g[:, N * c + HT * it:N * c + HT * it + HT],
                                          xn[:, it, 128 * c:128 * c + 128], ident[0:HT, 0:HT])
                mm.then_inc(done, 1)

            def exact(dst, lhs, rhs, blocks=DC):
                for n, (x_part, y_part) in enumerate(((0, 0), (0, 1), (1, 0))):
                    for c in range(blocks):
                        mm = pe.matmul(dst, lhs(x_part, c), rhs(y_part, c), start=(n + c == 0), stop=(n + c == blocks + 1))
                return mm

            def unit(s, u):
                kind, j = u
                g, done = fill(s, u)
                if kind == "v":
                    it, half = j // 2, j % 2
                    col = 2 * H * HD + 512 * half
                    mm = exact(g[0:HT, :], lambda p, c: xT[:, p, c, HT * it:HT * it + HT],
                               lambda p, c: wqkv[:, p, c, col:col + 512])
                else:
                    for a in range(2):
                        col = (H * HD if kind == "k" else 0) + 128 * (2 * j + a)
                        mm = exact(g[:, N * a:N * a + N], lambda p, c: wqkv[:, p, c, col:col + 128],
                                   lambda p, c: xT[:, p, c, :])
                mm.then_inc(done, 1)

            def scores(s, t):
                pe.wait_ge(roped, len(QK) * s.b + 2 * (t // 2) + 2)
                wait_for(pe, exped, PAIRS * s.b + t)
                for it in range(2):
                    for hd in range(2):
                        r = slice(64 * hd, 64 * hd + 64)
                        at = HT * it
                        pe.matmul(S[0:HT, hd, at:at + HT * (it + 1)], qT[r, s.par, t, at:at + HT],
                                  kT[r, s.par, t, 0:HT * (it + 1)], start=True, stop=False)
                    for hd in range(2):
                        mm = pe.matmul(S[0:HT, hd, 2 * HT * it:2 * HT * it + HT], maskb[:, :], idb[:, :],
                                       start=False, stop=True)
                mm.then_inc(s_full, 1)

            def turn_probs(s, t):
                pe.wait_ge(exped, PAIRS * s.b + t + 1)
                wait_for(pe, pt_out0, PAIRS * s.b + t)
                wait_for(pe, pt_out1, PAIRS * s.b + t)
                for hd in range(2):
                    for j in range(3):
                        mm = pe.transpose(PT[0:HT, hd, HT * j:HT * j + HT], pr[:, t % 2, hd, HT * j:HT * j + HT],
                                          ident[0:HT, 0:HT])
                mm.then_inc(pt_full, 1)

            def weigh_values(s, t):
                grp = t // 2
                pe.wait_ge(pt_out0, PAIRS * s.b + t + 1)
                pe.wait_ge(pt_out1, PAIRS * s.b + t + 1)
                if t % 2 == 0:
                    wait_for(pe, o_set, 4 * s.b + grp - 1)
                for hd in range(2):
                    hh = 2 * t + hd
                    hc = slice(HD * hh, HD * hh + HD)
                    at = HD * (hh % 4)
                    pe.matmul(O[grp % 2][0:HT, at:at + HD], prT[:, hd, 0:HT], v[:, s.par, 0, hc],
                              start=True, stop=True)
                    pe.matmul(O[grp % 2][0:HT, 256 + at:256 + at + HD], prT[:, hd, HT:2 * HT], v[:, s.par, 0, hc],
                              start=True, stop=False)
                    mm = pe.matmul(O[grp % 2][0:HT, 256 + at:256 + at + HD], prT[:, hd, 2 * HT:3 * HT],
                                   v[:, s.par, 1, hc], start=False, stop=True)
                mm.then_inc(av_done, 1)

            def turn_o(s, grp, b):
                g, done = fill(s, ("turn", grp))
                pe.wait_ge(o_set, 4 * b + grp + 1)
                for cc in range(2):
                    for it in range(2):
                        at = N * cc + HT * it
                        mm = pe.transpose(g[:, at:at + HT], o[:, it, 256 * grp + 128 * cc:256 * grp + 128 * cc + 128],
                                          ident[0:HT, 0:HT])
                mm.then_inc(done, 1)

            def project(s, it):
                g, done = fill(s, ("proj", it))
                if it == 0:
                    after(s, ("turn", 2))
                    after(s, ("turn", 3))
                exact(g[0:HT, 0:D], lambda p, c: oT[:, p, c, HT * it:HT * it + HT],
                      lambda p, c: wo[:, p, c, :], blocks=8).then_inc(done, 1)

            def body(s):
                before = s.before()
                for t in range(PAIRS):
                    p = (s, t - 1) if t else (before, PAIRS - 1)
                    names = in_step(s.b, t)
                    if ("xT", 0) in names:
                        turn_xn(s, ("xT", 0), s.b + 1)
                    if within(s.b):
                        scores(s, t)
                    if within(p[0].b):
                        turn_probs(*p)
                    if ("xT", 0) in names:
                        after(s, ("xT", 0))
                    for n in names:
                        if n in UNITS:
                            unit(s, n)
                        elif n[0] == "proj":
                            project(s, n[1])
                        elif n[0] == "freq":
                            freq_product(s, n, s.b + 2)
                        elif n[0] == "tok":
                            tok_product(s, n, ("freq", 0))
                    if within(p[0].b):
                        weigh_values(*p)
                    for n in names:
                        if n[0] == "turn":
                            turn_o(s, n[1], s.b if n[1] < 2 else before.b)

            st = Start()
            pe.wait_ge(loaded, LOADED)
            pe.wait_ge(ones_set, 2)
            pe.wait_ge(const_b, 2)
            freq_product(st, ("freq", 0), 0)
            tok_product(st, ("tok", 0), ("freq", 0))
            turn_xn(st, ("xT", 0), 0)
            after(st, ("xT", 0))
            freq_product(st, ("freq", 1), 1)
            tok_product(st, ("tok", 1), ("freq", 1))
            for u in UNITS:
                pe.wait_ge(w_split, needs[u])
                unit(st, u)
            body(Step(0, 0))
            pe.wait_ge(w_split, len(chunks))
            body(Step(0, 1))
            with pe.Fori(1, B // 2 - 1) as i:
                body(Step(i, 0))
                body(Step(i, 1))
            for b in range(B - 2, B + 1):
                body(Step(b // 2, b % 2))

        @block.scalar
        def _(act):
            def evict(s, name, dst, src, scale=None):
                bank, n = s.gen(name)
                act.wait_ge(filled[bank], n)
                if scale is None:
                    act.copy(dst, src(gen[bank])).then_inc(emptied[bank], 1)
                else:
                    act.mul(dst, src(gen[bank]), scale).then_inc(emptied[bank], 1)

            def freq_out(s, name):
                evict(s, name, freq[0:KF, :], lambda g: g[0:KF, 0:N])

            def xT_high_out(s, name):
                bank, n = s.gen(name)
                act.wait_ge(filled[bank], n)
                act.copy(xT[:, 0, :, :], halves(gen[bank])).then_inc(xT_high, 1)

            def unit_out(s, u, par, b):
                kind, j = u
                if kind == "v":
                    evict(s, u, v[:, par, j // 2, 512 * (j % 2):512 * (j % 2) + 512], lambda g: g[0:HT, :])
                else:
                    k = QK.index(u)
                    n = len(QK) * b + k - 1
                    wait_for(act, cos_set, n)
                    wait_for(act, shuf_set, n)
                    evict(s, u, raw[:, k % 2, :], lambda g: g[:, 0:2 * N], scale=HD ** -0.5 if kind == "q" else None)

            def weights_high(n):
                act.wait_ge(w_in[n % SLOTS], 16 * (n // SLOTS) + 16)
                act.copy(chunks[n][1][:, 0, :, :], wraw[:, n % SLOTS, :, :]).then_inc(w_high, 1)

            def exponentials(s, t):
                act.wait_ge(nmax_set, PAIRS * s.b + t + 1)
                grp = t // 2
                for it in range(2):
                    for hd in range(2):
                        c = slice(HT * it, HT * it + HT * (it + 1))
                        e = act.activation(pr[:, t % 2, hd, c], S[0:HT, hd, c], ACT.Exp,
                                           bias=nmax[:, t % 2, it, hd:hd + 1],
                                           accum_out=sums[:, grp % 2, it, 2 * (t % 2) + hd:2 * (t % 2) + hd + 1])
                e.then_inc(exped, 1)

            def probs_out(s, t):
                act.wait_ge(pt_full, PAIRS * s.b + t + 1)
                act.copy(prT[:, 0, :], PT[0:HT, 0, 0:3 * HT]).then_inc(pt_out0, 1)

            def tok_out(s, name, b):
                bank, n = s.gen(name)
                act.wait_ge(filled[bank], n)
                act.activation(h[:, bass.ds(b * (2 * D), 2 * D)], gen[bank][0:HT, :], ACT.Copy,
                               scale=alpha[:, 0:1]).then_inc(emptied[bank], 1)

            def turn_high_out(s, grp):
                bank, n = s.gen(("turn", grp))
                act.wait_ge(filled[bank], n)
                act.copy(oT[:, 0, 2 * grp:2 * grp + 2, :], halves(gen[bank])).then_inc(oT_high, 1)

            def body(s):
                before = s.before()
                for t in range(PAIRS):
                    p = (s, t - 1) if t else (before, PAIRS - 1)
                    names = in_step(s.b, t)
                    if ("xT", 0) in names:
                        xT_high_out(s, ("xT", 0))
                    if within(p[0].b):
                        probs_out(*p)
                    if within(s.b):
                        exponentials(s, t)
                    for n in names:
                        if n in UNITS:
                            unit_out(s, n, 1 - s.par, s.b + 1)
                        elif n[0] == "freq":
                            freq_out(s, n)
                        elif n[0] == "tok":
                            tok_out(s, n, s.b + 2)
                        elif n[0] == "turn":
                            turn_high_out(s, n[1])

            st = Start()
            act.wait_ge(loaded, LOADED)
            act.copy(idb[:, :], cst[0:HT, C_ID:C_ID + HT]).then_inc(const_b, 1)
            act.copy(maskb[:, :], cst[0:HT, C_MASK:C_MASK + HT]).then_inc(const_b, 1)
            act.copy(g.upb[:, :], cst[0:HT, C_UP:C_UP + HT])
            freq_out(st, ("freq", 0))
            tok_out(st, ("tok", 0), 0)
            xT_high_out(st, ("xT", 0))
            freq_out(st, ("freq", 1))
            tok_out(st, ("tok", 1), 1)
            for n in range(needs["q", 0]):
                weights_high(n)
            for i, u in enumerate(UNITS):
                for n in range(needs[u], needs[UNITS[min(i + 1, len(UNITS) - 1)]]):
                    weights_high(n)
                unit_out(st, u, 0, 0)
            body(Step(0, 0))
            for n in range(needs[UNITS[-1]], len(chunks)):
                weights_high(n)
            body(Step(0, 1))
            with act.Fori(1, B // 2 - 1) as i:
                body(Step(i, 0))
                body(Step(i, 1))
            for b in range(B - 2, B + 1):
                body(Step(b // 2, b % 2))

        @block.vector
        def _(dve):
            def settle(s, n):
                dve.wait_ge(s, n)
                dve.memset(scrap[0:1, 0:1], 0.0)

            def h_tiles(b):
                return h[:, bass.ds(b * (2 * D), 2 * D)]

            def norm_stats(s, name, b):
                bank, n = s.gen(name)
                settle(emptied[bank], n)
                for it in range(2):
                    dve.bn_stats(stats[:, it, :], h[:, bass.ds(b * (2 * D) + D * it, D)]).then_inc(ln_stat, 1)
                settle(ln_stat, 2 * b + 2)
                for it in range(2):
                    dve.bn_aggr(mv[:, it, :], stats[:, it, :]).then_inc(ln_mv, 1)
                dve.wait_ge(ln_mv, 2 * b + 2)
                dve.tensor_scalar(rstd[:, :], mv[:, :, 1], EPS, None, ALU.add).then_inc(ln_eps, 1)

            def norm(b):
                dve.wait_ge(ln_pow, b + 1)
                for it in range(2):
                    e = dve.tensor_scalar(xn[:, it, :], h[:, bass.ds(b * (2 * D) + D * it, D)], mv[:, it, 0:1],
                                          rstd[:, it:it + 1], ALU.subtract, ALU.mult)
                e.then_inc(ln_done, 1)

            def xT_low_out(s, name, b):
                bank, n = s.gen(name)
                dve.wait_ge(xT_high, b + 1)
                dve.tensor_tensor(xT[:, 1, :, :], halves(gen[bank]), xT[:, 0, :, :].bitcast(F32),
                                  ALU.subtract).then_inc(emptied[bank], 1)

            def turn_low_out(s, grp, b):
                bank, n = s.gen(("turn", grp))
                dve.wait_ge(oT_high, 4 * b + grp + 1)
                dve.tensor_tensor(oT[:, 1, 2 * grp:2 * grp + 2, :], halves(gen[bank]),
                                  oT[:, 0, 2 * grp:2 * grp + 2, :].bitcast(F32), ALU.subtract).then_inc(emptied[bank], 1)

            def weights_low(n):
                high, low = (chunks[n][1][:, part, :, :] for part in range(2))
                dve.wait_ge(w_high, n + 1)
                dve.tensor_tensor(low, wraw[:, n % SLOTS, :, :], high.bitcast(F32), ALU.subtract).then_inc(w_split, 1)

            def maxima(s, t):
                dve.wait_ge(s_full, PAIRS * s.b + t + 1)
                for it in range(2):
                    e = dve.tensor_reduce(nmax[:, t % 2, it, :], S[0:HT, :, HT * it:HT * it + HT * (it + 1)],
                                          AX.X, ALU.max, negate=True)
                e.then_inc(nmax_set, 1)

            def probs_out(s, t):
                dve.wait_ge(pt_full, PAIRS * s.b + t + 1)
                dve.tensor_copy(prT[:, 1, :], PT[0:HT, 1, 0:3 * HT]).then_inc(pt_out1, 1)

            def rope_parts(s, u, par, b):
                kind, j = u
                k = QK.index(u)
                bank, n = s.gen(u)
                cos = cst[:, C_COS:C_COS + N].unsqueeze(1).broadcast_to([128, 2, N])
                src = raw[:, k % 2, :].rearrange("p (a n) -> p a n", a=2)
                dve.wait_ge(emptied[bank], n)
                wait_for(dve, roped, len(QK) * b + k - 1)
                dve.tensor_tensor(rope_to(u, par), src, cos, ALU.mult).then_inc(cos_set, 1)
                dve.stream_shuffle(rot[:, k % 2, :], raw[:, k % 2, :], [(i + 16) % 32 for i in range(32)]).then_inc(shuf_set, 1)

            def rope_sum(u, par, b):
                k = QK.index(u)
                turned = rot[:, k % 2, :].rearrange("p (a n) -> p a n", a=2)
                dve.wait_ge(cos_set, len(QK) * b + k + 1)
                dve.wait_ge(rot_set, len(QK) * b + k + 1)
                dve.tensor_tensor(rope_to(u, par), rope_to(u, par), turned, ALU.add).then_inc(roped, 1)

            def rope_to(u, par):
                return (qT if u[0] == "q" else kT)[:, par, 2 * u[1]:2 * u[1] + 2, :]

            def normalise(s, grp):
                G = 4 * s.b + grp + 1
                dve.wait_ge(av_done, PAIRS * s.b + 2 * grp + 2)
                dve.reciprocal(rinv[:, grp % 2, :, :], sums[:, grp % 2, :, :]).then_inc(rinv_set, 1)
                dve.wait_ge(rinv_set, G)
                for it in range(2):
                    e = dve.tensor_tensor(o[:, it, 256 * grp:256 * grp + 256].rearrange("p (h d) -> p h d", d=HD),
                                      O[grp % 2][0:HT, 256 * it:256 * it + 256].rearrange("p (h d) -> p h d", d=HD),
                                      rinv[:, grp % 2, it, :].unsqueeze(2).broadcast_to([HT, 4, HD]), ALU.mult)
                e.then_inc(o_set, 1)

            def add_attention(s, it, b):
                bank, n = s.gen(("proj", it))
                tile = h[:, bass.ds(b * (2 * D) + D * it, D)]
                dve.wait_ge(filled[bank], n)
                dve.tensor_tensor(tile, gen[bank][0:HT, 0:D], tile, ALU.add).then_inc(emptied[bank], 1)

            def body(s):
                before = s.before()
                for t in range(PAIRS):
                    p = (s, t - 1) if t else (before, PAIRS - 1)
                    names = in_step(s.b, t)
                    if ("xT", 0) in names:
                        xT_low_out(s, ("xT", 0), s.b + 1)
                    if within(s.b):
                        maxima(s, t)
                    if within(p[0].b):
                        probs_out(*p)
                    if t == 1 and within(before.b):
                        normalise(before, 3)
                    if t in (3, 5, 7) and within(s.b):
                        normalise(s, (t - 3) // 2)
                    if t == 0 and within(s.b) and within(before.b):
                        rope_sum(QK[-1], s.par, s.b)
                    if t and within(s.b + 1):
                        rope_sum(QK[t - 1], 1 - s.par, s.b + 1)
                    if within(s.b + 1):
                        rope_parts(s, QK[t], 1 - s.par, s.b + 1)
                    if t == 4 and within(s.b + 2):
                        norm_stats(s, ("tok", 0), s.b + 2)
                    if t == 5 and within(s.b + 2):
                        norm(s.b + 2)
                    for n in names:
                        if n[0] == "proj":
                            add_attention(s, n[1], before.b)
                        elif n[0] == "turn":
                            turn_low_out(s, n[1], s.b if n[1] < 2 else before.b)

            st = Start()
            dve.memset(freq[KF:KF + 1, :], 1.0).then_inc(ones_set, 1)
            dve.memset(g.onesb[:, :], 1.0)
            dve.wait_ge(loaded, LOADED)
            norm_stats(st, ("tok", 0), 0)
            norm(0)
            xT_low_out(st, ("xT", 0), 0)
            norm_stats(st, ("tok", 1), 1)
            norm(1)
            for n in range(needs["q", 0]):
                weights_low(n)
            for i, u in enumerate(UNITS):
                for n in range(needs[u], needs[UNITS[min(i + 1, len(UNITS) - 1)]]):
                    weights_low(n)
                if u in QK:
                    rope_parts(st, u, 0, 0)
                    if u != QK[0]:
                        rope_sum(QK[QK.index(u) - 1], 0, 0)
            rope_sum(QK[-1], 0, 0)
            body(Step(0, 0))
            for n in range(needs[UNITS[-1]], len(chunks)):
                weights_low(n)
            body(Step(0, 1))
            with dve.Fori(1, B // 2 - 1) as i:
                body(Step(i, 0))
                body(Step(i, 1))
            for b in range(B - 2, B + 1):
                body(Step(b // 2, b % 2))

        @block.gpsimd
        def _(pool):
            def power(b):
                pool.wait_ge(ln_eps, b + 1)
                pool.tensor_tensor(rstd[:, :], rstd[:, :], mhalf[:, :], ALU.pow).then_inc(ln_pow, 1)

            def times_sine(b, k):
                pool.wait_ge(shuf_set, len(QK) * b + k + 1)
                turned = rot[:, k % 2, :].rearrange("p (a n) -> p a n", a=2)
                pool.tensor_tensor(turned, turned, cst[:, C_SIN:C_SIN + N].unsqueeze(1).broadcast_to([128, 2, N]),
                                   ALU.mult).then_inc(rot_set, 1)

            def body(s):
                for k in range(len(QK)):
                    if within(s.b + 1):
                        times_sine(s.b + 1, k)
                    if k == 4 and within(s.b + 2):
                        power(s.b + 2)

            pool.memset(mhalf[:, :], -0.5).then_inc(ones_set, 1)
            pool.wait_ge(ones_set, 2)
            pool.wait_ge(loaded, LOADED)
            power(0)
            power(1)
            for k in range(len(QK)):
                times_sine(0, k)
            body(Step(0, 0))
            body(Step(0, 1))
            with pool.Fori(1, B // 2 - 1) as i:
                body(Step(i, 0))
                body(Step(i, 1))
            for b in range(B - 2, B):
                body(Step(b // 2, b % 2))
def stage_ffn0(nc, g, w, xs, ys, xe, out):
    ctx = ExitStack()
    with ctx:
        def sb(name, shape, dt=F32):
            return ctx.enter_context(nc.sbuf_tensor(name, shape, dt))

        def sem(name):
            s = ctx.enter_context(nc.semaphore(name))
            assert not used_before(nc, [s])
            return s

        def ps(name):
            return ctx.enter_context(nc.psum_tensor(name, [128, 512], F32))

        h, cst = g.h, g.cst
        ident = cst[:, C_ID:C_ID + 128]
        SLOTS = 4
        xn = sb("b_xn", [HT, SLOTS, 2, D])
        stats = sb("b_stats", [HT, 2, 6])
        mv = sb("b_mv", [HT, 2, 2])
        rstd = sb("b_rstd", [HT, 2])
        xT = sb("b_xT", [128, DC, N])
        lg = sb("b_lg", [HT, 2, E0])
        top = sb("b_top", [HT, 2, 8])
        topi = sb("b_topi", [HT, 2, 8], U32)
        pick = sb("b_pick", [HT, 2])
        hot = sb("b_hot", [HT, 2, E0], BF16)
        rank = sb("b_rank", [HT, 2, E0])
        row = sb("b_row", [HT, 2])
        rowi = sb("b_rowi", [HT, SLOTS, 2], U32)
        fill_row = sb("b_fill", [128, E0])
        picks = sb("b_picks", [HT, NT])
        rows = sb("b_rows", [HT, NT])
        more = sb("b_more", [128, E0, NT])
        ntile = sb("b_ntile", [128, E0])
        tri = sb("b_tri", [128, E0, E0])
        tend = sb("b_tend", [128, E0])
        shift = sb("b_shift", [128, E0])
        hots = sb("b_hots", [HT, NT, E0])
        move = sb("b_move", [HT, NT])
        padf = sb("b_padf", [128, E0])
        padi = sb("b_padi", [1, E0], I32)
        zero = sb("b_zero", [128, ZROWS * ROW])
        over = sb("b_over", [1, TILES0, E0])
        te = sb("b_te", [1, 3, TILES0])
        tfirst = sb("b_tfirst", [1, TILES0])
        tab = sb("b_tab", [1, 2 * TILES0], I32)
        scrap = sb("b_scrap", [1, 8])
        tcst = sb("b_tcst", [128, C_END3])
        wgate = sb("b_wgate", [128, DC, E0])
        bgate = sb("b_bgate", [HT, E0])
        w1 = sb("b_w1", [128, E0 * DC * D])
        w2 = sb("b_w2", [128, E0 * DC * D])
        b1 = sb("b_b1", [128, E0 * D])
        b2 = sb("b_b2", [128, E0 * D])
        W_IN = 16 * (2 * E0 + 2)
        gate_in, w_in = sem("b_gate_in"), sem("b_w_in")

        ln_stat, ln_mv, ln_eps, ln_pow, ln_done = (sem("b_" + n) for n in ("ln_stat", "ln_mv", "ln_eps", "ln_pow", "ln_done"))
        t_full, t_out = sem("b_t_full"), sem("b_t_out")
        lg_full, lg_out = sem("b_lg_full"), sem("b_lg_out")
        topped, indexed, picked, hot_set = (sem("b_" + n) for n in ("topped", "indexed", "picked", "hot_set"))
        rank_full, ranked, masked, rowed, row_set, counted = (sem("b_" + n) for n in ("rank_full", "ranked", "masked", "rowed", "row_set", "counted"))
        scattered = [sem(f"b_scattered{i}") for i in range(SLOTS)]
        cleared = sem("b_cleared")
        zeroed, padded, chain, tabled, pad_set = (sem("b_" + n) for n in ("zeroed", "padded", "chain", "tabled", "pad_set"))

        tps, lps, rps = ps("b_tps"), ps("b_lps"), ps("b_rps")
        block = ctx.enter_context(nc.Block())

        @block.sync
        def _(sp):
            sp.dma_start(wgate[:, :, :], w["L0_ffn_Wg"].rearrange("(c p) e -> p c e", p=128)).then_inc(gate_in, 16)
            sp.dma_start(tcst[:, :], w["tile_consts"]).then_inc(gate_in, 16)
            sp.dma_start(bgate[:, :], w["L0_ffn_bg"].rearrange("(a e) -> a e", a=1).broadcast_to([HT, E0])).then_inc(gate_in, 16)
            for e in range(E0):
                at = slice(DC * D * e, DC * D * (e + 1))
                for dst, src in ((w1, w["L0_ffn_W1"]), (w2, w["L0_ffn_W2"])):
                    sp.dma_start(dst[:, at].rearrange("p (c i) -> p c i", c=DC),
                                 src[e].rearrange("(c p) i -> p c i", p=128)).then_inc(w_in, 16)
            for dst, src in ((b1, w["L0_ffn_b1"]), (b2, w["L0_ffn_b2"])):
                sp.dma_start(dst[:, :], src.rearrange("(a e) i -> a (e i)", a=1).broadcast_to([128, E0 * D])).then_inc(w_in, 16)

        @block.tensor
        def _(pe):
            def turn(b, slot):
                pe.wait_ge(ln_done, b + 1)
                for c in range(DC):
                    for it in range(2):
                        mm = pe.transpose(tps[:, N * c + HT * it:N * c + HT * it + HT],
                                          xn[:, slot, it, 128 * c:128 * c + 128], ident[0:HT, 0:HT])
                mm.then_inc(t_full, 1)

            def logits(b):
                pe.wait_ge(t_out, b + 1)
                pe.wait_ge(lg_out, b)
                for it in range(2):
                    for c in range(DC):
                        mm = pe.matmul(lps[0:HT, E0 * it:E0 * it + E0], xT[:, c, HT * it:HT * it + HT],
                                       wgate[:, c, :], start=(c == 0), stop=(c == DC - 1))
                mm.then_inc(lg_full, 1)

            def ranks(b):
                pe.wait_ge(hot_set, b + 1)
                pe.wait_ge(counted, b)
                pe.matmul(rps[0:HT, 0:E0], g.upb[:, :], hot[:, 0, :], start=True, stop=True)
                pe.matmul(rps[0:HT, E0:2 * E0], g.upb[:, :], hot[:, 1, :], start=True, stop=False)
                pe.matmul(rps[0:HT, E0:2 * E0], g.onesb[:, 0:HT], hot[:, 0, :], start=False, stop=True)
                pe.matmul(rps[:, 2 * E0:3 * E0], g.onesb[:, :], hot[:, 0, :], start=True, stop=False)
                pe.matmul(rps[:, 2 * E0:3 * E0], g.onesb[:, :], hot[:, 1, :], start=False, stop=True).then_inc(rank_full, 1)

            def body(b, q, last=False):
                if not last:
                    turn(b + 1, (q + 1) % SLOTS)
                ranks(b)
                if not last:
                    logits(b + 1)

            pe.wait_ge(gate_in, 48)
            turn(0, 0)
            logits(0)
            for q in range(SLOTS):
                body(q, q)
            with pe.Fori(1, B // SLOTS - 1) as i:
                for q in range(SLOTS):
                    body(SLOTS * i + q, q)
            for q in range(SLOTS):
                body(B - SLOTS + q, q, last=(q == SLOTS - 1))

        @block.scalar
        def _(act):
            def turn_out(b):
                act.wait_ge(t_full, b + 1)
                if not (isinstance(b, int) and b == 0):
                    act.wait_ge(lg_full, b)
                act.copy(xT[:, :, :], tps[:, 0:2 * N].rearrange("p (c n) -> p c n", c=DC)).then_inc(t_out, 1)

            turn_out(0)
            turn_out(1)
            with act.Fori(2, B) as b:
                turn_out(b)

        @block.vector
        def _(dve):
            def settle(s, n):
                dve.wait_ge(s, n)
                dve.memset(scrap[0:1, 0:1], 0.0)

            def statistics(b):
                if not (isinstance(b, int) and b == 0):
                    dve.wait_ge(ln_done, b)
                for it in range(2):
                    dve.bn_stats(stats[:, it, :], h[:, bass.ds(b * (2 * D) + D * it, D)]).then_inc(ln_stat, 1)
                settle(ln_stat, 2 * b + 2)
                for it in range(2):
                    dve.bn_aggr(mv[:, it, :], stats[:, it, :]).then_inc(ln_mv, 1)
                dve.wait_ge(ln_mv, 2 * b + 2)
                dve.tensor_scalar(rstd[:, :], mv[:, :, 1], EPS, None, ALU.add).then_inc(ln_eps, 1)

            def norm(b, slot, i):
                if i is not None:
                    dve.wait_ge(scattered[slot], 32 * i)
                dve.wait_ge(ln_pow, b + 1)
                for it in range(2):
                    e = dve.tensor_scalar(xn[:, slot, it, :], h[:, bass.ds(b * (2 * D) + D * it, D)], mv[:, it, 0:1],
                                          rstd[:, it:it + 1], ALU.subtract, ALU.mult)
                e.then_inc(ln_done, 1)

            def choose(b):
                dve.wait_ge(lg_full, b + 1)
                dve.tensor_tensor(lg[:, :, :], lps[0:HT, 0:2 * E0].rearrange("p (t e) -> p t e", t=2),
                                  bgate[:, :].unsqueeze(1).broadcast_to([HT, 2, E0]), ALU.add).then_inc(lg_out, 1)
                settle(lg_out, b + 1)
                for it in range(2):
                    dve.max(top[:, it, :], lg[:, it, :]).then_inc(topped, 1)
                settle(topped, 2 * b + 2)
                for it in range(2):
                    dve.max_index(topi[:, it, :], top[:, it, :], lg[:, it, :]).then_inc(indexed, 1)
                dve.wait_ge(indexed, 2 * b + 2)
                dve.tensor_copy(pick[:, :], topi[:, :, 0]).then_inc(picked, 1)
                dve.wait_ge(picked, b + 1)
                dve.tensor_copy(picks[:, bass.ds(2 * b, 2)], pick[:, :])
                dve.tensor_tensor(hot[:, :, :], pick[:, :].unsqueeze(2).broadcast_to([HT, 2, E0]),
                                  cst[0:HT, C_IOTA:C_IOTA + E0].unsqueeze(1).broadcast_to([HT, 2, E0]),
                                  ALU.is_equal).then_inc(hot_set, 1)

            def place(b, slot):
                dve.wait_ge(rank_full, b + 1)
                dve.wait_ge(counted, b)
                dve.tensor_tensor(rank[:, :, :], rps[0:HT, 0:2 * E0].rearrange("p (t e) -> p t e", t=2),
                                  fill_row[0:HT, :].unsqueeze(1).broadcast_to([HT, 2, E0]), ALU.add).then_inc(ranked, 1)
                dve.wait_ge(ranked, b + 1)
                dve.tensor_tensor(rank[:, :, :], rank[:, :, :], hot[:, :, :], ALU.mult).then_inc(masked, 1)
                dve.tensor_tensor(fill_row[:, :], rps[:, 2 * E0:3 * E0], fill_row[:, :], ALU.add).then_inc(counted, 1)
                dve.wait_ge(masked, b + 1)
                dve.tensor_reduce(row[:, :], rank[:, :, :], AX.X, ALU.add).then_inc(rowed, 1)
                dve.wait_ge(rowed, b + 1)
                dve.tensor_copy(rows[:, bass.ds(2 * b, 2)], row[:, :])
                dve.tensor_copy(rowi[:, slot, :], row[:, :]).then_inc(row_set, 1)

            steps = [0]

            def then(ins):
                steps[0] += 1
                ins.then_inc(chain, 1)
                dve.wait_ge(chain, steps[0])

            dve.wait_ge(gate_in, 48)
            dve.memset(zero[:, :], 0.0).then_inc(zeroed, 1)
            then(dve.tensor_copy(fill_row[:, :], tcst[:, C_BASE0:C_BASE0 + E0]))
            statistics(0)
            norm(0, 0, None)
            statistics(1)
            for b in range(SLOTS):
                norm(b + 1, (b + 1) % SLOTS, 1 if b == SLOTS - 1 else None)
                choose(b)
                statistics(b + 2)
                place(b, b)
            with dve.Fori(1, B // SLOTS - 1) as i:
                for q in range(SLOTS):
                    b = SLOTS * i + q
                    norm(b + 1, (q + 1) % SLOTS, i + (q == SLOTS - 1))
                    choose(b)
                    statistics(b + 2)
                    place(b, q)
            for q in range(SLOTS):
                b = B - SLOTS + q
                if q < SLOTS - 1:
                    norm(b + 1, q + 1, B // SLOTS - 1)
                choose(b)
                if b + 2 < B:
                    statistics(b + 2)
                place(b, q)

            dve.wait_ge(counted, B)
            dve.tensor_copy(padi[:, :], fill_row[0:1, :]).then_inc(pad_set, 1)
            then(dve.tensor_tensor(padf[:, :], fill_row[:, :], tcst[:, C_BASE0:C_BASE0 + E0], ALU.subtract))
            then(dve.tensor_tensor(more[:, :, :], padf[:, :].unsqueeze(2).broadcast_to([128, E0, NT]),
                                   tcst[:, C_M128:C_M128 + NT].unsqueeze(1).broadcast_to([128, E0, NT]), ALU.is_gt))
            then(dve.tensor_reduce(ntile[:, :], more[:, :, :], AX.X, ALU.add))
            then(dve.tensor_tensor(tri[:, :, :], ntile[:, :].unsqueeze(1).broadcast_to([128, E0, E0]),
                                   tcst[:, C_TRI:C_TRI + E0 * E0].rearrange("p (a b) -> p a b", a=E0), ALU.mult))
            then(dve.tensor_reduce(tend[:, :], tri[:, :, :], AX.X, ALU.add))
            then(dve.tensor_tensor(shift[:, :], tend[:, :], ntile[:, :], ALU.subtract))
            then(dve.scalar_tensor_tensor(out=shift[:, :], in0=shift[:, :], scalar=128.0, in1=tcst[:, C_BASE0:C_BASE0 + E0],
                                          op0=ALU.mult, op1=ALU.subtract))
            then(dve.tensor_tensor(over[:, :, :], tcst[0:1, C_SEQ:C_SEQ + TILES0].unsqueeze(2).broadcast_to([1, TILES0, E0]),
                                   tend[0:1, :].unsqueeze(1).broadcast_to([1, TILES0, E0]), ALU.is_ge))
            then(dve.tensor_reduce(te[:, 0, :], over[:, :, :], AX.X, ALU.add))
            then(dve.tensor_scalar(te[:, 1, :], te[:, 0, :], float(E0 - 1), None, ALU.min))
            then(dve.tensor_tensor(over[:, :, :], te[:, 1, :].unsqueeze(2).broadcast_to([1, TILES0, E0]),
                                   cst[0:1, C_IOTA:C_IOTA + E0].unsqueeze(1).broadcast_to([1, TILES0, E0]), ALU.is_equal))
            then(dve.tensor_tensor(over[:, :, :], over[:, :, :], shift[0:1, :].unsqueeze(1).broadcast_to([1, TILES0, E0]), ALU.mult))
            then(dve.tensor_reduce(te[:, 2, :], over[:, :, :], AX.X, ALU.add))
            then(dve.scalar_tensor_tensor(out=te[:, 2, :], in0=tcst[0:1, C_SEQ:C_SEQ + TILES0], scalar=128.0, in1=te[:, 2, :],
                                          op0=ALU.mult, op1=ALU.subtract))
            then(dve.tensor_scalar(te[:, 2, :], te[:, 2, :], -float((E0 - 1) * XROWS), None, ALU.add))
            then(dve.tensor_scalar(tfirst[:, :], te[:, 0, :], float(E0 - 1), None, ALU.is_le))
            then(dve.tensor_tensor(te[:, 2, :], te[:, 2, :], tfirst[:, :], ALU.mult))
            then(dve.tensor_scalar(te[:, 2, :], te[:, 2, :], float((E0 - 1) * XROWS), None, ALU.add))
            dve.tensor_copy(tab[:, 0:TILES0], te[:, 1, :]).then_inc(tabled, 1)
            dve.tensor_copy(tab[:, TILES0:2 * TILES0], te[:, 2, :]).then_inc(tabled, 1)
            then(dve.tensor_tensor(hots[:, :, :], picks[:, :].unsqueeze(2).broadcast_to([HT, NT, E0]),
                                   cst[0:HT, C_IOTA:C_IOTA + E0].unsqueeze(1).broadcast_to([HT, NT, E0]), ALU.is_equal))
            then(dve.tensor_tensor(hots[:, :, :], hots[:, :, :], shift[0:HT, :].unsqueeze(1).broadcast_to([HT, NT, E0]), ALU.mult))
            then(dve.tensor_reduce(move[:, :], hots[:, :, :], AX.X, ALU.add))
            then(dve.tensor_tensor(move[:, :], move[:, :], rows[:, :], ALU.add))
            then(dve.tensor_copy(g.back[:, :], move[:, :]))

        @block.gpsimd
        def _(pool):
            def power(b):
                pool.wait_ge(ln_eps, b + 1)
                pool.tensor_tensor(rstd[:, :], rstd[:, :], g.mhalf[:, :], ALU.pow).then_inc(ln_pow, 1)

            def scatter(b, slot):
                pool.wait_ge(row_set, b + 1)
                pool.tensor_tensor(scrap[0:1, 4 + slot:5 + slot], scrap[0:1, 2:3], scrap[0:1, 3:4], ALU.add)
                for it in range(2):
                    pool.indirect_dma_start(xs[:, :], bass.IndirectOffsetOnAxis(ap=rowi[:, slot, it:it + 1], axis=0),
                                            xn[:, slot, it, :], None, bounds_check=E0 * XROWS - 1,
                                            oob_is_err=True).then_inc(scattered[slot], 16)

            pool.memset(scrap[0:1, 2:4], 0.0).then_inc(zeroed, 1)
            pool.wait_ge(zeroed, 2)
            power(0)
            power(1)
            with pool.Fori(0, B // SLOTS - 1) as i:
                for q in range(SLOTS):
                    power(SLOTS * i + q + 2)
                    scatter(SLOTS * i + q, q)
            for q in range(SLOTS):
                if q < SLOTS - 2:
                    power(B - SLOTS + q + 2)
                scatter(B - SLOTS + q, q)

        RING = 3
        xg = sb("b_xg", [128, RING, D])
        xgT = sb("b_xgT", [128, RING, D])
        pre = sb("b_pre", [128, RING, D])
        act1 = sb("b_act", [128, RING, D])
        aT = sb("b_aT", [128, RING, D])
        yo = sb("b_yo", [128, RING, D])
        pT = [tps, lps]
        pA, pB = rps, ps("b_pB")
        x_in = [sem(f"b_x_in{i}") for i in range(RING)]
        xgt_full, xgt_out, a_full, a_pre, a_act, at_full, at_out, y_full, y_set = (sem("b_" + n) for n in (
            "xgt_full", "xgt_out", "a_full", "a_pre", "a_act", "at_full", "at_out", "y_full", "y_set"))
        y_out = [sem(f"b_y_out{i}") for i in range(RING)]
        pxT = ps("b_pxT")
        paT = ps("b_paT")

        @block.sync
        def _(sp):
            sp.wait_ge(zeroed, 2)
            sp.wait_ge(pad_set, 1)
            for e in range(E0):
                at = sp.value_load(padi[0:1, e:e + 1], min_val=0, max_val=E0 * XROWS - 128)
                sp.dma_start(xs[bass.ds(at, 128), :], zero[:, 0:D]).then_inc(padded, 16)
            for s in range(SLOTS):
                sp.wait_ge(scattered[s], 32 * (B // SLOTS))
            sp.wait_ge(padded, 16 * E0)
            sp.wait_ge(tabled, 2)

            def load(s, r, i):
                if i is not None:
                    sp.wait_ge(xgt_full, s - RING + 1)
                first = sp.value_load(tab[0:1, bass.ds(s + TILES0, 1)], min_val=0, max_val=E0 * XROWS - 128)
                sp.dma_start(xg[:, r, :], xs[bass.ds(first, 128), :]).then_inc(x_in[r], 16)

            def store(s, r):
                sp.wait_ge(y_set, s + 1)
                sp.dma_start(ys[bass.ds(s * 128, 128), :], yo[:, r, :]).then_inc(y_out[r], 16)

            FILLS = E1 * CAP1 // (128 * ZROWS)

            def clear(n):
                rows = 128 * ZROWS
                sp.dma_start(xe[bass.ds(n * rows, rows), :].rearrange("(p a) d -> p (a d)", a=ZROWS),
                             zero[:, :]).then_inc(cleared, 16)

            for s in range(RING):
                load(s, s, None)
            load(RING, 0, 0)
            with sp.Fori(0, TILES0 // RING - 2) as i:
                for r in range(RING):
                    load(RING * i + RING + r + 1, (r + 1) % RING, i)
                    store(RING * i + r, r)
                clear(i)
            for n in range(TILES0 // RING - 2, FILLS):
                clear(n)
            for t in range(CAP1 // 128):
                sp.dma_start(out[OUTROWS - 128 * (t + 1):OUTROWS - 128 * t, :], zero[:, 0:D]).then_inc(cleared, 16)
            for s in range(TILES0 - 2 * RING, TILES0):
                if s + RING + 1 < TILES0:
                    load(s + RING + 1, (s + 1) % RING, 0)
                store(s, s % RING)
            for r in range(RING):
                sp.wait_ge(y_out[r], 16 * (TILES0 // RING))
            sp.wait_ge(cleared, 16 * (FILLS + CAP1 // 128))

        @block.tensor
        def _(pe):
            pe.wait_ge(tabled, 2)
            pe.wait_ge(counted, B)
            pe.wait_ge(w_in, W_IN)

            def turn_x(s, r, i):
                pe.wait_ge(x_in[r], 16 * i + 16)
                if not (isinstance(s, int) and s == 0):
                    pe.wait_ge(xgt_out, s)
                for c in range(DC):
                    mm = pe.transpose(pxT[:, 128 * c:128 * c + 128], xg[:, r, 128 * c:128 * c + 128], ident)
                mm.then_inc(xgt_full, 1)

            def expert(s):
                return pe.value_load(tab[0:1, bass.ds(s, 1)], min_val=0, max_val=E0 - 1)

            def up(s, r, e):
                pe.wait_ge(xgt_out, s + 1)
                pe.wait_ge(a_pre, s)
                for c in range(DC):
                    mm = pe.matmul(pA[:, 0:D], xgT[:, r, 128 * c:128 * c + 128],
                                   w1[:, bass.ds(e * (DC * D) + D * c, D)], start=(c == 0), stop=(c == DC - 1))
                mm.then_inc(a_full, 1)

            def turn_a(s, r):
                pe.wait_ge(a_act, s + 1)
                pe.wait_ge(at_out, s)
                for c in range(DC):
                    mm = pe.transpose(paT[:, 128 * c:128 * c + 128], act1[:, r, 128 * c:128 * c + 128], ident)
                mm.then_inc(at_full, 1)

            def down(s, r, e):
                pe.wait_ge(at_out, s + 1)
                pe.wait_ge(y_set, s)
                for c in range(DC):
                    mm = pe.matmul(pB[:, 0:D], aT[:, r, 128 * c:128 * c + 128],
                                   w2[:, bass.ds(e * (DC * D) + D * c, D)], start=(c == 0), stop=(c == DC - 1))
                mm.then_inc(y_full, 1)

            turn_x(0, 0, 0)
            turn_x(1, 1, 0)
            up(0, 0, expert(0))

            def steps(i):
                e = expert(RING * i)
                for r in range(RING):
                    s = RING * i + r
                    e_next = expert(s + 1)
                    turn_a(s, r)
                    up(s + 1, (r + 1) % RING, e_next)
                    turn_x(s + 2, (r + 2) % RING, i + (r + 2) // RING)
                    down(s, r, e)
                    e = e_next

            steps(0)
            with pe.Fori(1, TILES0 // RING - 1) as i:
                steps(i)
            e = expert(TILES0 - RING)
            for r in range(RING):
                s = TILES0 - RING + r
                e_next = expert(s + 1) if r < RING - 1 else None
                turn_a(s, r)
                if r < RING - 1:
                    up(s + 1, r + 1, e_next)
                if r == 0:
                    turn_x(s + 2, 2, TILES0 // RING - 1)
                down(s, r, e)
                e = e_next

        @block.scalar
        def _(act):
            def xT_out(s, r):
                act.wait_ge(xgt_full, s + 1)
                act.copy(xgT[:, r, :], pxT[:, 0:D]).then_inc(xgt_out, 1)

            def gelu(s, r):
                act.wait_ge(a_pre, s + 1)
                act.activation(act1[:, r, :], pre[:, r, :], ACT.Gelu).then_inc(a_act, 1)

            def aT_out(s, r):
                act.wait_ge(at_full, s + 1)
                act.copy(aT[:, r, :], paT[:, 0:D]).then_inc(at_out, 1)

            xT_out(0, 0)
            xT_out(1, 1)
            gelu(0, 0)
            with act.Fori(0, TILES0 // RING - 1) as i:
                for r in range(RING):
                    s = RING * i + r
                    aT_out(s, r)
                    gelu(s + 1, (r + 1) % RING)
                    xT_out(s + 2, (r + 2) % RING)
            for r in range(RING):
                s = TILES0 - RING + r
                aT_out(s, r)
                if r < RING - 1:
                    gelu(s + 1, r + 1)
                if r == 0:
                    xT_out(s + 2, 2)

        @block.vector
        def _(dve):
            dve.wait_ge(tabled, 2)
            dve.wait_ge(w_in, W_IN)

            def expert(s):
                return dve.value_load(tab[0:1, bass.ds(s, 1)], min_val=0, max_val=E0 - 1)

            def bias1(s, r, e):
                dve.wait_ge(a_full, s + 1)
                dve.tensor_tensor(pre[:, r, :], pA[:, 0:D], b1[:, bass.ds(e * D, D)], ALU.add).then_inc(a_pre, 1)

            def bias2(s, r, i, e):
                dve.wait_ge(y_out[r], 16 * i)
                dve.wait_ge(y_full, s + 1)
                dve.tensor_tensor(yo[:, r, :], pB[:, 0:D], b2[:, bass.ds(e * D, D)], ALU.add).then_inc(y_set, 1)

            bias1(0, 0, expert(0))

            def steps(i):
                e = expert(RING * i)
                for r in range(RING):
                    s = RING * i + r
                    e_next = expert(s + 1)
                    bias1(s + 1, (r + 1) % RING, e_next)
                    bias2(s, r, i, e)
                    e = e_next

            steps(0)
            with dve.Fori(1, TILES0 // RING - 1) as i:
                steps(i)
            e = expert(TILES0 - RING)
            for r in range(RING):
                s = TILES0 - RING + r
                if r < RING - 1:
                    e_next = expert(s + 1)
                    bias1(s + 1, r + 1, e_next)
                bias2(s, r, TILES0 // RING - 1, e)
                e = e_next
def stage_attention1(nc, g, w, ys, xe):
    ctx = ExitStack()
    with ctx:
        def sb(name, shape, dt=F32):
            return ctx.enter_context(nc.sbuf_tensor("c_" + name, shape, dt))

        def ps(name):
            return ctx.enter_context(nc.psum_tensor("c_" + name, [128, 512], F32))

        taken = []

        def sem(name):
            taken.append(ctx.enter_context(nc.semaphore(name)))
            return taken[-1]

        def sems(names):
            return [sem("c_" + n) for n in names.split()]

        h, cst = g.h, g.cst
        dcst = sb("dcst", [HT, C_END2])
        ident = cst[:, C_ID:C_ID + 128]
        E, K, CAP = E1, TOPK, CAP1

        wraw = sb("wraw", [128, 4, DC, D])
        wT = sb("wT", [128, 4, DC, D])
        graw = sb("graw", [E, D])
        gT = sb("gT", [128, DC, E])
        wd = sb("wd", [128, DC])
        nbd = sb("nbd", [HT, 1])
        oscale = sb("oscale", [HT, 1])

        idx = sb("idx", [HT, 2, 2], U32)
        yg = sb("yg", [HT, 2, 2, D])
        stats = sb("stats", [HT, 2, 2, 6])
        mv = sb("mv", [HT, 2, 2, 2])
        rstd = sb("rstd", [HT, 2, 2])
        xn = sb("xn", [HT, 2, D])
        xT = sb("xT", [128, DC, N])
        qT = sb("qT", [128, DC, N])
        kT = sb("kT", [128, DC, N])
        v = sb("v", [HT, 2, D])
        dec = sb("dec", [HT, 4, 2])
        wgt = sb("wgt", [HT, 3 * HT])
        wgm = sb("wgm", [HT, 3 * HT])
        sc = sb("sc", [HT, 3 * HT])
        rT = sb("rT", [128, DC, N])
        xr = sb("xr", [HT, 2, 2, ROW])
        xTr = sb("xTr", [128, DC, N])
        lg = sb("lg", [HT, 2, E])
        top = sb("top", [HT, 2, 8])
        topi = sb("topi", [HT, 2, 8], U32)
        nmax = sb("nmax", [HT, 2])
        e4 = sb("e4", [HT, 2, K])
        esum = sb("esum", [HT, 2])
        einv = sb("einv", [HT, 2])
        pick = sb("pick", [HT, 2, K])
        hot = sb("hot", [HT, 2 * K, E], BF16)
        hots = sb("hots", [HT, 2, E], BF16)
        rank = sb("rank", [HT, 2, E])
        run = sb("run", [HT, E])
        spread = sb("spread", [HT, 2, K, E])
        slot = sb("slot", [HT, 2, K])
        lost = sb("lost", [HT, 2, K])
        row = sb("row", [HT, 2, K])
        rowi = sb("rowi", [HT, 2, 2, K], U32)
        scrap = sb("scrap", [1, 16])

        pT, pq, pk, pv, psc, pr, po, psm = (ps(n) for n in ("pT", "pq", "pk", "pv", "psc", "pr", "po", "psm"))

        loaded, turned, turned_out, zeroed = sems("loaded turned turned_out zeroed")
        fetched = sems("fetched0 fetched1")
        idx_set, y_added, stat3, mv3, eps3, pow3, norm3 = sems("idx_set y_added stat3 mv3 eps3 pow3 norm3")
        t3_full, t3_out, q_full, q_out, k_full, k_out, v_full, v_out = sems(
            "t3_full t3_out q_full q_out k_full k_out v_full v_out")
        dec_exp, dec1, dec_set, ln_set, wgt_set, wgm_set = sems("dec_exp dec1 dec_set ln_set wgt_set wgm_set")
        dec2, dec_full = sems("dec2 dec_full")
        s_full, s_out, r_full, r_out, o_full, o_added = sems("s_full s_out r_full r_out o_full o_added")
        stat4, mv4, eps4, pow4, norm4, t4_full, t4_out, t4_kept = sems("stat4 mv4 eps4 pow4 norm4 t4_full t4_out t4_kept")
        l_full, choosing, nmax_set, e4_set, hots_set = sems(
            "l_full choosing nmax_set e4_set hots_set")
        rank_full, placing, run_set = sems(
            "rank_full placing run_set")
        rowi_set = sem("c_rowi_set")
        scattered = sems("scattered0 scattered1")

        
        assert not used_before(nc, taken)
        g.ffn1_sems = {name: g.sem("d_" + name) for name in FFN1_SEMS.split()}
        loads = [(wraw[:, n, :, :], w[name].rearrange("(c p) d -> p c d", p=128))
                 for n, name in enumerate(("L1_attn_Wq", "L1_attn_Wk", "L1_attn_Wv", "L1_attn_Wo"))]
        loads += [(dcst[:, :], w["decay_consts"]), (graw[:, :], w["L1_ffn_gate_w"]),
                  (nbd[:, :], w["L1_attn_bd"].rearrange("(a d) -> a d", a=1).broadcast_to([HT, 1])),
                  (oscale[:, :], w["L1_attn_out_scale"].rearrange("(a d) -> a d", a=1).broadcast_to([HT, 1]))]
        LOADED = 16 * (len(loads) + 1)
        block = ctx.enter_context(nc.Block())

        class At:

            def __init__(self, k, par, half=None):
                self.k, self.par = k, par
                self.half = k // 2 if half is None else half
                known = isinstance(k, int)
                self.now = not known or 0 <= k < B
                self.next = not known or 0 <= k + 1 < B
                self.soon = not known or 0 <= k + 2 < B
                self.later = not known or 0 <= k + 3 < B
                self.gone = not known or 0 <= k - 2 < B
                self.past = not known or 0 <= k - 1 < B

        def run_steps(eng, body):
            for k in range(-3, 4):
                body(At(k, k % 2))
            with eng.Fori(2, B // 2 - 2) as i:
                for par in range(2):
                    body(At(2 * i + par, par, i))
            for k in range(B - 4, B + 2):
                body(At(k, k % 2))

        @block.sync
        def _(sp):
            for dst, src in loads:
                sp.dma_start(dst, src).then_inc(loaded, 16)
            for s in g.ffn1_sems.values():
                sp.sem_clear(s)
            with nc.allow_non_contiguous_dma(reason="256 numbers, once"):
                sp.dma_start(wd[:, :], w["L1_attn_Wd"].rearrange("a (c p) -> p (a c)", p=128)).then_inc(loaded, 16)


        @block.tensor
        def _(pe):
            pe.wait_ge(loaded, LOADED)
            for n, bank in enumerate((pq, pk, pv, po)):
                for c in range(DC):
                    for r in range(DC):
                        mm = pe.transpose(bank[:, D * c + 128 * r:D * c + 128 * r + 128],
                                          wraw[:, n, r, 128 * c:128 * c + 128], ident)
                mm.then_inc(turned, 1)
            for c in range(DC):
                mm = pe.transpose(psm[:, E * c:E * c + E], graw[:, 128 * c:128 * c + 128], ident[0:E, 0:E])
            mm.then_inc(turned, 1)
            pe.wait_ge(turned_out, 6)

            def turn(dst_full, src):
                for c in range(DC):
                    for it in range(2):
                        mm = pe.transpose(pT[:, N * c + HT * it:N * c + HT * it + HT],
                                          src[:, it, 128 * c:128 * c + 128], ident[0:HT, 0:HT])
                mm.then_inc(dst_full, 1)

            def project(bank, n):
                for a in range(DC):
                    for c in range(DC):
                        mm = pe.matmul(bank[:, N * a:N * a + N], wT[:, n, c, 128 * a:128 * a + 128], xT[:, c, :],
                                       start=(c == 0), stop=(c == DC - 1))
                return mm

            def step(s):
                k = s.k
                if s.now:
                    pe.wait_ge(s_out, k + 1)
                    pe.wait_ge(v_out, k + 1)
                    for a in range(DC):
                        pe.matmul(pr[:, N * a:N * a + N], v[:, 1, 128 * a:128 * a + 128], sc[:, HT:3 * HT],
                                  start=True, stop=False)
                        mm = pe.matmul(pr[:, N * a:N * a + HT], v[:, 0, 128 * a:128 * a + 128], sc[:, 0:HT],
                                       start=False, stop=True)
                    mm.then_inc(r_full, 1)
                if s.next:
                    pe.wait_ge(t3_out, k + 2)
                    wait_for(pe, k_out, k + 1)
                    for it in range(2):
                        for c in range(DC):
                            mm = pe.matmul(pk[0:HT, 2 * N + it:2 * N + it + 1], xT[:, c, HT * it:HT * it + HT],
                                           wd[:, c:c + 1], start=(c == 0), stop=(c == DC - 1))
                    mm.then_inc(dec_full, 1)
                if s.past:
                    pe.wait_ge(norm4, k)
                    if not s.next:
                        pe.wait_ge(t4_kept, k - 1)
                    turn(t4_full, xr[:, 1 - s.par, :, 0:D])
                if s.next:
                    project(pq, 0).then_inc(q_full, 1)
                if s.now:
                    pe.wait_ge(r_out, k + 1)
                    wait_for(pe, o_added, k)
                    for it in range(2):
                        for c in range(DC):
                            mm = pe.matmul(po[0:HT, D * it:D * it + D], rT[:, c, HT * it:HT * it + HT], wT[:, 3, c, :],
                                           start=(c == 0), stop=(c == DC - 1))
                    mm.then_inc(o_full, 1)
                if s.past:
                    pe.wait_ge(t4_out, k)
                    pe.wait_ge(run_set, k)
                    for it in range(2):
                        for c in range(DC):
                            mm = pe.matmul(psm[0:HT, E * it:E * it + E], xTr[:, c, HT * it:HT * it + HT], gT[:, c, :],
                                           start=(c == 0), stop=(c == DC - 1))
                    mm.then_inc(l_full, 1)
                if s.next:
                    pe.wait_ge(dec_exp, k + 2)
                    project(pk, 1).then_inc(k_full, 1)
                    wait_for(pe, v_out, k + 1)
                    for it in range(2):
                        for c in range(DC):
                            mm = pe.matmul(pv[0:HT, D * it:D * it + D], xT[:, c, HT * it:HT * it + HT], wT[:, 2, c, :],
                                           start=(c == 0), stop=(c == DC - 1))
                    mm.then_inc(v_full, 1)
                if s.past:
                    pe.wait_ge(hots_set, k)
                    pe.matmul(psm[0:HT, 0:E], g.upb[:, :], hots[:, 0, :], start=True, stop=True)
                    pe.matmul(psm[0:HT, E:2 * E], g.upb[:, :], hots[:, 1, :], start=True, stop=False)
                    pe.matmul(psm[0:HT, E:2 * E], g.onesb[:, 0:HT], hots[:, 0, :], start=False, stop=True)
                    pe.matmul(psm[0:HT, 2 * E:3 * E], g.onesb[:, 0:HT], hots[:, 0, :], start=True, stop=False)
                    pe.matmul(psm[0:HT, 2 * E:3 * E], g.onesb[:, 0:HT], hots[:, 1, :], start=False, stop=True).then_inc(rank_full, 1)
                if s.soon:
                    pe.wait_ge(norm3, k + 3)
                    if s.past:
                        pe.wait_ge(t4_kept, k)
                    elif k > -2:
                        pe.wait_ge(t3_out, k + 2)
                    turn(t3_full, xn)
                if s.next:
                    pe.wait_ge(q_out, k + 2)
                    pe.wait_ge(k_out, k + 2)
                    wait_for(pe, s_out, k + 1)
                    for st in range(2):
                        for c in range(DC):
                            mm = pe.matmul(psc[0:HT, HT * st:HT * st + HT * (st + 1)], kT[:, c, HT * st:HT * st + HT],
                                           qT[:, c, 0:HT * (st + 1)], start=(c == 0), stop=(c == DC - 1))
                    mm.then_inc(s_full, 1)

            run_steps(pe, step)

        @block.scalar
        def _(act):
            for n, bank in enumerate((pq, pk, pv, po)):
                act.wait_ge(turned, n + 1)
                act.copy(wT[:, n, :, :], bank[:, :].rearrange("p (c e) -> p c e", c=DC)).then_inc(turned_out, 1)
            act.wait_ge(turned, 5)
            act.copy(gT[:, :, :], psm[:, 0:DC * E].rearrange("p (c e) -> p c e", c=DC)).then_inc(turned_out, 1)
            act.mul(nbd[:, :], nbd[:, :], -1.0).then_inc(turned_out, 1)

            def halves(bank):
                return bank[:, 0:2 * N].rearrange("p (c n) -> p c n", c=DC)

            def step(s):
                k = s.k
                if s.now:
                    act.wait_ge(r_full, k + 1)
                    act.copy(rT[:, :, :], halves(pr)).then_inc(r_out, 1)
                if s.next:
                    act.wait_ge(dec_full, k + 2)
                    act.activation(dec[:, 0, :], pk[0:HT, 2 * N:2 * N + 2], ACT.Exp, bias=nbd[:, 0:1], scale=-1.0).then_inc(dec_exp, 1)
                if s.past:
                    act.wait_ge(t4_full, k)
                    act.copy(xTr[:, :, :], halves(pT)).then_inc(t4_out, 1)
                    act.copy(g.xTs[:, :, bass.ds(N * k - N, N)], halves(pT)).then_inc(t4_kept, 1)
                if s.next:
                    act.wait_ge(q_full, k + 2)
                    act.copy(qT[:, :, :], halves(pq)).then_inc(q_out, 1)
                    act.wait_ge(dec_set, k + 2)
                    act.activation(dec[:, 3, :], dec[:, 2, :], ACT.Ln).then_inc(ln_set, 1)
                    act.wait_ge(ln_set, k + 2)
                    if s.now:
                        act.wait_ge(wgm_set, k + 1)
                    for st in range(2):
                        e = act.activation(wgt[:, HT * st:HT * st + HT * (st + 1)],
                                           dcst[:, C_DIST + HT * st:C_DIST + HT * st + HT * (st + 1)], ACT.Exp,
                                           scale=dec[:, 3, st:st + 1])
                    e.then_inc(wgt_set, 1)
                    act.wait_ge(k_full, k + 2)
                    act.copy(kT[:, :, :], halves(pk)).then_inc(k_out, 1)
                if s.past:
                    act.wait_ge(nmax_set, k)
                    for it in range(2):
                        e = act.activation(e4[:, it, :], top[:, it, 0:K], ACT.Exp, bias=nmax[:, it:it + 1],
                                           accum_out=esum[:, it:it + 1])
                    e.then_inc(e4_set, 1)
                if s.next:
                    act.wait_ge(v_full, k + 2)
                    act.copy(v[:, :, :], pv[0:HT, :].rearrange("p (t d) -> p t d", t=2)).then_inc(v_out, 1)
                if s.soon:
                    act.wait_ge(t3_full, k + 3)
                    act.copy(xT[:, :, :], halves(pT)).then_inc(t3_out, 1)

            run_steps(act, step)

        @block.vector
        def _(dve):
            def settle(s, n):
                dve.wait_ge(s, n)
                dve.memset(scrap[0:1, 0:1], 0.0)

            def h_tile(b, it=None):
                if it is None:
                    return h[:, bass.ds(b * (2 * D), 2 * D)]
                return h[:, bass.ds(b * (2 * D) + D * it, D)]

            def statistics(b, n, added, stat, aggregated, eps):
                settle(added, b + 1)
                for it in range(2):
                    dve.bn_stats(stats[:, n, it, :], h_tile(b, it)).then_inc(stat, 1)
                settle(stat, 2 * b + 2)
                for it in range(2):
                    dve.bn_aggr(mv[:, n, it, :], stats[:, n, it, :]).then_inc(aggregated, 1)
                dve.wait_ge(aggregated, 2 * b + 2)
                dve.tensor_scalar(rstd[:, n, :], mv[:, n, :, 1], EPS, None, ALU.add).then_inc(eps, 1)

            def scale(b, n, power, dst, done):
                dve.wait_ge(power, b + 1)
                for it in range(2):
                    e = dve.tensor_scalar(dst[:, it, :], h_tile(b, it), mv[:, n, it, 0:1], rstd[:, n, it:it + 1],
                                          ALU.subtract, ALU.mult)
                e.then_inc(done, 1)

            def wide(ap, n):
                return ap.unsqueeze(2).broadcast_to([HT, ap.shape[1], n])

            dve.memset(run[:, :], 0.0).then_inc(run_set, 1)
            for par in range(2):
                for it in range(2):
                    dve.tensor_scalar(xr[:, par, it, ROW - 1:ROW], cst[0:HT, C_PART:C_PART + 1],
                                      float(1 + HT * it + N * par - 2 * N), None, ALU.add)
            dve.wait_ge(loaded, LOADED)

            def step(s):
                k = s.k
                if s.now:
                    dve.wait_ge(wgm_set, k + 1)
                    dve.wait_ge(s_full, k + 1)
                    dve.tensor_tensor(sc[:, :], psc[0:HT, 0:3 * HT], wgm[:, :], ALU.mult).then_inc(s_out, 1)
                if s.past:
                    if not isinstance(k, int) or k >= 3:
                        dve.wait_ge(scattered[1 - s.par], 16 * 2 * K * (s.half - (1 - s.par)))
                    scale(k - 1, 1, pow4, xr[:, 1 - s.par, :, 0:D], norm4)
                if s.soon:
                    wait_for(dve, t3_full, k + 2)
                    scale(k + 2, 0, pow3, xn, norm3)
                if s.later:
                    b = k + 3
                    dve.wait_ge(fetched[1 - s.par], 32 * (s.half + 2 + s.par))
                    dve.tensor_tensor(h_tile(b), h_tile(b), yg[:, 1 - s.par, :, :].rearrange("p t d -> p (t d)"), ALU.add).then_inc(y_added, 1)
                    statistics(b, 0, y_added, stat3, mv3, eps3)
                if s.next:
                    dve.wait_ge(dec_exp, k + 2)
                    dve.tensor_scalar(dec[:, 1, :], dec[:, 0, :], 1.0, None, ALU.add).then_inc(dec1, 1)
                    dve.wait_ge(dec1, k + 2)
                    dve.reciprocal(dec[:, 1, :], dec[:, 1, :]).then_inc(dec2, 1)
                    dve.wait_ge(dec2, k + 2)
                    dve.tensor_scalar(dec[:, 2, :], dec[:, 1, :], 1e-8, None, ALU.add).then_inc(dec_set, 1)
                if s.now:
                    dve.wait_ge(o_full, k + 1)
                    dve.scalar_tensor_tensor(out=h_tile(k), in0=po[0:HT, :], scalar=oscale[:, 0:1], in1=h_tile(k),
                                             op0=ALU.mult, op1=ALU.add).then_inc(o_added, 1)
                    statistics(k, 1, o_added, stat4, mv4, eps4)
                if s.past:
                    dve.wait_ge(l_full, k)
                    dve.tensor_copy(lg[:, :, :], psm[0:HT, 0:2 * E].rearrange("p (t e) -> p t e", t=2)).then_inc(choosing, 1)
                    settle(choosing, 7 * k - 6)
                    for it in range(2):
                        dve.max(top[:, it, :], lg[:, it, :]).then_inc(choosing, 1)
                    dve.wait_ge(choosing, 7 * k - 4)
                    dve.tensor_scalar(nmax[:, :], top[:, :, 0], -1.0, None, ALU.mult).then_inc(nmax_set, 1)
                    for it in range(2):
                        dve.max_index(topi[:, it, :], top[:, it, :], lg[:, it, :]).then_inc(choosing, 1)
                    dve.wait_ge(choosing, 7 * k - 2)
                    dve.tensor_copy(pick[:, :, :], topi[:, :, 0:K]).then_inc(choosing, 1)
                    dve.wait_ge(choosing, 7 * k - 1)
                    dve.tensor_tensor(hot[:, :, :], wide(pick[:, :, :].rearrange("p t k -> p (t k)"), E),
                                      cst[0:HT, C_IOTA:C_IOTA + E].unsqueeze(1).broadcast_to([HT, 2 * K, E]),
                                      ALU.is_equal).then_inc(choosing, 1)
                    dve.wait_ge(choosing, 7 * k)
                    with nc.allow_low_precision(reason="a sum of 0 and 1 that is at most 1"):
                        dve.tensor_reduce(hots[:, :, :], hot[:, :, :].rearrange("p (t k) e -> p t e k", k=K), AX.X,
                                          ALU.add).then_inc(hots_set, 1)
                if s.next:
                    dve.wait_ge(wgt_set, k + 2)
                    dve.tensor_tensor(wgm[:, :], wgt[:, :], dcst[:, C_LATER:C_LATER + 3 * HT], ALU.mult).then_inc(wgm_set, 1)
                if s.past:
                    dve.wait_ge(rank_full, k)
                    dve.wait_ge(run_set, k)
                    dve.tensor_tensor(rank[:, :, :], psm[0:HT, 0:2 * E].rearrange("p (t e) -> p t e", t=2),
                                      run[:, :].unsqueeze(1).broadcast_to([HT, 2, E]), ALU.add).then_inc(placing, 1)
                    dve.wait_ge(placing, 7 * k - 6)
                    dve.tensor_tensor(spread[:, :, :, :], hot[:, :, :].rearrange("p (t k) e -> p t k e", k=K),
                                      rank[:, :, :].unsqueeze(2).broadcast_to([HT, 2, K, E]), ALU.mult).then_inc(placing, 1)
                    dve.tensor_tensor(run[:, :], psm[0:HT, 2 * E:3 * E], run[:, :], ALU.add).then_inc(run_set, 1)
                    dve.wait_ge(placing, 7 * k - 5)
                    dve.tensor_reduce(slot[:, :, :], spread[:, :, :, :], AX.X, ALU.add).then_inc(placing, 1)
                    dve.wait_ge(placing, 7 * k - 4)
                    dve.tensor_scalar(lost[:, :, :], slot[:, :, :], float(CAP), float(2 * E * CAP), ALU.is_ge, ALU.mult).then_inc(placing, 1)
                    dve.scalar_tensor_tensor(out=row[:, :, :], in0=pick[:, :, :], scalar=float(CAP), in1=slot[:, :, :],
                                             op0=ALU.mult, op1=ALU.add).then_inc(placing, 1)
                    dve.wait_ge(placing, 7 * k - 2)
                    dve.tensor_tensor(row[:, :, :], row[:, :, :], lost[:, :, :], ALU.add).then_inc(placing, 1)
                    tag = xr[:, 1 - s.par, :, D:ROW]
                    dve.tensor_copy(tag[:, :, K:2 * K], pick[:, :, :]).then_inc(rowi_set, 1)
                    dve.tensor_scalar(tag[:, :, 2 * K], tag[:, :, 2 * K], float(2 * N), None, ALU.add).then_inc(rowi_set, 1)
                    dve.wait_ge(placing, 7 * k - 1)
                    dve.tensor_copy(rowi[:, 1 - s.par, :, :], row[:, :, :]).then_inc(rowi_set, 1)
                    dve.wait_ge(e4_set, k)
                    dve.reciprocal(einv[:, :], esum[:, :]).then_inc(placing, 1)
                    dve.wait_ge(placing, 7 * k)
                    dve.tensor_tensor(tag[:, :, 0:K], e4[:, :, :], wide(einv[:, :], K), ALU.mult).then_inc(rowi_set, 1)

            run_steps(dve, step)

        @block.gpsimd
        def _(pool):
            def fetch(b, par):
                if isinstance(b, int):
                    if b >= 2:
                        pool.wait_ge(y_added, b - 1)
                else:
                    pool.wait_ge(y_added, b - 1)
                pool.tensor_copy(idx[:, par, :], g.back[:, bass.ds(2 * b, 2)]).then_inc(idx_set, 1)
                pool.wait_ge(idx_set, b + 1)
                pool.tensor_tensor(scrap[0:1, 4 + par:5 + par], scrap[0:1, 2:3], scrap[0:1, 3:4], ALU.add)
                for it in range(2):
                    pool.indirect_dma_start(yg[:, par, it, :], None, ys[:, :],
                                            bass.IndirectOffsetOnAxis(ap=idx[:, par, it:it + 1], axis=0),
                                            bounds_check=128 * TILES0 - 1, oob_is_err=True).then_inc(fetched[par], 16)

            def power(n, eps, done, b):
                pool.wait_ge(eps, b + 1)
                pool.tensor_tensor(rstd[:, n, :], rstd[:, n, :], g.mhalf[:, :], ALU.pow).then_inc(done, 1)

            def scatter(par, it):
                for c in range(K):
                    pool.indirect_dma_start(xe[:, :], bass.IndirectOffsetOnAxis(ap=rowi[:, par, it, c:c + 1], axis=0),
                                            xr[:, par, it, :], None, bounds_check=E * CAP - 1,
                                            oob_is_err=False).then_inc(scattered[par], 16)

            pool.memset(scrap[0:1, 2:4], 0.0).then_inc(zeroed, 1)
            pool.wait_ge(zeroed, 1)
            fetch(0, 0)

            def step(s):
                k = s.k
                if s.gone:
                    pool.wait_ge(rowi_set, 4 * k - 4)
                    pool.tensor_tensor(scrap[0:1, 6 + s.par:7 + s.par], scrap[0:1, 2:3], scrap[0:1, 3:4], ALU.add)
                    scatter(s.par, 0)
                    scatter(s.par, 1)
                if s.later:
                    power(0, eps3, pow3, k + 3)
                if s.now:
                    power(1, eps4, pow4, k)
                if not isinstance(k, int) or k + 4 < B:
                    fetch(k + 4, s.par)

            run_steps(pool, step)
            for par in range(2):
                pool.wait_ge(scattered[par], 16 * 2 * K * (B // 2))
FFN1_SEMS = """sw_in sgu_full sgs_set sa_set sdn_full sh_added x_in0 x_in1
x_in2 x_in3 w_in0 w_in1 w_in2 w_in3 added0 added1
t_full t_out gu_full gs_set a_set dn_full y_set
weighing weighed placed marked zeroed base_out dumps_set"""


def stage_ffn1(nc, g, w, xe, out):
    ctx = ExitStack()
    with ctx:
        def sb(name, shape, dt=F32):
            return ctx.enter_context(nc.sbuf_tensor("d_" + name, shape, dt))

        def ps(name):
            return ctx.enter_context(nc.psum_tensor("d_" + name, [128, 512], F32))

        def sems(names):
            return [g.ffn1_sems[n] for n in names.split()]

        h, cst = g.h, g.cst
        ident = cst[:, C_ID:C_ID + 128]
        E, K, CAP = E1, TOPK, CAP1
        RING = 4
        AHEAD = RING - 1
        CT = CAP // 128

        swg = sb("swg", [128, DC, 2 * I1])
        swd = sb("swd", [I1, D])
        gs = sb("gs", [128, 2, CAP])
        a = sb("a", [128, 2, CAP])
        x = sb("x", [128, RING, CT, ROW])
        wgu = sb("wgu", [128, RING, DC, 2 * I1])
        wdn = sb("wdn", [I1, RING, D])
        xT = sb("xT", [128, 2, DC, CAP])
        yo = sb("yo", [128, 2, CT, D])
        hit = sb("hit", [128, 2, CT, K])
        part = sb("part", [128, 2, CT, K])
        dump = sb("dump", [128, CT])
        free = sb("free", [128, 2, CT])
        gate = sb("gate", [128, RING, CT])
        dest = sb("dest", [128, RING, CT], U32)
        scrap = sb("scrap", [1, 8])
        pT, pgu, pdn = [ps("pT0"), ps("pT1")], [ps("pgu0"), ps("pgu1")], [ps("pdn0"), ps("pdn1")]

        sw_in, = sems("sw_in")
        sgu_full, sgs_set, sa_set, sdn_full, sh_added = sems("sgu_full sgs_set sa_set sdn_full sh_added")
        x_in = sems("x_in0 x_in1 x_in2 x_in3")
        w_in = sems("w_in0 w_in1 w_in2 w_in3")
        added = sems("added0 added1")
        t_full, t_out, gu_full, gs_set, a_set, dn_full, y_set = sems("t_full t_out gu_full gs_set a_set dn_full y_set")
        weighing, weighed, placed = sems("weighing weighed placed")
        marked, zeroed, base_out, dumps_set = sems("marked zeroed base_out dumps_set")
        block = ctx.enter_context(nc.Block())

        @block.sync
        def _(sp):
            sp.dma_start(swg[:, :, :], w["L1_ffn_shared_w_gate_up"].rearrange("(c p) i -> p c i", p=128)).then_inc(sw_in, 16)
            sp.dma_start(swd[:, :], w["L1_ffn_shared_w_down"]).then_inc(sw_in, 16)

            def load(e, r, first=False):
                if not first:
                    sp.wait_ge(t_full, e - RING + 1)
                    sp.wait_ge(weighed, e - RING + 1)
                    sp.wait_ge(placed, e - RING + 1)
                    sp.wait_ge(dn_full, e - RING + 1)
                sp.dma_start(x[:, r, :, :], xe[bass.ds(e * CAP, CAP), :].rearrange("(a p) d -> p a d", p=128)).then_inc(x_in[r], 16)
                sp.dma_start(wgu[:, r, :, :], w["L1_ffn_w_gate_up"][bass.ds(e, 1), :, :].rearrange(
                    "e (c p) i -> p (e c) i", p=128)).then_inc(w_in[r], 16)
                sp.dma_start(wdn[:, r, :], w["L1_ffn_w_down"][bass.ds(e, 1), :, :].rearrange("e i d -> (e i) d")).then_inc(w_in[r], 16)

            for e in range(RING):
                load(e, e, True)
            with sp.Fori(0, B) as b:
                sp.wait_ge(sh_added, b + 1)
                sp.dma_start(out[bass.ds(b * N + 1, N), :].rearrange("(t p) d -> p t d", t=2),
                             h[:, bass.ds(b * (2 * D), 2 * D)].rearrange("p (t d) -> p t d", t=2)).then_inc(base_out, 16)
            with sp.Fori(1, E // RING) as i:
                for r in range(RING):
                    load(RING * i + r, r)
            for r in range(2):
                sp.wait_ge(added[r], 16 * CT * E // 2)

        @block.tensor
        def _(pe):
            pe.wait_ge(sw_in, 32)

            def shared_up(b, par):
                pe.wait_ge(sa_set, b - 1)
                for n in range(2):
                    for c in range(DC):
                        mm = pe.matmul(pgu[par][:, N * n:N * n + N], swg[:, c, I1 * n:I1 * n + I1],
                                       g.xTs[:, c, bass.ds(b * N, N)], start=(c == 0), stop=(c == DC - 1))
                mm.then_inc(sgu_full, 1)

            def shared_down(b, par):
                pe.wait_ge(sa_set, b + 1)
                pe.wait_ge(sh_added, b - 1)
                for it in range(2):
                    mm = pe.matmul(pdn[par][0:HT, D * it:D * it + D], a[:, par, HT * it:HT * it + HT], swd[:, :],
                                   start=True, stop=True)
                mm.then_inc(sdn_full, 1)

            def first_up(b):
                for n in range(2):
                    for c in range(DC):
                        mm = pe.matmul(pgu[b][:, N * n:N * n + N], swg[:, c, I1 * n:I1 * n + I1],
                                       g.xTs[:, c, N * b:N * b + N], start=(c == 0), stop=(c == DC - 1))
                mm.then_inc(sgu_full, 1)

            def first_down(b):
                pe.wait_ge(sa_set, b + 1)
                for it in range(2):
                    mm = pe.matmul(pdn[b][0:HT, D * it:D * it + D], a[:, b, HT * it:HT * it + HT], swd[:, :],
                                   start=True, stop=True)
                mm.then_inc(sdn_full, 1)

            first_up(0)
            first_up(1)
            first_down(0)
            shared_up(2, 0)
            first_down(1)
            with pe.Fori(1, B // 2 - 1) as i:
                for par in range(2):
                    shared_up(2 * i + par + 1, 1 - par)
                    shared_down(2 * i + par, par)
            shared_up(B - 1, 1)
            shared_down(B - 2, 0)
            shared_down(B - 1, 1)
            pe.wait_ge(sa_set, B)
            pe.wait_ge(sh_added, B)

            def turn(e, r, i):
                pe.wait_ge(x_in[r], 16 * i + 16)
                pe.wait_ge(t_out, e - 1) if not isinstance(e, int) or e > 1 else None
                for c in range(DC):
                    for t in range(CT):
                        mm = pe.transpose(pT[r % 2][:, CAP * c + 128 * t:CAP * c + 128 * t + 128],
                                          x[:, r, t, 128 * c:128 * c + 128], ident)
                mm.then_inc(t_full, 1)

            def up(e, r, i):
                pe.wait_ge(w_in[r], 32 * i + 32)
                pe.wait_ge(t_out, e + 1)
                pe.wait_ge(a_set, e - 1) if not isinstance(e, int) or e > 1 else None
                for n in range(2):
                    for c in range(DC):
                        mm = pe.matmul(pgu[r % 2][:, CAP * n:CAP * n + CAP], wgu[:, r, c, I1 * n:I1 * n + I1],
                                       xT[:, r % 2, c, :], start=(c == 0), stop=(c == DC - 1))
                mm.then_inc(gu_full, 1)

            def down(e, r):
                pe.wait_ge(a_set, e + 1)
                pe.wait_ge(y_set, e - 1) if not isinstance(e, int) or e > 1 else None
                for t in range(CT):
                    mm = pe.matmul(pdn[r % 2][:, D * t:D * t + D], a[:, r % 2, 128 * t:128 * t + 128], wdn[:, r, :],
                                   start=True, stop=True)
                mm.then_inc(dn_full, 1)

            turn(0, 0, 0)
            turn(1, 1, 0)
            up(0, 0, 0)
            turn(2, 2, 0)
            up(1, 1, 0)
            down(0, 0)
            turn(3, 3, 0)
            up(2, 2, 0)
            down(1, 1)
            with pe.Fori(0, E // RING - 1) as i:
                for r in range(RING):
                    e = RING * i + r
                    turn(e + RING, r, i + 1)
                    up(e + 3, (r + 3) % RING, i + (r + 3) // RING)
                    down(e + 2, (r + 2) % RING)
            up(E - 1, RING - 1, E // RING - 1)
            down(E - 2, RING - 2)
            down(E - 1, RING - 1)

        @block.scalar
        def _(act):
            def shared_silu(b, par):
                act.wait_ge(sgu_full, b + 1)
                if not (isinstance(b, int) and b < 2):
                    act.wait_ge(sa_set, b - 1)
                act.activation(gs[:, par, 0:N], pgu[par][:, 0:N], ACT.Silu).then_inc(sgs_set, 1)

            shared_silu(0, 0)
            shared_silu(1, 1)
            with act.Fori(1, B // 2) as i:
                for par in range(2):
                    shared_silu(2 * i + par, par)
            act.wait_ge(sa_set, B)

            def turn_out(e, r):
                act.wait_ge(t_full, e + 1)
                if not (isinstance(e, int) and e < 2):
                    act.wait_ge(gu_full, e - 1)
                act.copy(xT[:, r % 2, :, :], pT[r % 2][:, :].rearrange("p (c n) -> p c n", c=DC)).then_inc(t_out, 1)

            def silu(e, r):
                act.wait_ge(gu_full, e + 1)
                if not (isinstance(e, int) and e < 2):
                    act.wait_ge(a_set, e - 1)
                act.activation(gs[:, r % 2, :], pgu[r % 2][:, 0:CAP], ACT.Silu).then_inc(gs_set, 1)

            turn_out(0, 0)
            turn_out(1, 1)
            silu(0, 0)
            turn_out(2, 0)
            silu(1, 1)
            turn_out(3, 1)
            silu(2, 0)
            with act.Fori(0, E // 2 - 2) as i:
                for r in range(2):
                    turn_out(2 * i + r + 4, r)
                    silu(2 * i + r + 3, 1 - r)
            silu(E - 1, 1)

        @block.vector
        def _(dve):
            for t in range(CT):
                dve.tensor_scalar(dump[:, t:t + 1], cst[:, C_PART:C_PART + 1], float(OUTROWS - CAP + 128 * t), None,
                                  ALU.add).then_inc(dumps_set, 1)

            def shared_product(b, par):
                dve.wait_ge(sgs_set, b + 1)
                if not (isinstance(b, int) and b < 2):
                    dve.wait_ge(sdn_full, b - 1)
                dve.tensor_tensor(a[:, par, 0:N], pgu[par][:, N:2 * N], gs[:, par, 0:N], ALU.mult).then_inc(sa_set, 1)

            def shared_add(b, par):
                dve.wait_ge(sdn_full, b + 1)
                hb = h[:, bass.ds(b * (2 * D), 2 * D)]
                dve.tensor_tensor(hb, pdn[par][0:HT, :], hb, ALU.add).then_inc(sh_added, 1)

            shared_product(0, 0)
            shared_product(1, 1)
            shared_add(0, 0)
            with dve.Fori(1, B // 2) as i:
                for par in range(2):
                    shared_product(2 * i + par, par)
                    shared_add(2 * i + par - 1, 1 - par)
            shared_add(B - 1, 1)
            dve.wait_ge(sdn_full, B)

            def weigh(e, r, i):
                p = r % 2
                tag = x[:, r, :, D:ROW]
                dve.wait_ge(x_in[r], 16 * i + 16)
                if not (isinstance(e, int) and e < 2):
                    dve.wait_ge(weighed, e - 1)
                    dve.wait_ge(placed, e - 1)
                dve.tensor_tensor(hit[:, p, :, :], tag[:, :, K:2 * K], cst[:, bass.ds(e + C_IOTA, 1)].unsqueeze(1).broadcast_to([128, CT, K]),
                                  ALU.is_equal).then_inc(weighing, 1)
                dve.scalar_tensor_tensor(out=free[:, p, :], in0=tag[:, :, 2 * K], scalar=0.0, in1=dump[:, :],
                                         op0=ALU.is_equal, op1=ALU.mult).then_inc(weighing, 1)
                dve.wait_ge(weighing, 3 * e + 1)
                dve.tensor_tensor(part[:, p, :, :], hit[:, p, :, :], tag[:, :, 0:K], ALU.mult).then_inc(weighing, 1)
                dve.wait_ge(weighing, 3 * e + 2)
                dve.tensor_tensor(dest[:, r, :], free[:, p, :], tag[:, :, 2 * K], ALU.add).then_inc(placed, 1)
                dve.wait_ge(weighing, 3 * e + 3)
                dve.tensor_reduce(gate[:, r, :], part[:, p, :, :], AX.X, ALU.add).then_inc(weighed, 1)

            def product(e, r):
                dve.wait_ge(gs_set, e + 1)
                if not (isinstance(e, int) and e < 2):
                    dve.wait_ge(dn_full, e - 1)
                dve.tensor_tensor(a[:, r % 2, :], pgu[r % 2][:, CAP:2 * CAP], gs[:, r % 2, :], ALU.mult).then_inc(a_set, 1)

            def result(e, r):
                dve.wait_ge(dn_full, e + 1)
                dve.wait_ge(weighed, e + 1)
                dve.wait_ge(placed, e + 1)
                if not (isinstance(e, int) and e < 2):
                    dve.wait_ge(added[r % 2], 8 * CT * (e - r % 2))
                dve.tensor_tensor(yo[:, r % 2, :, :], pdn[r % 2][:, :].rearrange("p (t d) -> p t d", t=CT),
                                  gate[:, r, :].unsqueeze(2).broadcast_to([128, CT, D]), ALU.mult).then_inc(y_set, 1)

            dve.wait_ge(dumps_set, CT)
            weigh(0, 0, 0)
            product(0, 0)

            def steps(i):
                for r in range(RING):
                    e, r1 = RING * i + r, (r + 1) % RING
                    last = isinstance(e, int) and e == E - 1
                    if not last:
                        weigh(e + 1, r1, i + (r + 1) // RING)
                        product(e + 1, r1)
                    result(e, r)

            steps(0)
            with dve.Fori(1, E // RING - 1) as i:
                steps(i)
            steps(E // RING - 1)

        @block.gpsimd
        def _(pool):
            pool.memset(scrap[0:1, 0:2], 0.0).then_inc(zeroed, 1)
            pool.wait_ge(zeroed, 1)
            pool.wait_ge(base_out, 16 * B)

            def scatter(e, r):
                pool.wait_ge(y_set, e + 1)
                if r % 2:
                    pool.wait_ge(added[0], 8 * CT * (e + 1))
                elif not (isinstance(e, int) and e == 0):
                    pool.wait_ge(added[1], 8 * CT * e)
                wait_for(pool, marked, e)
                pool.tensor_tensor(scrap[0:1, 4:5], scrap[0:1, 0:1], scrap[0:1, 1:2], ALU.add).then_inc(marked, 1)
                for t in range(CT):
                    pool.indirect_dma_start(out[:, :], bass.IndirectOffsetOnAxis(ap=dest[:, r, t:t + 1], axis=0),
                                            yo[:, r % 2, t, :], None, bounds_check=OUTROWS - 1, oob_is_err=True,
                                            compute_op=ALU.add).then_inc(added[r % 2], 16)

            for e in range(RING):
                scatter(e, e)
            with pool.Fori(1, E // RING) as i:
                for r in range(RING):
                    scatter(RING * i + r, r)

class Shared:
    pass


def used_before(nc, sems):
    return any(s.num in nc.released_uncleared_semaphores for s in sems)


def audio_tower(nc, x, w, out):
    ctx = ExitStack()
    with ctx:
        def sb(name, shape, dt=F32):
            return ctx.enter_context(nc.sbuf_tensor(name, shape, dt))

        g = Shared()
        g.sem = lambda name: ctx.enter_context(nc.semaphore(name))
        g.h = sb("h", [HT, NT * D])
        g.cst = sb("cst", [128, C_END])
        g.mhalf = sb("mhalf", [HT, 2])
        g.upb = sb("upb", [HT, HT], BF16)
        g.onesb = sb("onesb", [HT, 128], BF16)
        g.back = sb("back", [HT, NT], U32)
        xe = nc.dram_tensor("xe", (E1 * CAP1, ROW), F32, kind="Internal").ap()
        xs = nc.dram_tensor("xs", (E0 * XROWS, D), F32, kind="Internal").ap()
        ys = nc.dram_tensor("ys", (128 * TILES0, D), F32, kind="Internal").ap()
        stage_attention0(nc, g, x, w)
        g.xTs = sb("xTs", [128, DC, B * N])
        stage_ffn0(nc, g, w, xs, ys, xe, out)
        stage_attention1(nc, g, w, ys, xe)
        stage_ffn1(nc, g, w, xe, out)

_INS = ["x", "L0_tok_W", "L0_tok_b", "L0_tok_alpha", "L0_attn_w_q", "L0_attn_w_kv", "L0_attn_w_out",
        "L0_ffn_Wg", "L0_ffn_bg", "L0_ffn_W1", "L0_ffn_b1", "L0_ffn_W2", "L0_ffn_b2",
        "L1_attn_Wq", "L1_attn_Wk", "L1_attn_Wv", "L1_attn_Wo", "L1_attn_Wd", "L1_attn_bd", "L1_attn_out_scale",
        "L1_ffn_gate_w", "L1_ffn_w_gate_up", "L1_ffn_w_down", "L1_ffn_shared_w_gate_up", "L1_ffn_shared_w_down"]


def constants():
    import numpy as np
    c = np.zeros((128, C_END), np.float32)
    l = np.arange(L)
    j = np.where(l % 2 == 0, l // 2, L - 1 - l // 2)
    dct = np.cos(2 * np.pi * ((j[:, None] * np.arange(KF)[None, :]) % L) / L)
    c[:, C_DCT:C_DCT + 256] = dct.reshape(128, 256)
    inv = (np.float32(1.0) / np.float32(10000.0) ** (np.arange(0, 32, 2, dtype=np.float32) / np.float32(32))).astype(np.float32)
    f = (np.arange(N, dtype=np.float32)[:, None] * inv[None, :]).astype(np.float32)
    d = np.arange(128) % HD
    c[:, C_COS:C_COS + N] = np.where(d[:, None] < 32, np.cos(f[:, d % 16]).T, 1.0)
    sign = np.where(d < 16, -1.0, np.where(d < 32, 1.0, 0.0))
    c[:, C_SIN:C_SIN + N] = sign[:, None] * np.sin(f[:, d % 16]).T
    c[:, C_ID:C_ID + 128] = np.eye(128)
    r = np.arange(HT)
    c[0:HT, C_MASK:C_MASK + HT] = np.where(r[:, None] > r[None, :], -1e30, 0.0)
    c[0:HT, C_UP:C_UP + HT] = r[:, None] < r[None, :]
    c[:, C_IOTA:C_IOTA + 32] = np.arange(32)
    c[:, C_PART] = np.arange(128)
    c3 = np.zeros((128, C_END3), np.float32)
    c3[:, C_SEQ:C_SEQ + 64] = np.arange(64)
    c3[:, C_M128:C_M128 + NT] = 128 * np.arange(NT)
    e = np.arange(E0)
    c3[:, C_TRI:C_TRI + E0 * E0] = (e[None, :] <= e[:, None]).reshape(-1)
    c3[:, C_BASE0:C_BASE0 + E0] = XROWS * e
    behind = np.concatenate([r[:, None] - r[None, :], HT + r[:, None] - np.arange(N)[None, :]], axis=1)
    c2 = np.zeros((HT, C_END2), np.float32)
    c2[:, C_DIST:C_DIST + 3 * HT] = np.maximum(behind - 1, 0)
    c2[:, C_LATER:C_LATER + 3 * HT] = (behind > 0) / D ** 0.5
    return c, c2, c3


def kernel(**inputs):
    import numpy as np
    import concourse.bacc as bacc
    from concourse.bass_utils import run_bass_kernel_spmd as run

    nc = bacc.Bacc("TRN2", target_bir_lowering=False, num_devices=1)
    arrays, aps = {}, {}
    given = {n: np.ascontiguousarray(inputs[n]) for n in _INS}
    given["consts"], given["decay_consts"], given["tile_consts"] = constants()
    for name, a in given.items():
        arrays[f"in_{name}_dram"] = a
        aps[name] = nc.dram_tensor(f"in_{name}_dram", a.shape, mybir.dt.from_np(a.dtype), kind="ExternalInput").ap()
    out = nc.dram_tensor("out_0_dram", (OUTROWS, D), F32, kind="ExternalOutput").ap()
    audio_tower(nc, aps["x"], aps, out)
    r = run(nc, [arrays], core_ids=[0])
    return r.results[0]["out_0_dram"][1:1 + B * N].reshape(B, N, D)
```
